# Optimizing a Trainium2 kernel written in Bass

```python
import numpy as np
import jax
import jax.numpy as jnp

def _softmax(x, axis=-1):
    return jax.nn.softmax(x, axis=axis)

def _gelu(x):
    return jax.nn.gelu(x, approximate=True)

def _silu(x):
    return jax.nn.silu(x)

def _sigmoid(x):
    return jax.nn.sigmoid(x)

def _layernorm(x, axis=-1, eps=1e-05):
    m = jnp.mean(x, axis=axis, keepdims=True)
    v = jnp.var(x, axis=axis, keepdims=True)
    return (x - m) / jnp.sqrt(v + eps)

def _scatter_add(tgt, idx, src, axis=0):
    return tgt.at[idx].add(src)

def _segment_sum(src, seg, n):
    return jax.ops.segment_sum(src, seg, n)
kernel_name = 'mk_recurrent_d2_jaxref_r8_15bdc5'

def setup_inputs(seed: int=0):
    np.random.seed(seed)
    _w = jnp.asarray

    def _L0_attn_setup():
        import jax, jax.numpy as jnp
        import numpy as np
        N_EMBD = 256
        DIM_ATT = 256
        HEAD_SIZE = 64
        N_HEAD = DIM_ATT // HEAD_SIZE
        D_MIX = 32
        D_DECAY = 64
        N_LAYER = 24
        LAYER_ID = 12
        EPS = 1e-05 * 8.0 ** 2

        def _wkv6(r, k, v, w, u):
            B, T, H, N = r.shape
            decay = jnp.exp(-jnp.exp(w))

            def step(S, inp):
                r_t, k_t, v_t, d_t = inp
                kv = k_t[..., :, None] * v_t[..., None, :]
                y = jnp.einsum('bhj,bhji->bhi', r_t, S + u[None, :, :, None] * kv)
                return (d_t[..., None] * S + kv, y)
            seq = (r.transpose(1, 0, 2, 3), k.transpose(1, 0, 2, 3), v.transpose(1, 0, 2, 3), decay.transpose(1, 0, 2, 3))
            S0 = jnp.zeros((B, H, N, N), r.dtype)
            _, ys = jax.lax.scan(step, S0, seq)
            return ys.transpose(1, 0, 2, 3)
        key = jax.random.key(seed)
        ks = jax.random.split(key, 10)
        B, T, C = (4, 256, N_EMBD)
        r0 = LAYER_ID / (N_LAYER - 1)
        r1 = 1.0 - LAYER_ID / N_LAYER
        ddd = np.arange(C, dtype=np.float64) / C
        f32 = np.float32
        time_maa_x = (1.0 - ddd ** r1).astype(f32)[None, None, :]
        time_maa_w = (1.0 - ddd ** r1).astype(f32)[None, None, :]
        time_maa_k = (1.0 - ddd ** r1).astype(f32)[None, None, :]
        time_maa_v = (1.0 - (ddd ** r1 + 0.3 * r0)).astype(f32)[None, None, :]
        time_maa_r = (1.0 - ddd ** (0.5 * r1)).astype(f32)[None, None, :]
        time_maa_g = (1.0 - ddd ** (0.5 * r1)).astype(f32)[None, None, :]
        n = np.arange(DIM_ATT, dtype=np.float64)
        decay_speed = (-6.0 + 5.0 * (n / (DIM_ATT - 1)) ** (0.7 + 1.3 * r0)).astype(f32)
        time_decay = decay_speed[None, None, :]
        zig = ((n + 1) % 3 - 1) * 0.1
        time_faaaa = (r0 * (1.0 - n / (DIM_ATT - 1)) + zig).astype(f32).reshape(N_HEAD, HEAD_SIZE)
        u = lambda k, sh: jax.random.uniform(k, sh, jnp.float32, -0.01, 0.01)
        inp = {'x': jax.random.normal(ks[0], (B, T, C), jnp.float32), 'time_maa_x': jnp.asarray(time_maa_x), 'time_maa_w': jnp.asarray(time_maa_w), 'time_maa_k': jnp.asarray(time_maa_k), 'time_maa_v': jnp.asarray(time_maa_v), 'time_maa_r': jnp.asarray(time_maa_r), 'time_maa_g': jnp.asarray(time_maa_g), 'time_maa_w1': u(ks[1], (C, D_MIX * 5)), 'time_maa_w2': u(ks[2], (5, D_MIX, C)), 'time_decay': jnp.asarray(time_decay), 'time_decay_w1': u(ks[3], (C, D_DECAY)), 'time_decay_w2': u(ks[4], (D_DECAY, DIM_ATT)), 'time_faaaa': jnp.asarray(time_faaaa), 'W_r': jax.random.normal(ks[5], (DIM_ATT, C), jnp.float32) * 0.02, 'W_k': jax.random.normal(ks[6], (DIM_ATT, C), jnp.float32) * 0.02, 'W_v': jax.random.normal(ks[7], (DIM_ATT, C), jnp.float32) * 0.02, 'W_g': jax.random.normal(ks[8], (DIM_ATT, C), jnp.float32) * 0.02, 'W_o': jax.random.normal(ks[9], (C, DIM_ATT), jnp.float32) * 0.02, 'ln_gamma': jnp.ones((DIM_ATT,), jnp.float32), 'ln_beta': jnp.zeros((DIM_ATT,), jnp.float32)}
        return inp
    _L0_attn_in = _L0_attn_setup()

    def _L0_ffn_setup():
        import jax, jax.numpy as jnp
        import numpy as np

        def _sparsify_2to4(h):
            B, S, I = h.shape
            g = h.reshape(B, S, I // 4, 4)
            a = jnp.abs(g)
            _, idx = jax.lax.top_k(a, 2)
            pos = jnp.arange(4)
            mask = (pos == idx[..., 0:1]) | (pos == idx[..., 1:2])
            return (g * mask.astype(g.dtype)).reshape(B, S, I)
        key = jax.random.key(seed)
        k1, k2, k3, k4 = jax.random.split(key, 4)
        B, S, H, I = (4, 256, 256, 1024)
        x = jax.random.normal(k1, (B, S, H), dtype=jnp.float32)
        w_gate = jax.random.normal(k2, (H, I), dtype=jnp.float32) / np.sqrt(H)
        w_up = jax.random.normal(k3, (H, I), dtype=jnp.float32) / np.sqrt(H)
        w_down = jax.random.normal(k4, (I, H), dtype=jnp.float32) / np.sqrt(I)
        return {'x': x, 'w_gate': w_gate, 'w_up': w_up, 'w_down': w_down}
    _L0_ffn_in = _L0_ffn_setup()

    def _L1_attn_setup():
        import jax, jax.numpy as jnp
        import numpy as np
        D_MODEL = 256
        D_STATE = 64
        D_HEAD = 64
        EXPAND = 2
        CHUNK = 32
        D_INNER = EXPAND * D_MODEL
        N_HEADS = D_INNER // D_HEAD
        PARAM_DIM = 1 + 2 * D_STATE

        def _ssd(a, Bm, Cm, X, Q):
            nb, l = a.shape
            ds = Bm.shape[-1]
            dh = X.shape[-1]
            nc = l // Q
            la = jnp.log(a).reshape(nb, nc, Q)
            cs = jnp.cumsum(la, axis=-1)
            Bc = Bm.reshape(nb, nc, Q, ds)
            Cc = Cm.reshape(nb, nc, Q, ds)
            Xc = X.reshape(nb, nc, Q, dh)
            tri = jnp.tril(jnp.ones((Q, Q), bool))
            L = jnp.where(tri, jnp.exp(cs[..., :, None] - cs[..., None, :]), 0.0)
            scores = jnp.einsum('znid,znjd->znij', Cc, Bc) * L
            y_diag = jnp.einsum('znij,znjh->znih', scores, Xc)
            decay_states = jnp.exp(cs[..., -1:] - cs)
            states = jnp.einsum('znj,znjd,znjh->zndh', decay_states, Bc, Xc)
            A_chunk = jnp.exp(cs[..., -1])

            def step(S, inp):
                Ac, st = inp
                S_prev = S
                return (Ac[:, None, None] * S + st, S_prev)
            S0 = jnp.zeros((nb, ds, dh), a.dtype)
            _, S_prev = jax.lax.scan(step, S0, (A_chunk.T, jnp.moveaxis(states, 1, 0)))
            S_prev = jnp.moveaxis(S_prev, 0, 1)
            y_inter = jnp.einsum('znid,zndh,zni->znih', Cc, S_prev, jnp.exp(cs))
            return (y_diag + y_inter).reshape(nb, l, dh)
        key = jax.random.key(seed)
        k0, k1, k2, k3 = jax.random.split(key, 4)
        x = jax.random.normal(k0, (1, 512, D_MODEL), jnp.float32)
        w_in = jax.random.normal(k1, (2 * D_INNER, D_MODEL), jnp.float32) * 0.02
        w_param = jax.random.normal(k2, (N_HEADS * PARAM_DIM, D_MODEL), jnp.float32) * 0.02
        w_out = jax.random.normal(k3, (D_MODEL, D_INNER), jnp.float32) * 0.02
        return {'x': x, 'w_in': w_in, 'w_param': w_param, 'w_out': w_out}
    _L1_attn_in = _L1_attn_setup()

    def _L1_ffn_setup():
        import jax, jax.numpy as jnp
        import numpy as np
        DIM_IN = 256
        DIM_HIDDEN = 1024
        key = jax.random.key(seed)
        k_x, k_g, k_u, k_d = jax.random.split(key, 4)
        s_in = 1.0 / np.sqrt(DIM_IN)
        s_hid = 1.0 / np.sqrt(DIM_HIDDEN)
        x = jax.random.normal(k_x, (4, 256, DIM_IN), dtype=jnp.float32)
        w_gate = jax.random.uniform(k_g, (DIM_HIDDEN, DIM_IN), jnp.float32, -s_in, s_in)
        w_up = jax.random.uniform(k_u, (DIM_HIDDEN, DIM_IN), jnp.float32, -s_in, s_in)
        w_down = jax.random.uniform(k_d, (DIM_IN, DIM_HIDDEN), jnp.float32, -s_hid, s_hid)
        return {'x': x, 'w_gate': w_gate, 'w_up': w_up, 'w_down': w_down}
    _L1_ffn_in = _L1_ffn_setup()
    _d = {'L0_attn_x': _L0_attn_in['x'], 'L0_attn_time_maa_x': _L0_attn_in['time_maa_x'], 'L0_attn_time_maa_w': _L0_attn_in['time_maa_w'], 'L0_attn_time_maa_k': _L0_attn_in['time_maa_k'], 'L0_attn_time_maa_v': _L0_attn_in['time_maa_v'], 'L0_attn_time_maa_r': _L0_attn_in['time_maa_r'], 'L0_attn_time_maa_g': _L0_attn_in['time_maa_g'], 'L0_attn_time_maa_w1': _L0_attn_in['time_maa_w1'], 'L0_attn_time_maa_w2': _L0_attn_in['time_maa_w2'], 'L0_attn_time_decay': _L0_attn_in['time_decay'], 'L0_attn_time_decay_w1': _L0_attn_in['time_decay_w1'], 'L0_attn_time_decay_w2': _L0_attn_in['time_decay_w2'], 'L0_attn_time_faaaa': _L0_attn_in['time_faaaa'], 'L0_attn_W_r': _L0_attn_in['W_r'], 'L0_attn_W_k': _L0_attn_in['W_k'], 'L0_attn_W_v': _L0_attn_in['W_v'], 'L0_attn_W_g': _L0_attn_in['W_g'], 'L0_attn_W_o': _L0_attn_in['W_o'], 'L0_attn_ln_gamma': _L0_attn_in['ln_gamma'], 'L0_attn_ln_beta': _L0_attn_in['ln_beta'], 'L0_ffn_w_gate': _L0_ffn_in['w_gate'], 'L0_ffn_w_up': _L0_ffn_in['w_up'], 'L0_ffn_w_down': _L0_ffn_in['w_down'], 'L1_attn_w_in': _L1_attn_in['w_in'], 'L1_attn_w_param': _L1_attn_in['w_param'], 'L1_attn_w_out': _L1_attn_in['w_out'], 'L1_ffn_w_gate': _L1_ffn_in['w_gate'], 'L1_ffn_w_up': _L1_ffn_in['w_up'], 'L1_ffn_w_down': _L1_ffn_in['w_down']}
    _x0 = _d['L0_attn_x']
    _d['L0_attn_x'] = jax.random.normal(jax.random.fold_in(jax.random.key(seed), 1), (2, 1024, 256), dtype=_x0.dtype)
    del _x0
    return _d

def reference(L0_attn_x, L0_attn_time_maa_x, L0_attn_time_maa_w, L0_attn_time_maa_k, L0_attn_time_maa_v, L0_attn_time_maa_r, L0_attn_time_maa_g, L0_attn_time_maa_w1, L0_attn_time_maa_w2, L0_attn_time_decay, L0_attn_time_decay_w1, L0_attn_time_decay_w2, L0_attn_time_faaaa, L0_attn_W_r, L0_attn_W_k, L0_attn_W_v, L0_attn_W_g, L0_attn_W_o, L0_attn_ln_gamma, L0_attn_ln_beta, L0_ffn_w_gate, L0_ffn_w_up, L0_ffn_w_down, L1_attn_w_in, L1_attn_w_param, L1_attn_w_out, L1_ffn_w_gate, L1_ffn_w_up, L1_ffn_w_down):

    def _L0_attn_ref(x, time_maa_x, time_maa_w, time_maa_k, time_maa_v, time_maa_r, time_maa_g, time_maa_w1, time_maa_w2, time_decay, time_decay_w1, time_decay_w2, time_faaaa, W_r, W_k, W_v, W_g, W_o, ln_gamma, ln_beta):
        import jax, jax.numpy as jnp
        import numpy as np
        N_EMBD = 256
        DIM_ATT = 256
        HEAD_SIZE = 64
        N_HEAD = DIM_ATT // HEAD_SIZE
        D_MIX = 32
        D_DECAY = 64
        N_LAYER = 24
        LAYER_ID = 12
        EPS = 1e-05 * 8.0 ** 2

        def _wkv6(r, k, v, w, u):
            B, T, H, N = r.shape
            decay = jnp.exp(-jnp.exp(w))

            def step(S, inp):
                r_t, k_t, v_t, d_t = inp
                kv = k_t[..., :, None] * v_t[..., None, :]
                y = jnp.einsum('bhj,bhji->bhi', r_t, S + u[None, :, :, None] * kv)
                return (d_t[..., None] * S + kv, y)
            seq = (r.transpose(1, 0, 2, 3), k.transpose(1, 0, 2, 3), v.transpose(1, 0, 2, 3), decay.transpose(1, 0, 2, 3))
            S0 = jnp.zeros((B, H, N, N), r.dtype)
            _, ys = jax.lax.scan(step, S0, seq)
            return ys.transpose(1, 0, 2, 3)
        B, T, C = x.shape
        H, N = time_faaaa.shape
        xx = jnp.concatenate([jnp.zeros_like(x[:, :1]), x[:, :-1]], axis=1) - x
        xxx = x + xx * time_maa_x
        D = time_maa_w2.shape[1]
        a = jnp.tanh(xxx @ time_maa_w1).reshape(B, T, 5, D)
        m = jnp.einsum('btfd,fdc->fbtc', a, time_maa_w2)
        mw, mk, mv, mr, mg = (m[0], m[1], m[2], m[3], m[4])
        xw = x + xx * (time_maa_w + mw)
        xk = x + xx * (time_maa_k + mk)
        xv = x + xx * (time_maa_v + mv)
        xr = x + xx * (time_maa_r + mr)
        xg = x + xx * (time_maa_g + mg)
        r = xr @ W_r.T
        k = xk @ W_k.T
        v = xv @ W_v.T
        g = jax.nn.silu(xg @ W_g.T)
        w = time_decay + jnp.tanh(xw @ time_decay_w1) @ time_decay_w2
        y = _wkv6(r.reshape(B, T, H, N), k.reshape(B, T, H, N), v.reshape(B, T, H, N), w.reshape(B, T, H, N), time_faaaa)
        mean = y.mean(-1, keepdims=True)
        var = y.var(-1, keepdims=True)
        yn = ((y - mean) * jax.lax.rsqrt(var + EPS)).reshape(B, T, H * N)
        yn = yn * ln_gamma + ln_beta
        return yn * g @ W_o.T

    def _L0_ffn_ref(x, w_gate, w_up, w_down):
        import jax, jax.numpy as jnp
        import numpy as np

        def _sparsify_2to4(h):
            B, S, I = h.shape
            g = h.reshape(B, S, I // 4, 4)
            a = jnp.abs(g)
            _, idx = jax.lax.top_k(a, 2)
            pos = jnp.arange(4)
            mask = (pos == idx[..., 0:1]) | (pos == idx[..., 1:2])
            return (g * mask.astype(g.dtype)).reshape(B, S, I)
        h = jax.nn.silu(jnp.einsum('bsh,hi->bsi', x, w_gate)) * jnp.einsum('bsh,hi->bsi', x, w_up)
        h_sparse = _sparsify_2to4(h)
        return jnp.einsum('bsi,ih->bsh', h_sparse, w_down)

    def _L1_attn_ref(x, w_in, w_param, w_out):
        import jax, jax.numpy as jnp
        import numpy as np
        D_MODEL = 256
        D_STATE = 64
        D_HEAD = 64
        EXPAND = 2
        CHUNK = 32
        D_INNER = EXPAND * D_MODEL
        N_HEADS = D_INNER // D_HEAD
        PARAM_DIM = 1 + 2 * D_STATE

        def _ssd(a, Bm, Cm, X, Q):
            nb, l = a.shape
            ds = Bm.shape[-1]
            dh = X.shape[-1]
            nc = l // Q
            la = jnp.log(a).reshape(nb, nc, Q)
            cs = jnp.cumsum(la, axis=-1)
            Bc = Bm.reshape(nb, nc, Q, ds)
            Cc = Cm.reshape(nb, nc, Q, ds)
            Xc = X.reshape(nb, nc, Q, dh)
            tri = jnp.tril(jnp.ones((Q, Q), bool))
            L = jnp.where(tri, jnp.exp(cs[..., :, None] - cs[..., None, :]), 0.0)
            scores = jnp.einsum('znid,znjd->znij', Cc, Bc) * L
            y_diag = jnp.einsum('znij,znjh->znih', scores, Xc)
            decay_states = jnp.exp(cs[..., -1:] - cs)
            states = jnp.einsum('znj,znjd,znjh->zndh', decay_states, Bc, Xc)
            A_chunk = jnp.exp(cs[..., -1])

            def step(S, inp):
                Ac, st = inp
                S_prev = S
                return (Ac[:, None, None] * S + st, S_prev)
            S0 = jnp.zeros((nb, ds, dh), a.dtype)
            _, S_prev = jax.lax.scan(step, S0, (A_chunk.T, jnp.moveaxis(states, 1, 0)))
            S_prev = jnp.moveaxis(S_prev, 0, 1)
            y_inter = jnp.einsum('znid,zndh,zni->znih', Cc, S_prev, jnp.exp(cs))
            return (y_diag + y_inter).reshape(nb, l, dh)
        b, l, _ = x.shape
        xr = x @ w_in.T
        inp, res = (xr[..., :D_INNER], xr[..., D_INNER:])
        params = (x @ w_param.T).reshape(b, l, N_HEADS, PARAM_DIM)
        dt = jax.nn.softplus(params[..., 0])
        a = jnp.exp(-dt)
        Bp = params[..., 1:1 + D_STATE]
        Cp = params[..., 1 + D_STATE:]
        nb = b * N_HEADS
        y = _ssd(a.reshape(nb, l), Bp.reshape(nb, l, D_STATE), Cp.reshape(nb, l, D_STATE), inp.reshape(nb, l, D_HEAD), CHUNK)
        y = y.reshape(b, l, D_INNER)
        out = y * jax.nn.silu(res)
        return out @ w_out.T

    def _L1_ffn_ref(x, w_gate, w_up, w_down):
        import jax, jax.numpy as jnp
        import numpy as np
        DIM_IN = 256
        DIM_HIDDEN = 1024
        gate = jnp.einsum('bsd,hd->bsh', x, w_gate)
        up = jnp.einsum('bsd,hd->bsh', x, w_up)
        gated = jax.nn.silu(gate) * up
        return jnp.einsum('bsh,dh->bsd', gated, w_down)
    x = L0_attn_x
    xn = _layernorm(x, axis=-1)
    s = _L0_attn_ref(xn, L0_attn_time_maa_x, L0_attn_time_maa_w, L0_attn_time_maa_k, L0_attn_time_maa_v, L0_attn_time_maa_r, L0_attn_time_maa_g, L0_attn_time_maa_w1, L0_attn_time_maa_w2, L0_attn_time_decay, L0_attn_time_decay_w1, L0_attn_time_decay_w2, L0_attn_time_faaaa, L0_attn_W_r, L0_attn_W_k, L0_attn_W_v, L0_attn_W_g, L0_attn_W_o, L0_attn_ln_gamma, L0_attn_ln_beta)
    g = _silu(_L0_ffn_ref(xn, L0_ffn_w_gate, L0_ffn_w_up, L0_ffn_w_down))
    x = x + s * g
    xn = _layernorm(x, axis=-1)
    s = _L1_attn_ref(xn, L1_attn_w_in, L1_attn_w_param, L1_attn_w_out)
    g = _silu(_L1_ffn_ref(xn, L1_ffn_w_gate, L1_ffn_w_up, L1_ffn_w_down))
    x = x + s * g
    return x

_drawn_inputs = setup_inputs


def setup_inputs(seed=0):
    import zlib

    import numpy as np

    out = dict(_drawn_inputs(seed))
    spreads = {'L0_attn_ln_gamma': (1.0, 0.2), 'L0_attn_ln_beta': (0.0, 0.1)}
    factors = {}
    for name, (base, spread) in spreads.items():
        noise = np.random.default_rng([zlib.crc32(name.encode()), seed]).standard_normal(out[name].shape)
        drawn = base * np.exp(spread * noise) if base else spread * noise
        out[name] = jnp.asarray(drawn.astype(out[name].dtype))
    for name, factor in factors.items():
        out[name] = (out[name] * factor).astype(out[name].dtype)
    return out
```

```python
from contextlib import ExitStack

import concourse.bass as bass
from concourse import mybir

F32 = mybir.dt.float32
BF16 = mybir.dt.bfloat16
I8 = mybir.dt.int8
ALU = mybir.AluOpType
ACT = mybir.ActivationFunctionType
AX = mybir.AxisListType

P = 128
TOKENS, BATCH, C = 2048, 2, 256
T = 256
NT = TOKENS // T
NQ = T // P
CH = C // P
HEADS, HD = 4, 64
DMIX, NMIX, DDEC = 32, 5, 64
HID = 1024
SH, SD = 8, 64
SEQ_T = 128
SCH = SEQ_T * SH // P
CHT = P // SH
LN_EPS = 1e-5
GN_EPS = 1e-5 * 8.0 ** 2
DECAY_CAP = 110.0
NEG = -1.0e30
LEVELS = [64, 32, 16, 8, 4, 2, 1]

VEC = {n: i for i, n in enumerate(["maa_x", "maa_w", "maa_k", "maa_v", "maa_r", "maa_g", "decay", "bonus", "gamma", "beta"])}
FEAT = {"w": 0, "k": 1, "v": 2, "r": 3, "g": 4}

BANKS = 8
FILLS = ["xT", "p0g", "p0u", "a", "p1g", "p1u", "mix_w", "mix_k", "dw", "mix_r", "k", "w", "mix_v", "r",
         "mix_g", "lev1a", "lev1b", "v", "g", "p2g", "p2u", "lev64a", "lev64b", "lev32a", "lev32b", "p3g", "p3u", "lev16a", "lev16b", "lev8a", "lev8b", "lev4a", "lev4b",
         "lev2a", "lev2b", "bonus", "k0T", "kv", "F0", "y", "n0g", "n0u", "n1g", "n1u", "yT", "n2g", "n2u", "s0",
         "n3g", "n3u", "F1", "xT1", "dt", "X0", "X1", "B0", "csum", "B1", "C0", "C1", "res0", "res1",
         "csT", "bt0", "bt1", "sc0", "sc1", "sc2", "sc3", "st", "ys0", "ys1", "s1"]
BANK = {n: i % BANKS for i, n in enumerate(FILLS)}
NTH = {n: i // BANKS + 1 for i, n in enumerate(FILLS)}
PER = [sum(BANK[n] == b for n in FILLS) for b in range(BANKS)]
for i, n in enumerate(["e0g", "e0u", "e1g", "e1u", "e2g", "e2u", "e3g", "e3u", "eF"]):
    BANK[n], NTH[n] = i % BANKS, i // BANKS + 1


def build_block(nc, A):
    with ExitStack() as ctx:
        def sb(name, shape, dt=F32):
            return ctx.enter_context(nc.sbuf_tensor(name, shape, dt))

        def sem(name):
            return ctx.enter_context(nc.semaphore(name))

        W = {n: sb("sb_" + n, list(A[n].shape)) for n in A if n not in ("x", "out", "cs_dram", "x_dram")}
        vec = W["vecs"]

        ident = sb("ident", [P, P])
        masks = sb("masks", [P, len(LEVELS), NQ * CH * 64], I8)
        causal = sb("causal", [P, P])
        before = sb("before", [P, P])
        chunk_reset = sb("chunk_reset", [P, T])
        head_reset = sb("head_reset", [P, NQ * SH])
        head_sel = sb("head_sel", [P, CH, HEADS])
        keep = sb("keep", [P, NT])
        half_neg = sb("half_neg", [P, 8])

        X = sb("X", [P, NQ, C])
        xn = sb("xn", [P, NQ, C])
        xnT = sb("xnT", [P, CH, T + 1])
        dxT = sb("dxT", [P, CH, T])
        xxxT = sb("xxxT", [P, CH, T])
        mixed = {f: sb("mixed_" + f, [P, CH, T]) for f in "wkrvg"}
        aT = sb("aT", [P, T])
        aT4 = sb("aT4", [DMIX, T])
        decT = sb("decT", [DDEC, T])
        kT = sb("kT", [P, CH, T])
        rT = sb("rT", [P, CH, T])
        v = sb("v", [P, NQ, C])
        gT = sb("gT", [P, CH, T])
        cum = sb("cum", [P, CH * T + 64])
        dec = sb("dec", [P, CH * NQ, P + 1])
        lev = [sb(f"lev{i}_kr", [P, CH * T]) for i in range(3)]
        att = sb("att", [P, NQ * HEADS * P])
        S = sb("S", [P, NQ + 1, CH, P])
        bonus = sb("bonus_sb", [P, NQ * HEADS])
        x1 = sb("x1", [P, NQ, C])
        x1_prev = sb("x1_prev", [P, NQ, C])
        stats = sb("stats", [P, NQ * 6])
        meanvar = sb("meanvar", [P, NQ * 2])
        var_eps = sb("var_eps", [P, NQ * HEADS])
        rstd = sb("rstd", [P, NQ * HEADS])
        gsum = sb("gsum", [P, NQ * HEADS])
        th = [sb(f"th{i}", [P, 512]) for i in range(2)]
        thF = sb("thF", [P, NQ * C])
        hid = sb("hid", [P, 8, T])
        k0n, y, yc, ysq, ynT, ygT = (mixed["w"], mixed["k"], mixed["r"], mixed["v"], mixed["g"], xxxT)
        prodT, k0f = dxT, xxxT

        xn1T = sb("xn1T", [P, CH, T])
        BC = sb("BC", [P, 2, SEQ_T, SH])
        cs_row = sb("cs_row", [P, 2 * SCH, P])
        cs_half = sb("cs_half", [P, SEQ_T * SH])
        prefix = sb("prefix", [P, NQ * SH])
        cs_nat = sb("cs_nat", [P, NQ, SH])
        cs16 = sb("cs16", [NQ * SCH, P])
        cs_col = sb("cs_col", [P, NQ * SCH])
        to_end = sb("to_end", [P, NQ * SCH])
        chunk_dec = sb("chunk_dec", [P, SCH])
        sp = [sb(f"sp{i}", [P, NQ * SH]) for i in range(4)]
        Xnat = sb("Xnat", [P, NQ, SH * SD])
        Xrow = sb("Xrow", [P, NQ, SCH, SD])
        Brow = sb("Brow", [P, NQ, SCH, SD])
        S1 = sb("S1", [P, SCH, SD])
        gate = sb("gate", [P, SH // 2, T])
        s1 = sb("s1", [P, NQ, C])
        outb = sb("outb", [P, NQ, C])
        habs = BC[:, :, :, :].rearrange("p a t h -> p (a t h)").rearrange("p (m i t) -> p m i t", m=2, i=4)
        beats = cs_row[:, :, :].rearrange("p a b -> p (a b)").bitcast(BF16)[:, 0:2 * 6 * T].rearrange(
            "p (m i t) -> p m i t", m=2, i=6)
        wins = gate[:, :, :].rearrange("p a b -> p (a b)").bitcast(BF16).rearrange("p (m i t) -> p m i t", m=2, i=4)

        bank = [ctx.enter_context(nc.psum_tensor(f"bank{b}", [P, 512], F32)) for b in range(BANKS)]

        def ps(name):
            return bank[BANK[name]]

        filled = [sem(f"filled{b}") for b in range(BANKS)]
        freed = [sem(f"freed{b}") for b in range(BANKS)]
        loads = {g: sem("loads_" + g) for g in ("vecs", "mix", "proj", "ffn0", "ssd", "ffn1")}
        x_loaded = sem("x_loaded")
        const_ready = sem("const_ready")
        pool_step = sem("pool_step")
        act_step = sem("act_step")
        dve_step = sem("dve_step")
        passed = sem("passed")
        carry_ready = sem("carry_ready")
        xn_ready = sem("xn_ready")
        xxx_ready = sem("xxx_ready")
        a_ready = sem("a_ready")
        mix_ready = sem("mix_ready")
        cum_ready = sem("cum_ready")
        g_tanh = sem("g_tanh")
        arg_ready = sem("arg_ready")
        fac_ready = sem("fac_ready")
        dec0_ready = sem("dec0_ready")
        lev_ready = sem("lev_ready")
        prod_ready = sem("prod_ready")
        th_ready = sem("th_ready")
        abs_ready = sem("abs_ready")
        sparse_ready = sem("sparse_ready")
        yc_ready = sem("yc_ready")
        ysq_ready = sem("ysq_ready")
        var_ready = sem("var_ready")
        rstd_ready = sem("rstd_ready")
        yn_ready = sem("yn_ready")
        yg_ready = sem("yg_ready")
        thF_ready = sem("thF_ready")
        x_used = sem("x_used")
        out_ready = sem("out_ready")
        out_stored = sem("out_stored")
        x1_saved = sem("x1_saved")
        soft_ready = sem("soft_ready")
        prefix_ready = sem("prefix_ready")
        cs_stored = sem("cs_stored")
        cs_loaded = sem("cs_loaded")
        X_stored = sem("X_stored")
        X_rows = sem("X_rows")
        res_tanh = sem("res_tanh")
        cs_half_exp = sem("cs_half_exp")
        end_arg = sem("end_arg")
        to_end_ready = sem("to_end_ready")
        L_arg = sem("L_arg")
        L_exp = sem("L_exp")
        Cdec_ready = sem("Cdec_ready")

        block = ctx.enter_context(nc.Block())

        class Steps:

            def __init__(self, eng, s):
                self.eng, self.s, self.n = eng, s, 0

            def did(self, ins):
                self.n += 1
                ins.then_inc(self.s, 1)
                return self.n

            def after(self, n=None):
                self.eng.wait_ge(self.s, self.n if n is None else n)

            def restart(self):
                self.after()
                self.eng.sem_clear(self.s)
                self.n = 0

        def wait_filled(eng, it, name):
            eng.wait_ge(filled[BANK[name]], it * PER[BANK[name]] + NTH[name])

        def wait_freed(eng, it, name):
            eng.wait_ge(freed[BANK[name]], it * PER[BANK[name]] + NTH[name] + 1)

        def free(ins, name):
            ins.then_inc(freed[BANK[name]], 1)

        def flat(t):
            return t[:, :, :].rearrange("p a b -> p (a b)")

        cs_dram, x_dram = A["cs_dram"], A["x_dram"]

        @block.sync
        def _(sp_):
            def load(names, group):
                for n in names:
                    sp_.dma_start(W[n][:, :], A[n]).then_inc(loads[group], 16)

            def tokens(name, first):
                return A[name][bass.ds(first, T), :].rearrange("(q p) c -> p q c", p=P)

            def wait(s, value):
                sp_.wait_ge(s, value)
                sp_.sem_inc(passed, 1)

            def one_tile(it, x_from, out_to):
                wait(x_used, it + 1)
                sp_.dma_start(X[:, :, :], tokens("x", x_from)).then_inc(x_loaded, 16)
                if out_to is not None:
                    wait(out_ready, it + 1)
                    sp_.dma_start(tokens("out", out_to), outb[:, :, :]).then_inc(out_stored, 16)
                wait_freed(sp_, it, "X1")
                sp_.sem_inc(passed, 1)
                wait(X_rows, it * 16 + 16)
                sp_.dma_start(x_dram.rearrange("(q p n) -> p q n", q=NQ, p=P), Xnat[:, :, :]).then_inc(X_stored, 16)
                wait_freed(sp_, it, "csum")
                sp_.sem_inc(passed, 1)
                wait(cs_loaded, it * 64 + 16)
                sp_.dma_start(cs_dram.rearrange("(q p h) -> p q h", q=NQ, p=P), cs_nat[:, :, :]).then_inc(cs_stored, 16)
                wait(cs_stored, it * 16 + 32)
                sp_.dma_start(cs16[:, :], cs_dram.rearrange("(c p) -> c p", p=P)).then_inc(cs_loaded, 16)
                sp_.dma_start(flat(cs_row), cs_dram.partition_broadcast(P)).then_inc(cs_loaded, 16)
                n = SEQ_T * SH
                for q in range(NQ):
                    sp_.dma_start(cs_half[64 * q:64 * q + 64, :],
                                  cs_dram[q * n:(q + 1) * n].partition_broadcast(64)).then_inc(cs_loaded, 16)
                wait(X_stored, it * 16 + 32)
                sp_.dma_start(Xrow[:, :, :, :].rearrange("p q c d -> p (q c) d"),
                              x_dram.rearrange("(c p d) -> p c d", p=P, d=SD)).then_inc(X_rows, 16)

            for s in (X_rows, X_stored, cs_stored, cs_loaded):
                sp_.sem_inc(s, 16)
            sp_.sem_inc(out_stored, 32)
            sp_.sem_inc(x1_saved, 1)
            load(["vecs"], "vecs")
            sp_.dma_start(X[:, :, :], tokens("x", 0)).then_inc(x_loaded, 16)
            load(["f_gate", "f_up"], "ffn0")
            load(["w_mix1", "w_mix2a", "w_mix2b"], "mix")
            load(["w_dec1", "w_dec2", "w_rkvgo"], "proj")
            load(["n_gate", "n_up", "n_down", "f_down"], "ffn1")
            load(["w_dt", "w_X", "w_B", "w_C", "w_res", "w_sout"], "ssd")
            one_tile(0, T, None)
            with sp_.Fori(1, NT - 1) as it:
                one_tile(it, (it + 1) * T, (it - 1) * T)
            one_tile(NT - 1, (NT - 1) * T, (NT - 2) * T)
            sp_.wait_ge(out_ready, NT + 1)
            sp_.dma_start(tokens("out", (NT - 1) * T), outb[:, :, :]).then_inc(out_stored, 16)
            sp_.wait_ge(out_stored, 16 * (NT + 2))

        @block.gpsimd
        def _(pool):
            steps = Steps(pool, pool_step)

            def did(ins):
                steps.did(ins)
                steps.after()

            g = nc.gpsimd
            did(g.memset(ident[:, :], 0.0))
            did(g.affine_select(out=ident[:, :], in_=ident[:, :], compare_op=ALU.not_equal, fill=1.0, base=0,
                                pattern=[[-1, P]], channel_multiplier=1))
            did(g.memset(causal[:, :], 0.0))
            did(g.affine_select(out=causal[:, :], in_=causal[:, :], compare_op=ALU.is_ge, fill=NEG, base=0,
                                pattern=[[1, P]], channel_multiplier=-1))
            did(g.memset(before[:, :], 1.0))
            bv = before[:, :].rearrange("p (b q) -> p b q", q=CHT)
            did(g.affine_select(out=bv, in_=bv, compare_op=ALU.is_ge, fill=0.0, base=0,
                                pattern=[[-CHT, P // CHT], [0, CHT]], channel_multiplier=1))
            did(g.affine_select(out=bv, in_=bv, compare_op=ALU.is_gt, fill=0.0, base=0,
                                pattern=[[CHT, P // CHT], [1, CHT]], channel_multiplier=-1))
            did(g.memset(half_neg[:, :], -0.5))
            for n, s in enumerate(LEVELS):
                tmp = lev[n % 2][:, 0:64]
                tv = tmp.rearrange("p (b q) -> p b q", q=s)
                did(g.memset(tmp, 1.0))
                did(g.affine_select(out=tv, in_=tv, compare_op=ALU.is_ge, fill=0.0, base=0,
                                    pattern=[[-2 * s, 64 // s], [0, s]], channel_multiplier=1))
                did(g.affine_select(out=tv, in_=tv, compare_op=ALU.is_ge, fill=0.0, base=s - 1,
                                    pattern=[[2 * s, 64 // s], [0, s]], channel_multiplier=-1))
                for rep in range(NQ * CH):
                    did(g.tensor_copy(masks[:, n, rep * 64:(rep + 1) * 64], tmp))
            g.memset(rstd[:, :], 1.0).then_inc(const_ready, 1)
            steps.restart()

            def rsqrt(count, n):
                pool.wait_ge(var_ready, count)
                g.tensor_tensor(rstd[:, 0:n], var_eps[:, 0:n], half_neg[:, 0:n], ALU.pow).then_inc(rstd_ready, 1)

            pool.wait_ge(const_ready, 1)
            rsqrt(1, NQ)
            with pool.Fori(0, NT) as it:
                rsqrt(it * 3 + 2, NQ * HEADS)
                rsqrt(it * 3 + 3, NQ)
                rsqrt(it * 3 + 4, NQ)

        @block.scalar
        def _(act):
            steps = Steps(act, act_step)
            a = nc.scalar

            def ffn_tanh(it, name, n, made=None):
                wait_filled(act, it, name + "g")
                if made:
                    wait_freed(act, it, made + "u")
                a.activation(th[n % 2][:, :], ps(name + "g")[:, :], ACT.Tanh, scale=0.5).then_inc(th_ready, 1)

            def ffn_abs(it, n):
                wait_freed(act, it, f"p{n}u")
                a.activation(habs.rearrange("p m i t -> p (m i t)")[:, n * 512:(n + 1) * 512],
                             hid[:, 2 * n:2 * n + 2, :].rearrange("p a b -> p (a b)"), ACT.Abs).then_inc(abs_ready, 1)

            def copy(it, dst, name, src, s=None):
                wait_filled(act, it, name)
                ins = a.activation(dst, src, ACT.Identity)
                free(ins, name)

            def level_exp(it, n):
                act.wait_ge(arg_ready, it * 7 + n + 1)
                a.activation(lev[n % 3][:, :], lev[n % 3][:, :], ACT.Exp).then_inc(fac_ready, 1)

            def ffn_out(it, name, n):
                wait_filled(act, it, name)
                a.activation(thF[:, :], ps(name)[:, :], ACT.Tanh, scale=0.25).then_inc(thF_ready, 1)

            act.wait_ge(loads["vecs"], 16)
            with act.Fori(0, NT) as it:
                act.wait_ge(carry_ready, it + 1)
                copy(it, xnT[:, :, 1:T + 1], "xT", ps("xT")[:, :].rearrange("p (h t) -> p h t", h=CH))
                ffn_tanh(it, "p0", 0)
                wait_filled(act, it, "a")
                a.activation(aT[:, :], ps("a")[:, 0:T], ACT.Tanh).then_inc(a_ready, 1)
                free(a.activation(aT4[:, :], ps("a")[0:DMIX, T:2 * T], ACT.Tanh), "a")
                ffn_abs(it, 0)
                ffn_tanh(it, "p1", 1)
                ffn_abs(it, 1)
                wait_filled(act, it, "dw")
                free(a.activation(decT[:, :], ps("dw")[0:DDEC, 0:T], ACT.Tanh), "dw")
                copy(it, kT[:, :, :], "k", ps("k")[:, :].rearrange("p (h t) -> p h t", h=CH))
                wait_filled(act, it, "w")
                for h in range(CH):
                    ins = a.activation(lev[2][:, h * T:(h + 1) * T], ps("w")[:, h * T:(h + 1) * T], ACT.Exp,
                                       bias=vec[:, 2 * VEC["decay"] + h:2 * VEC["decay"] + h + 1])
                free(ins, "w")
                copy(it, rT[:, :, :], "r", ps("r")[:, :].rearrange("p (h t) -> p h t", h=CH))
                act.wait_ge(cum_ready, it + 1)
                a.activation(dec[:, :, 1:P + 1], cum[:, 0:CH * T].rearrange("p (a b) -> p a b", b=P), ACT.Exp,
                             scale=-1.0).then_inc(dec0_ready, 1)
                copy(it, v[:, :, :], "v", ps("v")[:, :].rearrange("p (h t) -> p h t", h=NQ))
                wait_filled(act, it, "g")
                a.activation(gT[:, :, :], ps("g")[:, :].rearrange("p (h t) -> p h t", h=CH), ACT.Tanh,
                             scale=0.5).then_inc(g_tanh, 1)
                level_exp(it, 0)
                level_exp(it, 1)
                ffn_tanh(it, "p2", 2, "p0")
                ffn_abs(it, 2)
                level_exp(it, 2)
                ffn_tanh(it, "p3", 3, "p1")
                ffn_abs(it, 3)
                level_exp(it, 3)
                level_exp(it, 4)
                level_exp(it, 5)
                act.wait_ge(arg_ready, it * 7 + 7)
                a.activation(flat(k0f), flat(k0f), ACT.Exp).then_inc(fac_ready, 1)
                copy(it, k0n[:, :, :], "k0T", ps("k0T")[:, :].rearrange("p (h t) -> p h t", h=NQ))
                ffn_out(it, "F0", 0)
                act.wait_ge(yc_ready, it + 1)
                a.activation(flat(ysq), flat(yc), ACT.Square).then_inc(ysq_ready, 1)
                ffn_tanh(it, "n0", 4, "p2")
                ffn_tanh(it, "n1", 5, "p3")
                wait_filled(act, it, "yT")
                for h in range(CH):
                    g0, b0 = 2 * VEC["gamma"] + h, 2 * VEC["beta"] + h
                    ins = a.activation(ynT[:, h, :], ps("yT")[:, h * T:(h + 1) * T], ACT.Identity,
                                       scale=vec[:, g0:g0 + 1], bias=vec[:, b0:b0 + 1])
                free(ins, "yT")
                ffn_tanh(it, "n2", 6, "n0")
                ffn_tanh(it, "n3", 7, "n1")
                act.wait_ge(x_used, it + 1)
                ffn_out(it, "F1", 1)
                act.wait_ge(out_ready, it + 1)
                a.activation(flat(x1_prev), flat(x1), ACT.Identity).then_inc(x1_saved, 1)
                copy(it, xn1T[:, :, :], "xT1", ps("xT1")[:, :].rearrange("p (h t) -> p h t", h=CH))
                wait_filled(act, it, "dt")
                steps.did(a.activation(sp[0][:, :], ps("dt")[:, 0:NQ * SH], ACT.Abs))
                steps.after()
                steps.did(a.activation(sp[1][:, :], sp[0][:, :], ACT.Exp, scale=-1.0))
                steps.after()
                a.activation(sp[2][:, :], sp[1][:, :], ACT.Ln, bias=1.0).then_inc(soft_ready, 1)
                for q in range(NQ):
                    act.wait_ge(X_stored, it * 16 + 16)
                    wait_filled(act, it, f"X{q}")
                    free(a.activation(Xnat[:, q, :], ps(f"X{q}")[:, :], ACT.Identity), f"X{q}")

                def bc(name, which, pair):
                    wait_filled(act, it, name)
                    src = ps(name)[:, :].rearrange("p (m s t) -> p m s t", m=2, s=NQ)
                    for par in range(2):
                        for s in range(NQ):
                            cols = BC[64 * s:64 * s + 64, which, :, :].rearrange("p t (m e) -> p e m t", e=2)
                            ins = a.activation(cols[:, par, 2 * pair:2 * pair + 2, :],
                                               src[64 * par:64 * par + 64, :, s, :], ACT.Identity)
                    free(ins, name)

                bc("B0", 0, 0)
                bc("B1", 0, 1)
                bc("C0", 1, 0)
                bc("C1", 1, 1)
                for n in range(2):
                    wait_filled(act, it, f"res{n}")
                    a.activation(gate[:, 2 * n:2 * n + 2, :].rearrange("p a b -> p (a b)"), ps(f"res{n}")[:, :],
                                 ACT.Tanh, scale=0.5).then_inc(res_tanh, 1)
                act.wait_ge(cs_loaded, it * 64 + 80)
                a.activation(cs_half[:, :], cs_half[:, :], ACT.Exp).then_inc(cs_half_exp, 1)
                act.wait_ge(end_arg, it + 1)
                a.activation(to_end[:, :], to_end[:, :], ACT.Exp).then_inc(to_end_ready, 1)
                for s in range(NQ):
                    act.wait_ge(L_arg, it * NQ + s + 1)
                    w = cs_row[:, s * SCH:(s + 1) * SCH, :].rearrange("p a b -> p (a b)")
                    a.activation(w, w, ACT.Exp).then_inc(L_exp, 1)
                wait_filled(act, it, "s1")
                free(a.activation(flat(s1), ps("s1")[:, :], ACT.Identity), "s1")
                steps.restart()
            for n in range(4):
                ffn_tanh(NT, f"e{n}", n, f"e{n - 2}" if n >= 2 else None)
            ffn_out(NT, "eF", 0)

        @block.vector
        def _(dve):
            steps = Steps(dve, dve_step)
            did, after = steps.did, steps.after
            d = nc.vector

            for t in (flat(xnT), flat(xn1T), flat(x1_prev), flat(s1), att[:, :],
                      S[:, :, :, :].rearrange("p a b c -> p (a b c)"), flat(head_sel)):
                did(d.memset(t, 0.0))
            for t in (flat(dec), chunk_reset[:, :], head_reset[:, :], keep[:, :]):
                did(d.memset(t, 1.0))
            after()
            for t in (chunk_reset[:, :].rearrange("p (a b) -> p a b", b=P)[:, :, 0:1],
                      head_reset[:, :].rearrange("p (a b) -> p a b", b=SH)[:, :, 0:1],
                      keep[:, :].rearrange("p (a b) -> p a b", b=NT // BATCH)[:, :, 0:1]):
                did(d.memset(t, 0.0))
            for h in range(HEADS):
                did(d.memset(head_sel[64 * (h % 2):64 * (h % 2) + 64, h // 2, h:h + 1], 1.0))

            def norm_stats(src):
                for q in range(NQ):
                    did(d.bn_stats(stats[:, 6 * q:6 * q + 6], src[:, q, :]))
                after()
                for q in range(NQ):
                    did(d.bn_aggr(meanvar[:, 2 * q:2 * q + 2], stats[:, 6 * q:6 * q + 6]))
                after()
                mv = meanvar[:, :].rearrange("p (q two) -> p q two", two=2)
                d.tensor_scalar(var_eps[:, 0:NQ], mv[:, :, 1], LN_EPS, None, ALU.add).then_inc(var_ready, 1)

            def norm_apply(src, rstd_count, xn_count=None):
                dve.wait_ge(rstd_ready, rstd_count)
                for q in range(NQ):
                    ins = d.tensor_scalar(xn[:, q, :], src[:, q, :], meanvar[:, 2 * q:2 * q + 1], rstd[:, q:q + 1],
                                          ALU.subtract, ALU.mult)
                    if q < NQ - 1:
                        did(ins)
                ins.then_inc(xn_ready, 1)

            dve.wait_ge(const_ready, 1)
            dve.wait_ge(x_loaded, 16)
            norm_stats(X)
            norm_apply(X, 1)
            steps.restart()
            dve.wait_ge(loads["vecs"], 16)

            def vcol(name, h):
                return vec[:, 2 * VEC[name] + h:2 * VEC[name] + h + 1]

            def hidden(it, name, n):
                t = th[n % 2]
                dve.wait_ge(th_ready, it * 8 + n + 1)
                free(d.scalar_tensor_tensor(out=t[:, :], in0=t[:, :], scalar=1.0, in1=ps(name + "g")[:, :],
                                            op0=ALU.add, op1=ALU.mult), name + "g")
                wait_freed(dve, it, name + "g")
                wait_filled(dve, it, name + "u")
                k = n % 4
                free(d.tensor_tensor(hid[:, 2 * k:2 * k + 2, :].rearrange("p a b -> p (a b)"), t[:, :],
                                     ps(name + "u")[:, :], ALU.mult), name + "u")

            def ffn_gate(it, name, count):
                dve.wait_ge(thF_ready, count)
                free(d.scalar_tensor_tensor(out=thF[:, :], in0=thF[:, :], scalar=1.0, in1=ps(name)[:, :],
                                            op0=ALU.add, op1=ALU.mult), name)

            with dve.Fori(0, NT) as it:
                kp = keep[:, bass.ds(it, 1)]
                d.tensor_scalar(xnT[:, :, 0:1], xnT[:, :, T:T + 1], kp, None, ALU.mult).then_inc(carry_ready, 1)
                did(d.tensor_scalar(flat(S[:, 0:1, :, :].rearrange("p z a b -> p (z a) b")), flat(S[:, NQ:NQ + 1, :, :].rearrange("p z a b -> p (z a) b")), kp, None, ALU.mult))

                wait_freed(dve, it, "xT")
                did(d.tensor_tensor(dxT[:, :, :], xnT[:, :, 0:T], xnT[:, :, 1:T + 1], ALU.subtract))
                after()
                for h in range(CH):
                    ins = d.scalar_tensor_tensor(out=xxxT[:, h, :], in0=dxT[:, h, :], scalar=vcol("maa_x", h),
                                                 in1=xnT[:, h, 1:T + 1], op0=ALU.mult, op1=ALU.add)
                    if h == 0:
                        did(ins)
                ins.then_inc(xxx_ready, 1)
                hidden(it, "p0", 0)
                hidden(it, "p1", 1)

                def mix_scaled(f):
                    wait_filled(dve, it, "mix_" + f)
                    for h in range(CH):
                        ins = d.scalar_tensor_tensor(out=mixed[f][:, h, :], in0=ps("mix_" + f)[:, h * T:(h + 1) * T],
                                                     scalar=vcol("maa_" + f, h), in1=dxT[:, h, :],
                                                     op0=ALU.add, op1=ALU.mult)
                        if h == 0:
                            did(ins)
                    free(ins, "mix_" + f)

                def mix_add(f):
                    wait_freed(dve, it, "mix_" + f)
                    d.tensor_tensor(mixed[f][:, :, :], mixed[f][:, :, :], xnT[:, :, 1:T + 1],
                                    ALU.add).then_inc(mix_ready, 1)

                mix_scaled("w")
                mix_scaled("k")
                mix_add("w")
                mix_scaled("r")
                mix_add("k")
                mix_scaled("v")
                mix_add("r")

                wait_freed(dve, it, "w")
                did(d.tensor_scalar(lev[2][:, :], lev[2][:, :], DECAY_CAP, None, ALU.min))
                mix_scaled("g")
                after()
                for h in range(CH):
                    ins = d.tensor_tensor_scan(cum[:, h * T:(h + 1) * T], chunk_reset[:, :],
                                               lev[2][:, h * T:(h + 1) * T], 0.0, ALU.mult, ALU.add)
                    if h == 0:
                        did(ins)
                ins.then_inc(cum_ready, 1)
                mix_add("v")
                mix_add("g")

                def halves(t, s):
                    return t.rearrange("p (b two s) -> p b two s", two=2, s=s)

                def level_args(n):
                    s = LEVELS[n]
                    c, f = halves(cum[:, 0:CH * T], s), halves(lev[n % 3][:, :], s)
                    one_back = cum[:, s - 1:s - 1 + CH * T].rearrange("p (b w) -> p b w", w=2 * s)[:, :, 0:s]
                    mid = c[:, :, 0, s - 1:s].to_broadcast([P, CH * T // (2 * s), s])
                    did(d.tensor_tensor(f[:, :, 0, :], c[:, :, 0, :], mid, ALU.subtract))
                    d.tensor_tensor(f[:, :, 1, :], mid, one_back, ALU.subtract).then_inc(arg_ready, 1)

                def level_scale(n):
                    s = LEVELS[n]
                    dve.wait_ge(fac_ready, it * 7 + n + 1)
                    f = halves(lev[n % 3][:, :], s)
                    kk, rr = halves(flat(kT), s), halves(flat(rT), s)
                    did(d.tensor_tensor(f[:, :, 0, :], f[:, :, 0, :], kk[:, :, 0, :], ALU.mult))
                    d.tensor_tensor(f[:, :, 1, :], f[:, :, 1, :], rr[:, :, 1, :], ALU.mult).then_inc(lev_ready, 1)

                def level_take(n):
                    s = LEVELS[n]
                    for par, name in enumerate((f"lev{s}a", f"lev{s}b")):
                        if s > 1:
                            wait_freed(dve, it, f"lev{LEVELS[n - 1]}{name[-1]}")
                        wait_filled(dve, it, name)
                        dve.sem_inc(passed, 1)
                        out = att[:, par * 512:(par + 1) * 512].rearrange("p (b w) -> p b w", w=2 * s)[:, :, s:2 * s]
                        free(d.copy_predicated(out, masks[:, n, :].rearrange("p (b s) -> p b s", s=s),
                                               ps(name)[:, 0:256].rearrange("p (b s) -> p b s", s=s)), name)

                dve.wait_ge(cum_ready, it + 1)
                level_args(0)
                level_args(1)
                level_take(6)
                dve.wait_ge(g_tanh, it + 1)
                free(d.scalar_tensor_tensor(out=flat(gT), in0=flat(gT), scalar=1.0, in1=ps("g")[:, :],
                                            op0=ALU.add, op1=ALU.mult), "g")
                level_scale(0)
                level_args(2)
                hidden(it, "p2", 2)
                level_scale(1)
                level_take(0)
                level_args(3)
                level_scale(2)
                level_take(1)
                level_args(4)
                hidden(it, "p3", 3)
                level_scale(3)
                level_take(2)
                level_args(5)
                cq = cum[:, 0:CH * T].rearrange("p (a b) -> p a b", b=P)
                kf = flat(k0f).rearrange("p (a b) -> p a b", b=P)
                d.tensor_tensor(kf, cq, cq[:, :, P - 1:P].to_broadcast([P, CH * NQ, P]),
                                ALU.subtract).then_inc(arg_ready, 1)
                for h in range(CH):
                    ins = d.scalar_tensor_tensor(out=prodT[:, h, :], in0=kT[:, h, :], scalar=vcol("bonus", h),
                                                 in1=rT[:, h, :], op0=ALU.mult, op1=ALU.mult)
                    if h == 0:
                        did(ins)
                ins.then_inc(prod_ready, 1)
                level_scale(4)
                level_take(3)
                level_scale(5)
                level_take(4)

                dve.wait_ge(abs_ready, it * 4 + 4)

                def pairs_of(i, first, count):
                    did(d.tensor_tensor(beats[:, :, first:first + count, :],
                                        habs[:, :, i:i + 1, :].to_broadcast([P, 2, count, T]),
                                        habs[:, :, i + 1:4, :], ALU.is_ge))

                pairs_of(0, 0, 3)
                pairs_of(1, 3, 2)
                pairs_of(2, 5, 1)
                after()
                B01, B02, B03, B12, B13, B23 = (beats[:, :, n, :] for n in range(6))
                W0, W1, W2, W3 = (wins[:, :, n, :] for n in range(4))
                did(d.tensor_tensor(W0, B01, B02, ALU.add))
                did(d.tensor_tensor(W1, B12, B13, ALU.add))
                did(d.tensor_tensor(W2, B23, B02, ALU.subtract))
                n3 = did(d.tensor_tensor(W3, B03, B13, ALU.add))
                after(n3 - 3)
                did(d.tensor_tensor(W0, W0, B03, ALU.add))
                after(n3 - 2)
                did(d.tensor_tensor(W1, W1, B01, ALU.subtract))
                after(n3 - 1)
                did(d.tensor_tensor(W2, W2, B12, ALU.subtract))
                after(n3)
                did(d.tensor_tensor(W3, W3, B23, ALU.add))
                hv = hid[:, :, :].rearrange("p (m i) t -> p m i t", i=4)
                for i, (w, least, op) in enumerate([(W0, 1.5, ALU.is_ge), (W1, 0.5, ALU.is_ge), (W2, -0.5, ALU.is_ge),
                                                    (W3, 1.5, ALU.is_le)]):
                    after(n3 + 1 + i)
                    ins = d.scalar_tensor_tensor(out=hv[:, :, i, :], in0=w, scalar=least, in1=hv[:, :, i, :],
                                                 op0=op, op1=ALU.mult)
                    if i < 3:
                        did(ins)
                ins.then_inc(sparse_ready, 1)

                level_take(5)
                wait_filled(dve, it, "bonus")
                free(d.tensor_copy(bonus[:, :], ps("bonus")[:, 0:NQ * HEADS]), "bonus")
                dve.wait_ge(fac_ready, it * 7 + 7)
                wait_filled(dve, it, "lev1b")
                d.tensor_tensor(flat(kT), flat(kT), flat(k0f), ALU.mult).then_inc(prod_ready, 1)
                dve.wait_ge(dec0_ready, it + 1)
                rq = flat(rT).rearrange("p (a b) -> p a b", b=P)
                d.tensor_tensor(rq, rq, dec[:, :, 0:P], ALU.mult).then_inc(prod_ready, 1)

                wait_filled(dve, it, "kv")
                kv = ps("kv")[:, :].rearrange("p (q h c) -> p q h c", q=NQ, h=CH)
                for q in range(NQ):
                    if q:
                        after()
                    for h in range(CH):
                        for par in range(2):
                            r, cols = slice(64 * par, 64 * par + 64), slice(64 * par, 64 * par + 64)
                            ins = d.scalar_tensor_tensor(out=S[r, q + 1, h, cols], in0=S[r, q, h, cols],
                                                         scalar=dec[r, h * NQ + q, P:P + 1], in1=kv[r, q, h, cols],
                                                         op0=ALU.mult, op1=ALU.add)
                            if (q, h, par) != (NQ - 1, CH - 1, 1):
                                did(ins)
                free(ins, "kv")

                ffn_gate(it, "F0", it * 2 + 1)

                wait_filled(dve, it, "y")
                wait_freed(dve, it, "bonus")
                for n in range(NQ * HEADS):
                    q, h = n // HEADS, n % HEADS
                    ins = d.scalar_tensor_tensor(out=y[:, q, h * HD:(h + 1) * HD], in0=v[:, q, h * HD:(h + 1) * HD],
                                                 scalar=bonus[:, n:n + 1],
                                                 in1=ps("y")[:, n * HD:(n + 1) * HD], op0=ALU.mult, op1=ALU.add)
                    if n < NQ * HEADS - 1:
                        did(ins)
                free(ins, "y")
                y3, yc3, ysq3 = (flat(t).rearrange("p (n d) -> p n d", d=HD) for t in (y, yc, ysq))
                wait_freed(dve, it, "y")
                did(d.tensor_reduce(gsum[:, :], y3, AX.X, ALU.add))
                after()
                did(d.tensor_scalar(gsum[:, :], gsum[:, :], 1.0 / HD, None, ALU.mult))
                after()
                d.tensor_tensor(yc3, y3, gsum[:, :].unsqueeze(2).to_broadcast([P, NQ * HEADS, HD]),
                                ALU.subtract).then_inc(yc_ready, 1)
                hidden(it, "n0", 4)
                dve.wait_ge(ysq_ready, it + 1)
                did(d.tensor_reduce(gsum[:, :], ysq3, AX.X, ALU.add))
                after()
                d.tensor_scalar(var_eps[:, :], gsum[:, :], 1.0 / HD, GN_EPS, ALU.mult, ALU.add).then_inc(var_ready, 1)
                hidden(it, "n1", 5)
                dve.wait_ge(rstd_ready, it * 3 + 2)
                d.tensor_tensor(y3, yc3, rstd[:, :].unsqueeze(2).to_broadcast([P, NQ * HEADS, HD]),
                                ALU.mult).then_inc(yn_ready, 1)
                wait_freed(dve, it, "yT")
                d.tensor_tensor(flat(ygT), flat(ynT), flat(gT), ALU.mult).then_inc(yg_ready, 1)
                hidden(it, "n2", 6)

                wait_filled(dve, it, "s0")
                wait_freed(dve, it, "F0")
                free(d.tensor_tensor(thF[:, :], thF[:, :], ps("s0")[:, :], ALU.mult), "s0")
                wait_freed(dve, it, "s0")
                dve.wait_ge(x1_saved, it + 1)
                d.scalar_tensor_tensor(out=flat(x1), in0=thF[:, :], scalar=0.125, in1=flat(X),
                                       op0=ALU.mult, op1=ALU.add).then_inc(x_used, 1)
                dve.wait_ge(x_used, it + 1)
                norm_stats(x1)
                norm_apply(x1, it * 3 + 3)
                hidden(it, "n3", 7)

                def finish(it, name, count):
                    ffn_gate(it, name, count)
                    wait_freed(dve, it, name)
                    did(d.tensor_tensor(thF[:, :], thF[:, :], flat(s1), ALU.mult))
                    after()
                    dve.wait_ge(out_stored, it * 16 + 16)
                    d.scalar_tensor_tensor(out=flat(outb), in0=thF[:, :], scalar=0.125, in1=flat(x1_prev),
                                           op0=ALU.mult, op1=ALU.add).then_inc(out_ready, 1)

                finish(it, "F1", it * 2 + 2)

                dve.wait_ge(soft_ready, it + 1)
                free(d.scalar_tensor_tensor(out=sp[3][:, :], in0=ps("dt")[:, 0:NQ * SH], scalar=0.0, in1=sp[2][:, :],
                                            op0=ALU.max, op1=ALU.add), "dt")
                wait_freed(dve, it, "dt")
                d.tensor_tensor_scan(prefix[:, :], head_reset[:, :], sp[3][:, :], 0.0, ALU.mult,
                                     ALU.add).then_inc(prefix_ready, 1)
                dve.wait_ge(prefix_ready, it + 1)
                wait_filled(dve, it, "csum")
                dve.wait_ge(cs_stored, it * 16 + 16)
                free(d.scalar_tensor_tensor(out=cs_nat[:, :, :], in0=prefix[:, :].rearrange("p (q h) -> p q h", h=SH),
                                            scalar=-1.0, in1=ps("csum")[:, 0:NQ].unsqueeze(2).to_broadcast([P, NQ, SH]),
                                            op0=ALU.mult, op1=ALU.subtract), "csum")
                for n in range(2):
                    dve.wait_ge(res_tanh, it * 2 + n + 1)
                    gv = gate[:, 2 * n:2 * n + 2, :].rearrange("p a b -> p (a b)")
                    free(d.scalar_tensor_tensor(out=gv, in0=gv, scalar=1.0, in1=ps(f"res{n}")[:, :],
                                                op0=ALU.add, op1=ALU.mult), f"res{n}")
                dve.wait_ge(x_loaded, it * 16 + 32)
                wait_filled(dve, it, "xT1")
                norm_stats(X)
                norm_apply(X, it * 3 + 4)

                wait_filled(dve, it, "csT")
                free(d.tensor_copy(cs_col[:, :], ps("csT")[:, 0:NQ * SCH]), "csT")
                wait_freed(dve, it, "csT")
                dve.wait_ge(cs_loaded, it * 64 + 80)
                d.tensor_tensor(to_end[:, :], cs_row[:, :, P - 1], cs_col[:, :], ALU.subtract).then_inc(end_arg, 1)
                dve.wait_ge(end_arg, it + 1)
                for n in range(NQ * SCH):
                    ins = d.scalar_tensor_tensor(out=cs_row[:, n, :], in0=cs_row[:, n, :], scalar=cs_col[:, n:n + 1],
                                                 in1=causal[:, :], op0=ALU.subtract, op1=ALU.min)
                    if n % SCH == SCH - 1:
                        ins.then_inc(L_arg, 1)
                    else:
                        did(ins)
                dve.wait_ge(cs_half_exp, it + 1)
                ch = cs_half[:, :].rearrange("p (c w) -> p c w", w=P)
                did(d.tensor_copy(chunk_dec[:, :], ch[:, :, P - 1]))
                after()
                wait_freed(dve, it, "C1")
                d.tensor_tensor(cs_half[:, :], cs_half[:, :], BC[:, 1, :, :].rearrange("p t h -> p (t h)"),
                                ALU.mult).then_inc(Cdec_ready, 1)
                dve.wait_ge(to_end_ready, it + 1)
                for s in range(NQ):
                    wait_filled(dve, it, f"bt{s}")
                    free(d.tensor_tensor(Brow[:, s, 0:SCH - 1, :],
                                         ps(f"bt{s}")[:, 0:(SCH - 1) * SD].rearrange("p (c d) -> p c d", d=SD),
                                         to_end[:, s * SCH:(s + 1) * SCH - 1].unsqueeze(2).to_broadcast(
                                             [P, SCH - 1, SD]), ALU.mult), f"bt{s}")
                for n in range(4):
                    dve.wait_ge(L_exp, it * NQ + n // 2 + 1)
                    wait_filled(dve, it, f"sc{n}")
                    w = flat(cs_row)[:, n * 512:(n + 1) * 512]
                    free(d.tensor_tensor(w, w, ps(f"sc{n}")[:, :], ALU.mult), f"sc{n}")
                wait_filled(dve, it, "st")
                did(d.tensor_copy(S1[:, 1, :], ps("st")[:, 0:SD]))
                for c in range(1, SCH - 1):
                    after()
                    ins = d.scalar_tensor_tensor(out=S1[:, c + 1, :], in0=S1[:, c, :], scalar=chunk_dec[:, c:c + 1],
                                                 in1=ps("st")[:, c * SD:(c + 1) * SD], op0=ALU.mult, op1=ALU.add)
                    if c < SCH - 2:
                        did(ins)
                free(ins, "st")
                for s in range(NQ):
                    wait_filled(dve, it, f"ys{s}")
                    gv = gate[:, :, s * P:(s + 1) * P]
                    free(d.tensor_tensor(gv, gv, ps(f"ys{s}")[:, :].rearrange("p (t m) -> p m t", m=SH // 2),
                                         ALU.mult), f"ys{s}")
                steps.restart()
            for n in range(4):
                hidden(NT, f"e{n}", n)
            finish(NT, "eF", NT * 2 + 1)

        @block.tensor
        def _(pe):
            t_ = nc.tensor

            def open_bank(it, name):
                b, n = BANK[name], NTH[name]
                pe.wait_ge(freed[b], it * PER[b] + n)

            def close_bank(ins, name):
                ins.then_inc(filled[BANK[name]], 1)

            def project(it, name, parts):
                open_bank(it, name)
                for col, rows, ws, xs in parts:
                    for k, (w, x) in enumerate(zip(ws, xs)):
                        n = x.free_size()
                        ins = t_.matmul(ps(name)[0:rows, col:col + n], w, x, start=(k == 0), stop=(k == len(ws) - 1))
                close_bank(ins, name)

            def weights_first(it, name, w, k, cols, x, width=P):
                project(it, name, [(i * T, width, [w(h, c, width) for h in range(k)], [x(h) for h in range(k)])
                                   for i, c in enumerate(cols)])

            def packed(n, width):
                return lambda h, c, w: W[n][:, h * width + c:h * width + c + w]

            def halves_of(t):
                return lambda h: t[:, h, :]

            def ffn(it, name, gate_w, up_w, pair, x):
                for suffix, w in (("g", gate_w), ("u", up_w)):
                    weights_first(it, name + suffix, packed(w, HID), CH, [2 * pair * P, (2 * pair + 1) * P], x)

            def ffn_down(it, name, w):
                project(it, name, [(q * C, P, [hid[:, m, q * P:(q + 1) * P] for m in range(8)],
                                    [W[w][:, m * C:(m + 1) * C] for m in range(8)]) for q in range(NQ)])

            def transposes(it, name, src):
                open_bank(it, name)
                for h in range(CH):
                    for q in range(NQ):
                        ins = t_.transpose(ps(name)[:, h * T + q * P:h * T + (q + 1) * P],
                                           src[:, q, h * P:(h + 1) * P], ident[:, :])
                close_bank(ins, name)

            for f in freed:
                pe.sem_inc(f, 1)
            pe.wait_ge(const_ready, 1)

            def body(it):
                pe.wait_ge(xn_ready, it * 2 + 1)
                transposes(it, "xT", xn)
                wait_freed(pe, it, "xT")
                pe.wait_ge(loads["ffn0"], 32)
                xh = lambda h: xnT[:, h, 1:T + 1]
                ffn(it, "p0", "f_gate", "f_up", 0, xh)
                pe.wait_ge(loads["mix"], 48)
                pe.wait_ge(xxx_ready, it + 1)
                w1 = packed("w_mix1", NMIX * DMIX)
                project(it, "a", [(0, P, [w1(h, 0, P) for h in range(CH)], [xxxT[:, h, :] for h in range(CH)]),
                                  (T, DMIX, [w1(h, P, DMIX) for h in range(CH)], [xxxT[:, h, :] for h in range(CH)])])
                ffn(it, "p1", "f_gate", "f_up", 1, xh)

                def mix(f):
                    n = FEAT[f]
                    r = slice(32 * n, 32 * n + 32) if n < 4 else slice(0, 32)
                    src, w = (aT, W["w_mix2a"]) if n < 4 else (aT4, W["w_mix2b"])
                    project(it, "mix_" + f, [(h * T, P, [w[r, h * P:(h + 1) * P]], [src[r, :]]) for h in range(CH)])

                def proj(f):
                    i = "rkvgo".index(f)
                    weights_first(it, f, lambda h, c, w: W["w_rkvgo"][:, i * 2 * C + h * C + c:i * 2 * C + h * C + c + w],
                                  CH, [0, P], halves_of(mixed[f]))

                pe.wait_ge(a_ready, it + 1)
                mix("w")
                mix("k")
                pe.wait_ge(loads["proj"], 48)
                pe.wait_ge(mix_ready, it * 5 + 1)
                project(it, "dw", [(0, DDEC, [W["w_dec1"][:, h * DDEC:(h + 1) * DDEC] for h in range(CH)],
                                    [mixed["w"][:, h, :] for h in range(CH)])])
                mix("r")
                pe.wait_ge(mix_ready, it * 5 + 2)
                proj("k")
                wait_freed(pe, it, "dw")
                project(it, "w", [(h * T, P, [W["w_dec2"][:, h * P:(h + 1) * P]], [decT[:, :]]) for h in range(CH)])
                mix("v")
                pe.wait_ge(mix_ready, it * 5 + 3)
                proj("r")
                wait_freed(pe, it, "a")
                mix("g")

                def level(s, src):
                    names = (f"lev{s}a", f"lev{s}b")
                    for name in names:
                        open_bank(it, name)
                    for q in range(NQ):
                        for h in range(CH):
                            for par, name in enumerate(names):
                                r, c0, n = slice(64 * par, 64 * par + 64), h * T + q * P, (q * CH + h) * 64
                                keys, queries = src[0][r, c0:c0 + P], src[1][r, c0:c0 + P]
                                qs = queries.rearrange("p (b two s) -> p b two s", two=2, s=s)[:, :, 1, :]
                                ins = t_.matmul(ps(name)[:, n:n + 64], keys, qs, start=True, stop=True)
                                if (q, h) == (NQ - 1, CH - 1):
                                    close_bank(ins, name)

                wait_freed(pe, it, "k")
                wait_freed(pe, it, "r")
                level(1, (flat(kT), flat(rT)))
                pe.wait_ge(mix_ready, it * 5 + 4)
                project(it, "v", [(q * C, P, [mixed["v"][:, h, q * P:(q + 1) * P] for h in range(CH)],
                                   [W["w_rkvgo"][:, 4 * C + h * C:4 * C + (h + 1) * C] for h in range(CH)])
                                  for q in range(NQ)])
                pe.wait_ge(mix_ready, it * 5 + 5)
                proj("g")
                ffn(it, "p2", "f_gate", "f_up", 2, xh)

                def scaled_level(n):
                    pe.wait_ge(lev_ready, it * 6 + n + 1)
                    level(LEVELS[n], (lev[n % 3][:, :], lev[n % 3][:, :]))

                scaled_level(0)
                scaled_level(1)
                ffn(it, "p3", "f_gate", "f_up", 3, xh)
                scaled_level(2)
                scaled_level(3)
                scaled_level(4)
                scaled_level(5)

                pe.wait_ge(prod_ready, it * 3 + 1)
                project(it, "bonus", [(q * HEADS, P, [prodT[:, h, q * P:(q + 1) * P] for h in range(CH)],
                                       [head_sel[:, h, :] for h in range(CH)]) for q in range(NQ)])
                pe.wait_ge(prod_ready, it * 3 + 2)
                open_bank(it, "k0T")
                for q in range(NQ):
                    for h in range(CH):
                        ins = t_.transpose(ps("k0T")[:, q * C + h * P:q * C + (h + 1) * P],
                                           kT[:, h, q * P:(q + 1) * P], ident[:, :])
                close_bank(ins, "k0T")
                wait_freed(pe, it, "k0T")
                wait_freed(pe, it, "v")
                project(it, "kv", [(q * C + h * P, P, [k0n[:, q, h * P:(h + 1) * P]], [v[:, q, h * P:(h + 1) * P]])
                                   for q in range(NQ) for h in range(CH)])
                pe.wait_ge(sparse_ready, it + 1)
                pe.wait_ge(loads["ffn1"], 64)
                ffn_down(it, "F0", "f_down")

                wait_freed(pe, it, "kv")
                wait_freed(pe, it, "lev2b")
                pe.wait_ge(prod_ready, it * 3 + 3)
                open_bank(it, "y")
                for q in range(NQ):
                    for h in range(CH):
                        n = q * C + h * P
                        t_.matmul(ps("y")[:, n:n + P], rT[:, h, q * P:(q + 1) * P], S[:, q, h, :],
                                  start=(n == 0), stop=False, skip_group_check=True)
                    for hd in range(HEADS):
                        n, i = q * C + hd * HD, (hd % 2) * NQ * CH + q * CH + hd // 2
                        ins = t_.matmul(ps("y")[:, n:n + HD], att[:, i * P:(i + 1) * P],
                                        v[:, q, hd * HD:(hd + 1) * HD], start=False, stop=True, skip_group_check=True)
                close_bank(ins, "y")

                xp = halves_of(xn1T)
                ffn(it, "n0", "n_gate", "n_up", 0, xp)
                ffn(it, "n1", "n_gate", "n_up", 1, xp)
                pe.wait_ge(yn_ready, it + 1)
                transposes(it, "yT", y)
                ffn(it, "n2", "n_gate", "n_up", 2, xp)
                pe.wait_ge(yg_ready, it + 1)
                project(it, "s0", [(q * C, P, [ygT[:, h, q * P:(q + 1) * P] for h in range(CH)],
                                    [W["w_rkvgo"][:, 8 * C + h * C:8 * C + (h + 1) * C] for h in range(CH)])
                                   for q in range(NQ)])
                ffn(it, "n3", "n_gate", "n_up", 3, xp)
                wait_freed(pe, it, "n3u")
                ffn_down(it, "F1", "n_down")

                pe.wait_ge(xn_ready, it * 2 + 2)
                transposes(it, "xT1", xn)
                wait_freed(pe, it, "xT1")
                pe.wait_ge(loads["ssd"], 96)

                def tokens_first(name, w, width, q, col):
                    return (col, P, [xn1T[:, h, q * P:(q + 1) * P] for h in range(CH)],
                            [W[w][:, h * width:(h + 1) * width] for h in range(CH)])

                project(it, "dt", [tokens_first("dt", "w_dt", SH, q, q * SH) for q in range(NQ)])
                for q in range(NQ):
                    project(it, f"X{q}", [tokens_first("X", "w_X", SH * SD, q, 0)])
                x1h = halves_of(xn1T)
                weights_first(it, "B0", packed("w_B", SH * SD), CH, [0, P], x1h)
                pe.wait_ge(prefix_ready, it + 1)
                project(it, "csum", [(0, P, [before[:, :]],
                                      [prefix[:, :].rearrange("p (q h) -> p q h", h=SH)[:, :, SH - 1]])])
                weights_first(it, "B1", packed("w_B", SH * SD), CH, [2 * P, 3 * P], x1h)
                weights_first(it, "C0", packed("w_C", SH * SD), CH, [0, P], x1h)
                weights_first(it, "C1", packed("w_C", SH * SD), CH, [2 * P, 3 * P], x1h)
                weights_first(it, "res0", packed("w_res", SH * SD), CH, [0, P], x1h)
                weights_first(it, "res1", packed("w_res", SH * SD), CH, [2 * P, 3 * P], x1h)

                pe.wait_ge(cs_loaded, it * 64 + 80)
                open_bank(it, "csT")
                pe.sem_inc(passed, 1)
                close_bank(t_.transpose(ps("csT")[:, 0:NQ * SCH], cs16[:, :], ident[0:NQ * SCH, 0:NQ * SCH]), "csT")

                Bf, Cf = (BC[:, n, :, :].rearrange("p t h -> p (t h)") for n in range(2))
                wait_freed(pe, it, "B1")
                for s in range(NQ):
                    r = slice(64 * s, 64 * s + 64)
                    open_bank(it, f"bt{s}")
                    pe.sem_inc(passed, 1)
                    for c in range(SCH - 1):
                        ins = t_.transpose(ps(f"bt{s}")[:, c * SD:(c + 1) * SD], Bf[r, c * P:(c + 1) * P], ident[r, r])
                    close_bank(ins, f"bt{s}")
                wait_freed(pe, it, "C1")
                for n in range(4):
                    s = n // 2
                    r = slice(64 * s, 64 * s + 64)
                    open_bank(it, f"sc{n}")
                    for i in range(4):
                        c = (n % 2) * 4 + i
                        ins = t_.matmul(ps(f"sc{n}")[:, i * P:(i + 1) * P], Bf[r, c * P:(c + 1) * P],
                                        Cf[r, c * P:(c + 1) * P], start=True, stop=True)
                    close_bank(ins, f"sc{n}")

                pe.wait_ge(X_rows, it * 16 + 32)
                open_bank(it, "st")
                for s in range(NQ):
                    wait_freed(pe, it, f"bt{s}")
                    for c in range(SCH - 1):
                        ins = t_.matmul(ps("st")[64 * s:64 * s + 64, c * SD:(c + 1) * SD], Brow[:, s, c, :],
                                        Xrow[:, s, c, :], start=True, stop=True)
                close_bank(ins, "st")

                pe.wait_ge(Cdec_ready, it + 1)
                for s in range(NQ):
                    r = slice(64 * s, 64 * s + 64)
                    if s == 0:
                        wait_freed(pe, it, "sc1")
                        wait_freed(pe, it, "st")
                    else:
                        wait_freed(pe, it, "sc3")
                    open_bank(it, f"ys{s}")
                    for c in range(SCH):
                        m = cs_row[:, s * SCH + c, :].rearrange("p (n e) -> p e n", e=2)
                        cd = cs_half[r, c * P:(c + 1) * P].rearrange("p (n e) -> p e n", e=2)
                        for par in range(2):
                            out = ps(f"ys{s}")[64 * par:64 * par + 64, c * 64:(c + 1) * 64]
                            ins = t_.matmul(out, Xrow[:, s, c, :], m[:, par, :], start=(c == 0), stop=(c == 0),
                                            skip_group_check=True)
                            if c:
                                ins = t_.matmul(out, S1[r, c, :], cd[:, par, :], start=False, stop=True,
                                                skip_group_check=True)
                    close_bank(ins, f"ys{s}")

                wait_freed(pe, it, "ys0")
                wait_freed(pe, it, "ys1")
                project(it, "s1", [(q * C, P, [gate[:, m, q * P:(q + 1) * P] for m in range(SH // 2)],
                                    [W["w_sout"][:, m * C:(m + 1) * C] for m in range(SH // 2)]) for q in range(NQ)])

            with pe.Fori(0, NT) as it:
                body(it)
            for n in range(4):
                ffn(NT, f"e{n}", "n_gate", "n_up", n, halves_of(xn1T))
            wait_freed(pe, NT, "e3u")
            ffn_down(NT, "eF", "n_down")
    return nc


def _tiles(np, w):
    k, n = w.shape[0] // P, w.shape[1]
    return np.ascontiguousarray(w.reshape(k, P, n).transpose(1, 0, 2).reshape(P, k * n))


def _layout(np, v):
    pre = "L0_attn_"
    vecs = np.stack([v[pre + n].reshape(C) for n in
                     ("time_maa_x", "time_maa_w", "time_maa_k", "time_maa_v", "time_maa_r", "time_maa_g",
                      "time_decay", "time_faaaa", "ln_gamma", "ln_beta")])
    out = {"x": v[pre + "x"].reshape(TOKENS, C),
           "vecs": vecs.reshape(len(VEC), CH, P).transpose(2, 0, 1).reshape(P, len(VEC) * CH),
           "w_mix1": _tiles(np, v[pre + "time_maa_w1"]),
           "w_mix2a": v[pre + "time_maa_w2"][0:4].reshape(4 * DMIX, C),
           "w_mix2b": v[pre + "time_maa_w2"][4],
           "w_dec1": _tiles(np, v[pre + "time_decay_w1"]),
           "w_dec2": v[pre + "time_decay_w2"],
           "w_rkvgo": np.concatenate([_tiles(np, v[pre + "W_" + n].T) for n in "rkvgo"], axis=1)}

    def units(w):
        return w.reshape(C, 2, P, 4).transpose(0, 1, 3, 2).reshape(C, HID)

    out["f_gate"] = _tiles(np, units(v["L0_ffn_w_gate"]))
    out["f_up"] = _tiles(np, units(v["L0_ffn_w_up"]))
    out["f_down"] = v["L0_ffn_w_down"].reshape(2, P, 4, C).transpose(1, 0, 2, 3).reshape(P, 8 * C)
    inner = SH * SD
    w_in = v["L1_attn_w_in"]
    out["w_X"] = _tiles(np, w_in[0:inner].T)
    out["w_res"] = _tiles(np, w_in[inner:].T)
    par = v["L1_attn_w_param"].reshape(SH, 1 + 2 * SD, C)
    out["w_dt"] = _tiles(np, par[:, 0].T)
    out["w_B"] = _tiles(np, par[:, 1:1 + SD].reshape(inner, C).T)
    out["w_C"] = _tiles(np, par[:, 1 + SD:].reshape(inner, C).T)
    out["w_sout"] = _tiles(np, v["L1_attn_w_out"].T)
    out["n_gate"] = _tiles(np, v["L1_ffn_w_gate"].T)
    out["n_up"] = _tiles(np, v["L1_ffn_w_up"].T)
    out["n_down"] = _tiles(np, v["L1_ffn_w_down"].T)
    return {n: np.ascontiguousarray(a) for n, a in out.items()}


def kernel(**inputs):
    import numpy as np
    import concourse.bacc as bacc
    from concourse.bass_utils import run_bass_kernel_spmd

    arrays = _layout(np, {n: np.asarray(a) for n, a in inputs.items()})
    nc = bacc.Bacc("TRN2", target_bir_lowering=False, num_devices=1)
    aps = {n: nc.dram_tensor("in_" + n, a.shape, mybir.dt.from_np(a.dtype), kind="ExternalInput").ap()
           for n, a in arrays.items()}
    aps["out"] = nc.dram_tensor("out_tokens", (TOKENS, C), F32, kind="ExternalOutput").ap()
    aps["cs_dram"] = nc.dram_tensor("cs_dram", (T * SH,), F32).ap()
    aps["x_dram"] = nc.dram_tensor("x_dram", (T * SH * SD,), F32).ap()
    build_block(nc, aps)
    r = run_bass_kernel_spmd(nc, [{"in_" + n: a for n, a in arrays.items()}], core_ids=[0])
    return r.results[0]["out_tokens"].reshape(BATCH, TOKENS // BATCH, C)
```

```python
from contextlib import ExitStack

import concourse.bass as bass
from concourse import mybir

F32 = mybir.dt.float32
BF16 = mybir.dt.bfloat16
I8 = mybir.dt.int8
ALU = mybir.AluOpType
ACT = mybir.ActivationFunctionType
AX = mybir.AxisListType

P = 128
TOKENS, BATCH, C = 2048, 2, 256
T = 256
NT = TOKENS // T
NQ = T // P
CH = C // P
HEADS, HD = 4, 64
DMIX, NMIX, DDEC = 32, 5, 64
HID = 1024
SH, SD = 8, 64
SEQ_T = 128
SCH = SEQ_T * SH // P
CHT = P // SH
LN_EPS = 1e-5
GN_EPS = 1e-5 * 8.0 ** 2
DECAY_CAP = 110.0
NEG = -1.0e30
LEVELS = [64, 32, 16, 8, 4, 2, 1]

VEC = {n: i for i, n in enumerate(["maa_x", "maa_w", "maa_k", "maa_v", "maa_r", "maa_g", "decay", "bonus", "gamma", "beta"])}
FEAT = {"w": 0, "k": 1, "v": 2, "r": 3, "g": 4}

RING = 4
FILLS = [["xT", "p0g", "p0u", "a", "p1g", "p1u", "mix_w", "mix_k", "mix_r", "dw", "mix_v", "k", "w", "mix_g", "r",
          "v", "lev1", "g", "lev64", "lev32", "lev16", "lev8",
          "lev4", "p2g", "p2u", "lev2", "p3g", "p3u", "k0T", "kv", "bonus", "y", "F0", "yT",
          "s0"],
         ["xT1", "dt", "X0", "X1", "B0", "B1", "csum", "C0", "C1", "res0", "res1", "csT", "bt0", "bt1", "sc0",
          "sc1", "sc2", "sc3", "st", "ys0", "ys1", "n0g", "n0u", "n1g", "n1u", "n2g", "n2u", "n3g", "n3u", "s1",
          "F1"]]
BANK = {n: ring * RING + i % RING for ring in range(2) for i, n in enumerate(FILLS[ring])}
NTH = {n: i // RING + 1 for ring in range(2) for i, n in enumerate(FILLS[ring])}
BANKS = 2 * RING
PER = [sum(BANK[n] == b for n in FILLS[b // RING]) for b in range(BANKS)]


class Tile:

    def __init__(self, reg, off=0):
        self.reg, self.off = reg, off

    def count(self, per, n):
        return n + per * self.off if self.reg is None else self.reg * per + (n + per * self.off)

    def at(self):
        return self.off if self.reg is None else self.reg + self.off

    def next(self):
        return Tile(self.reg, self.off + 1)


def build_block(nc, A):
    with ExitStack() as ctx:
        def sb(name, shape, dt=F32):
            return ctx.enter_context(nc.sbuf_tensor(name, shape, dt))

        def sem(name):
            return ctx.enter_context(nc.semaphore(name))

        W = {n: sb("sb_" + n, list(A[n].shape)) for n in A
             if n not in ("x", "out", "cs_dram", "x_dram", "w_mix2b", "w_dec2")}
        low = sb("sb_mix2b_dec2", [P, C])
        W["w_mix2b"], W["w_dec2"] = low[0:DMIX, :], low[DDEC:P, :]
        vec = W["vecs"]

        ident = sb("ident", [P, P])
        masks = sb("masks", [P, len(LEVELS), 512], I8)
        causal = sb("causal", [P, P])
        before = sb("before", [P, P])
        chunk_reset = sb("chunk_reset", [P, T])
        head_reset = sb("head_reset", [P, NQ * SH])
        head_sel = sb("head_sel", [P, CH, HEADS])
        keep = sb("keep", [P, NT + 1])
        half_neg = sb("half_neg", [P, 8])

        X = sb("X", [P, NQ, C])
        xn = sb("xn", [P, NQ, C])
        xnT = sb("xnT", [P, CH, T + 1])
        dxT = sb("dxT", [P, CH, T])
        mixed = {f: sb("mixed_" + f, [P, CH, T]) for f in "wkrvg"}
        aT = sb("aT", [P, T])
        aT4_decT = sb("aT4_decT", [P, T])
        aT4, decT = aT4_decT[0:DMIX, :], aT4_decT[DDEC:P, :]
        kT = sb("kT", [P, CH, T])
        rT = sb("rT", [P, CH, T])
        v = sb("v", [P, NQ, C])
        gT = sb("gT", [P, CH, T])
        cum = sb("cum", [P, CH * T + 64])
        dec = sb("dec", [P, CH * NQ, P + 1])
        lev = [sb(f"lev{i}_kr", [P, CH * T]) for i in range(3)]
        pair_q = [sb(f"pair_q{i}", [P, NQ * HEADS * 64]) for i in range(2)]
        att = sb("att", [P, NQ * HEADS * P])
        S = sb("S", [P, NQ + 1, CH, P])
        bonus = sb("bonus_sb", [P, NQ * HEADS])
        x1 = sb("x1", [P, NQ, C])
        x1_prev = sb("x1_prev", [P, NQ, C])
        stats = sb("stats", [P, NQ * 6])
        meanvar = sb("meanvar", [P, NQ * 2])
        var_eps = sb("var_eps", [P, NQ * HEADS])
        rstd = sb("rstd", [P, NQ * HEADS])
        gsum = sb("gsum", [P, NQ * HEADS])
        th = [sb(f"th{i}", [P, 512]) for i in range(2)]
        thF = sb("thF", [P, NQ * C])
        hid = sb("hid", [P, 8, T])
        habs = sb("habs", [P, 4, T])
        beats = sb("beats", [P, 6, T], BF16)
        wins = sb("wins", [P, 4, T], BF16)
        xxxT = k0f = k0n = ygT = mixed["w"]
        y, yc, ysq, ynT = mixed["k"], mixed["r"], mixed["v"], mixed["g"]
        prodT = dxT

        xn1T = sb("xn1T", [P, CH, T])
        BC = sb("BC", [P, 2, SEQ_T, SH])
        cs_row = sb("cs_row", [P, 2 * SCH, P])
        cs_half = sb("cs_half", [P, SEQ_T * SH])
        prefix = sb("prefix", [P, NQ * SH])
        cs_nat = sb("cs_nat", [P, NQ, SH])
        cs16 = sb("cs16", [NQ * SCH, P])
        cs_col = sb("cs_col", [P, NQ * SCH])
        to_end = sb("to_end", [P, NQ * SCH])
        chunk_dec = sb("chunk_dec", [P, SCH])
        sp = [sb(f"sp{i}", [P, NQ * SH]) for i in range(4)]
        S1 = sb("S1", [P, SCH, SD])
        gate = sb("gate", [P, SH // 2, T])
        thB = [sb(f"thB{i}", [P, 512]) for i in range(2)]
        thFB = sb("thFB", [P, NQ * C])
        hidB = sb("hidB", [P, 8, T])
        Xnat = gate[:, :, :].rearrange("p a b -> p (a b)").rearrange("p (q n) -> p q n", q=NQ)
        Brow, Xrow = (hidB[:, 4 * i:4 * i + 4, :].rearrange("p a b -> p (a b)").rearrange(
            "p (q c d) -> p q c d", q=NQ, c=SCH) for i in range(2))
        xn1 = habs[:, 0:2, :]

        bank = [ctx.enter_context(nc.psum_tensor(f"bank{b}", [P, 512], F32)) for b in range(BANKS)]

        def ps(name):
            return bank[BANK[name]]

        filled = [sem(f"filled{b}") for b in range(BANKS)]
        freed = [sem(f"freed{b}") for b in range(BANKS)]
        loads = {g: sem("loads_" + g) for g in ("vecs", "ffn0", "mix", "proj", "down0", "ssd", "ffn1")}
        x_loaded = sem("x_loaded")
        const_ready = sem("const_ready")
        masks_ready = sem("masks_ready")
        pool_step = sem("pool_step")
        act_step = sem("act_step")
        dve_step = sem("dve_step")
        passed = sem("passed")
        carry_ready = sem("carry_ready")
        xn_ready = sem("xn_ready")
        xn1_ready = sem("xn1_ready")
        xxx_ready = sem("xxx_ready")
        a_ready = sem("a_ready")
        mix_ready = sem("mix_ready")
        cum_ready = sem("cum_ready")
        g_tanh = sem("g_tanh")
        arg_ready = sem("arg_ready")
        fac_ready = sem("fac_ready")
        dec0_ready = sem("dec0_ready")
        lev_ready = sem("lev_ready")
        prod_ready = sem("prod_ready")
        th_ready = sem("th_ready")
        thB_ready = sem("thB_ready")
        abs_ready = sem("abs_ready")
        sparse_ready = sem("sparse_ready")
        yc_ready = sem("yc_ready")
        ysq_ready = sem("ysq_ready")
        var_ready = sem("var_ready")
        rstd_ready = sem("rstd_ready")
        yn_ready = sem("yn_ready")
        yg_ready = sem("yg_ready")
        thF_ready = sem("thF_ready")
        thFB_ready = sem("thFB_ready")
        x1_loaded = sem("x1_loaded")
        x1_ready = sem("x1_ready")
        out_ready = sem("out_ready")
        out_stored = sem("out_stored")
        x1_saved = sem("x1_saved")
        soft_ready = sem("soft_ready")
        prefix_ready = sem("prefix_ready")
        cs_stored = sem("cs_stored")
        cs_loaded = sem("cs_loaded")
        X_stored = sem("X_stored")
        X_rows = sem("X_rows")
        res_tanh = sem("res_tanh")
        cs_half_exp = sem("cs_half_exp")
        end_arg = sem("end_arg")
        to_end_ready = sem("to_end_ready")
        cs_masked = sem("cs_masked")
        L_exp = sem("L_exp")
        Cdec_ready = sem("Cdec_ready")

        block = ctx.enter_context(nc.Block())

        class Steps:

            def __init__(self, eng, s):
                self.eng, self.s, self.n = eng, s, 0

            def did(self, ins):
                self.n += 1
                ins.then_inc(self.s, 1)
                return self.n

            def after(self, n=None):
                if self.n:
                    self.eng.wait_ge(self.s, self.n if n is None else n)

            def restart(self):
                self.after()
                self.eng.sem_clear(self.s)
                self.n = 0

        def wait_filled(eng, t, name):
            eng.wait_ge(filled[BANK[name]], t.count(PER[BANK[name]], NTH[name]))

        def wait_freed(eng, t, name):
            eng.wait_ge(freed[BANK[name]], t.count(PER[BANK[name]], NTH[name] + 1))

        def free(ins, name):
            ins.then_inc(freed[BANK[name]], 1)

        def flat(t):
            return t[:, :, :].rearrange("p a b -> p (a b)")

        def second_halves(t, s, par):
            return t[64 * par:64 * par + 64, :].rearrange("p (g b two s) -> p g b two s", g=CH * NQ, two=2, s=s)[:, :, :, 1, :]

        def paired(t, s, par):
            return t[64 * par:64 * par + 64, :].rearrange("p (g e b s) -> p g e b s", g=CH * NQ, e=2, s=s)[:, :, par, :, :]

        def key_rows(s):
            return P - s if s >= 32 else P

        cs_dram, x_dram = A["cs_dram"], A["x_dram"]

        def rounds(eng, one, first=0):
            one(Tile(None, 0), None)
            with eng.Fori(1, NT) as it:
                one(Tile(it), Tile(it, -1))
            one(None, Tile(None, NT - 1))

        @block.sync
        def _(sp_):
            def load(names, group):
                for n in names:
                    dst = W[n] if n in ("w_mix2b", "w_dec2") else W[n][:, :]
                    sp_.dma_start(dst, A[n]).then_inc(loads[group], 16)

            def tokens(name, first):
                return A[name][bass.ds(first, T), :].rearrange("(q p) c -> p q c", p=P)

            def wait(s, value):
                sp_.wait_ge(s, value)
                sp_.sem_inc(passed, 1)

            def one(a, b, last=False):
                if a:
                    wait(xn_ready, a.count(1, 1))
                    sp_.dma_start(X[:, :, :], tokens("x", a.at() * T if last else a.next().at() * T)).then_inc(x_loaded, 16)
                    wait(x1_saved, a.count(1, 1))
                    if b:
                        wait(xn1_ready, b.count(1, 1))
                    sp_.dma_start(x1[:, :, :], tokens("x", a.at() * T)).then_inc(x1_loaded, 16)
                if b:
                    wait_freed(sp_, b, "X1")
                    sp_.sem_inc(passed, 1)
                    wait(X_rows, b.count(16, 16))
                    sp_.dma_start(x_dram.rearrange("(q p n) -> p q n", q=NQ, p=P), Xnat).then_inc(X_stored, 16)
                    wait_freed(sp_, b, "csum")
                    sp_.sem_inc(passed, 1)
                    wait(cs_loaded, b.count(64, 16))
                    sp_.dma_start(cs_dram.rearrange("(q p h) -> p q h", q=NQ, p=P), cs_nat[:, :, :]).then_inc(cs_stored, 16)
                    wait(cs_stored, b.count(16, 32))
                    sp_.dma_start(cs16[:, :], cs_dram.rearrange("(c p) -> c p", p=P)).then_inc(cs_loaded, 16)
                    sp_.dma_start(flat(cs_row), cs_dram.partition_broadcast(P)).then_inc(cs_loaded, 16)
                    n = SEQ_T * SH
                    for q in range(NQ):
                        sp_.dma_start(cs_half[64 * q:64 * q + 64, :],
                                      cs_dram[q * n:(q + 1) * n].partition_broadcast(64)).then_inc(cs_loaded, 16)
                    wait(X_stored, b.count(16, 32))
                    sp_.dma_start(Xrow.rearrange("p q c d -> p (q c) d"),
                                  x_dram.rearrange("(c p d) -> p c d", p=P, d=SD)).then_inc(X_rows, 16)
                    wait(out_ready, b.count(1, 2))
                    sp_.dma_start(tokens("out", b.at() * T), thFB[:, :].rearrange("p (q c) -> p q c", q=NQ)).then_inc(
                        out_stored, 16)

            for s in (X_rows, X_stored, cs_stored, cs_loaded, out_stored):
                sp_.sem_inc(s, 16)
            for s in (x1_saved, out_ready):
                sp_.sem_inc(s, 1)
            load(["vecs"], "vecs")
            sp_.dma_start(X[:, :, :], tokens("x", 0)).then_inc(x_loaded, 16)
            load(["f_gate", "f_up"], "ffn0")
            load(["w_mix1", "w_mix2a", "w_mix2b"], "mix")
            load(["w_dec1", "w_dec2", "w_rkvgo"], "proj")
            load(["f_down"], "down0")
            load(["w_dt", "w_X", "w_B", "w_C", "w_res", "w_sout"], "ssd")
            load(["n_gate", "n_up", "n_down"], "ffn1")
            one(Tile(None, 0), None)
            with sp_.Fori(1, NT - 1) as it:
                one(Tile(it), Tile(it, -1))
            one(Tile(None, NT - 1), Tile(None, NT - 2), last=True)
            one(None, Tile(None, NT - 1))
            sp_.wait_ge(out_stored, 16 * (NT + 1))

        @block.gpsimd
        def _(pool):
            steps = Steps(pool, pool_step)

            def did(ins):
                steps.did(ins)
                steps.after()

            g = nc.gpsimd
            did(g.memset(ident[:, :], 0.0))
            did(g.affine_select(out=ident[:, :], in_=ident[:, :], compare_op=ALU.not_equal, fill=1.0, base=0,
                                pattern=[[-1, P]], channel_multiplier=1))
            did(g.memset(half_neg[:, :], -0.5))
            g.memset(rstd[:, :], 1.0).then_inc(const_ready, 1)

            def rsqrt(count, n):
                pool.wait_ge(var_ready, count)
                g.tensor_tensor(rstd[:, 0:n], var_eps[:, 0:n], half_neg[:, 0:n], ALU.pow).then_inc(rstd_ready, 1)

            pool.wait_ge(const_ready, 2)
            rsqrt(1, NQ)
            did(g.memset(causal[:, :], 0.0))
            did(g.affine_select(out=causal[:, :], in_=causal[:, :], compare_op=ALU.is_ge, fill=NEG, base=0,
                                pattern=[[1, P]], channel_multiplier=-1))
            did(g.memset(before[:, :], 1.0))
            bv = before[:, :].rearrange("p (b q) -> p b q", q=CHT)
            did(g.affine_select(out=bv, in_=bv, compare_op=ALU.is_ge, fill=0.0, base=0,
                                pattern=[[-CHT, P // CHT], [0, CHT]], channel_multiplier=1))
            did(g.affine_select(out=bv, in_=bv, compare_op=ALU.is_gt, fill=0.0, base=0,
                                pattern=[[CHT, P // CHT], [1, CHT]], channel_multiplier=-1))
            for n, s in enumerate(LEVELS):
                tmp = lev[n % 2][:, 0:64]
                tv = tmp.rearrange("p (b q) -> p b q", q=s)
                did(g.memset(tmp, 1.0))
                did(g.affine_select(out=tv, in_=tv, compare_op=ALU.is_ge, fill=0.0, base=0,
                                    pattern=[[-2 * s, 64 // s], [0, s]], channel_multiplier=1))
                did(g.affine_select(out=tv, in_=tv, compare_op=ALU.is_ge, fill=0.0, base=s - 1,
                                    pattern=[[2 * s, 64 // s], [0, s]], channel_multiplier=-1))
                did(g.tensor_copy(masks[:, n, :].rearrange("p (r x) -> p r x", x=64),
                                  tmp.unsqueeze(1).to_broadcast([P, NQ * HEADS, 64])))
            pool.sem_inc(masks_ready, 1)
            steps.restart()

            def one(a, b):
                if a:
                    rsqrt(a.count(3, 2), NQ)
                if b:
                    pool.wait_ge(cs_loaded, b.count(64, 80))
                    g.tensor_tensor(cs_row[:, :, :], cs_row[:, :, :],
                                    causal[:, :].unsqueeze(1).to_broadcast([P, NQ * SCH, P]),
                                    ALU.add).then_inc(cs_masked, 1)
                    pool.wait_ge(cs_half_exp, b.count(1, 1))
                    wait_freed(pool, b, "C1")
                    g.tensor_tensor(cs_half[:, :], cs_half[:, :], BC[:, 1, :, :].rearrange("p t h -> p (t h)"),
                                    ALU.mult).then_inc(Cdec_ready, 1)
                if a:
                    rsqrt(a.count(3, 3), NQ * HEADS)
                    rsqrt(a.count(3, 4), NQ)

            rounds(pool, one)

        @block.scalar
        def _(act):
            steps = Steps(act, act_step)
            a_ = nc.scalar

            def ffn_tanh(t, name, buf, ready, made=None):
                wait_filled(act, t, name + "g")
                if made:
                    wait_freed(act, t, made + "u")
                a_.activation(buf[:, :], ps(name + "g")[:, :], ACT.Tanh, scale=0.5).then_inc(ready, 1)

            def ffn_abs(t, n):
                wait_freed(act, t, f"p{n}u")
                if n >= 2:
                    act.wait_ge(sparse_ready, t.count(2, 1))
                i = 2 * (n % 2)
                a_.activation(habs[:, i:i + 2, :], hid[:, 2 * n:2 * n + 2, :], ACT.Abs).then_inc(abs_ready, 1)

            def copy(t, dst, name, parts):
                wait_filled(act, t, name)
                free(a_.activation(dst, ps(name)[:, :].rearrange("p (h t) -> p h t", h=parts), ACT.Identity), name)

            def level_exp(t, n):
                act.wait_ge(arg_ready, t.count(7, n + 1))
                a_.activation(lev[n % 3][:, :], lev[n % 3][:, :], ACT.Exp).then_inc(fac_ready, 1)

            def bc(t, name, which, pair):
                wait_filled(act, t, name)
                src = ps(name)[:, :].rearrange("p (m s t) -> p m s t", m=2, s=NQ)
                for par in range(2):
                    for s in range(NQ):
                        cols = BC[64 * s:64 * s + 64, which, :, :].rearrange("p t (m e) -> p e m t", e=2)
                        ins = a_.activation(cols[:, par, 2 * pair:2 * pair + 2, :],
                                            src[64 * par:64 * par + 64, :, s, :], ACT.Identity)
                free(ins, name)

            def x_copy(t, q):
                act.wait_ge(X_stored, t.count(16, 16))
                wait_filled(act, t, f"X{q}")
                free(a_.activation(Xnat[:, q, :], ps(f"X{q}")[:, :], ACT.Identity), f"X{q}")

            def xnT_copy(t):
                wait_filled(act, t, "xT")
                free(a_.activation(xnT[:, :, 1:T + 1], ps("xT")[:, :].rearrange("p (h t) -> p h t", h=CH),
                                   ACT.Identity), "xT")

            def one(a, b):
                if b:
                    act.wait_ge(x1_ready, b.count(1, 1))
                    act.wait_ge(out_ready, b.count(1, 1))
                    a_.activation(flat(x1_prev), flat(x1), ACT.Identity).then_inc(x1_saved, 1)
                if a:
                    ffn_tanh(a, "p0", th[0], th_ready)
                    wait_filled(act, a, "a")
                    a_.activation(aT[:, :], ps("a")[:, 0:T], ACT.Tanh).then_inc(a_ready, 1)
                    free(a_.activation(aT4, ps("a")[0:DMIX, T:2 * T], ACT.Tanh), "a")
                if b:
                    copy(b, xn1T[:, :, :], "xT1", CH)
                if a:
                    ffn_tanh(a, "p1", th[1], th_ready)
                    ffn_abs(a, 0)
                if b:
                    wait_filled(act, b, "dt")
                    steps.did(a_.activation(sp[0][:, :], ps("dt")[:, 0:NQ * SH], ACT.Abs))
                    steps.after()
                    steps.did(a_.activation(sp[1][:, :], sp[0][:, :], ACT.Exp, scale=-1.0))
                    steps.after()
                    a_.activation(sp[2][:, :], sp[1][:, :], ACT.Ln, bias=1.0).then_inc(soft_ready, 1)
                    x_copy(b, 0)
                if a:
                    ffn_abs(a, 1)
                if b:
                    x_copy(b, 1)
                if a:
                    wait_filled(act, a, "dw")
                    free(a_.activation(decT, ps("dw")[DDEC:P, 0:T], ACT.Tanh), "dw")
                if b:
                    bc(b, "B0", 0, 0)
                if a:
                    copy(a, kT[:, :, :], "k", CH)
                if b:
                    bc(b, "B1", 0, 1)
                if a:
                    wait_filled(act, a, "w")
                    for h in range(CH):
                        ins = a_.activation(lev[2][:, h * T:(h + 1) * T], ps("w")[:, h * T:(h + 1) * T], ACT.Exp,
                                            bias=vec[:, 2 * VEC["decay"] + h:2 * VEC["decay"] + h + 1])
                    free(ins, "w")
                    wait_filled(act, a, "r")
                    a_.activation(flat(rT), ps("r")[:, :], ACT.Identity)
                    for par in range(2):
                        ins = a_.activation(paired(pair_q[1], 1, par), second_halves(ps("r")[:, :], 1, par), ACT.Identity)
                    free(ins, "r")
                if b:
                    bc(b, "C0", 1, 0)
                if a:
                    level_exp(a, 0)
                    level_exp(a, 1)
                    act.wait_ge(cum_ready, a.count(1, 1))
                    a_.activation(dec[:, :, 1:P + 1], cum[:, 0:CH * T].rearrange("p (a b) -> p a b", b=P), ACT.Exp,
                                  scale=-1.0).then_inc(dec0_ready, 1)
                    copy(a, v[:, :, :], "v", NQ)
                if b:
                    bc(b, "C1", 1, 1)
                if a:
                    level_exp(a, 2)
                    wait_filled(act, a, "g")
                    a_.activation(flat(gT), ps("g")[:, :], ACT.Tanh, scale=0.5).then_inc(g_tanh, 1)
                if b:
                    act.wait_ge(X_stored, b.count(16, 32))
                    for n in range(2):
                        wait_filled(act, b, f"res{n}")
                        a_.activation(gate[:, 2 * n:2 * n + 2, :].rearrange("p a b -> p (a b)"), ps(f"res{n}")[:, :],
                                      ACT.Tanh, scale=0.5).then_inc(res_tanh, 1)
                    act.wait_ge(cs_loaded, b.count(64, 80))
                    steps.did(a_.activation(chunk_dec[:, :], cs_half[:, :].rearrange("p (c w) -> p c w", w=P)[:, :, P - 1],
                                            ACT.Exp))
                    steps.after()
                    a_.activation(cs_half[:, :], cs_half[:, :], ACT.Exp).then_inc(cs_half_exp, 1)
                if a:
                    level_exp(a, 3)
                    level_exp(a, 4)
                if b:
                    act.wait_ge(end_arg, b.count(1, 1))
                    a_.activation(to_end[:, :], to_end[:, :], ACT.Exp).then_inc(to_end_ready, 1)

                def L_exps(s):
                    act.wait_ge(cs_masked, b.count(1, 1))
                    for n in range(s * SCH, (s + 1) * SCH):
                        ins = a_.activation(cs_row[:, n, :], cs_row[:, n, :], ACT.Exp, bias=cs_col[:, n:n + 1])
                    ins.then_inc(L_exp, 1)

                if b:
                    L_exps(0)
                if a:
                    level_exp(a, 5)
                if b:
                    L_exps(1)
                if a:
                    act.wait_ge(arg_ready, a.count(7, 7))
                    a_.activation(flat(k0f), flat(k0f), ACT.Exp).then_inc(fac_ready, 1)
                    ffn_tanh(a, "p2", th[0], th_ready, "p0")
                    ffn_tanh(a, "p3", th[1], th_ready, "p1")
                    copy(a, k0n[:, :, :], "k0T", NQ)
                    ffn_abs(a, 2)
                    ffn_abs(a, 3)
                if b:
                    ffn_tanh(b, "n0", thB[0], thB_ready)
                if a:
                    act.wait_ge(yc_ready, a.count(1, 1))
                    a_.activation(flat(ysq), flat(yc), ACT.Square).then_inc(ysq_ready, 1)
                    wait_filled(act, a, "F0")
                    a_.activation(thF[:, :], ps("F0")[:, :], ACT.Tanh, scale=0.25).then_inc(thF_ready, 1)
                    wait_filled(act, a, "yT")
                    for h in range(CH):
                        g0, b0 = 2 * VEC["gamma"] + h, 2 * VEC["beta"] + h
                        ins = a_.activation(ynT[:, h, :], ps("yT")[:, h * T:(h + 1) * T], ACT.Identity,
                                            scale=vec[:, g0:g0 + 1], bias=vec[:, b0:b0 + 1])
                    free(ins, "yT")
                if b:
                    ffn_tanh(b, "n1", thB[1], thB_ready)
                if b:
                    ffn_tanh(b, "n2", thB[0], thB_ready, "n0")
                    ffn_tanh(b, "n3", thB[1], thB_ready, "n1")
                    act.wait_ge(out_stored, b.count(16, 16))
                    wait_filled(act, b, "F1")
                    a_.activation(thFB[:, :], ps("F1")[:, :], ACT.Tanh, scale=0.25).then_inc(thFB_ready, 1)
                if a:
                    act.wait_ge(carry_ready, a.count(1, 1))
                    xnT_copy(a.next())
                steps.restart()

            act.wait_ge(loads["vecs"], 16)
            act.wait_ge(const_ready, 2)
            xnT_copy(Tile(None, 0))
            rounds(act, one)

        @block.vector
        def _(dve):
            steps = Steps(dve, dve_step)
            did, after = steps.did, steps.after
            d = nc.vector

            for t in (flat(xnT), att[:, :], pair_q[0][:, :], pair_q[1][:, :], S[:, :, :, :].rearrange("p a b c -> p (a b c)"), flat(head_sel)):
                did(d.memset(t, 0.0))
            for t in (flat(dec), chunk_reset[:, :], head_reset[:, :], keep[:, :]):
                did(d.memset(t, 1.0))
            after()
            for t in (chunk_reset[:, :].rearrange("p (a b) -> p a b", b=P)[:, :, 0:1],
                      head_reset[:, :].rearrange("p (a b) -> p a b", b=SH)[:, :, 0:1],
                      keep[:, 0:NT].rearrange("p (a b) -> p a b", b=NT // BATCH)[:, :, 0:1]):
                did(d.memset(t, 0.0))
            for h in range(HEADS):
                did(d.memset(head_sel[64 * (h % 2):64 * (h % 2) + 64, h // 2, h:h + 1], 1.0))
            after()
            dve.sem_inc(const_ready, 1)

            def norm_stats(src):
                for q in range(NQ):
                    did(d.bn_stats(stats[:, 6 * q:6 * q + 6], src[:, q, :]))
                after()
                for q in range(NQ):
                    did(d.bn_aggr(meanvar[:, 2 * q:2 * q + 2], stats[:, 6 * q:6 * q + 6]))
                after()
                mv = meanvar[:, :].rearrange("p (q two) -> p q two", two=2)
                d.tensor_scalar(var_eps[:, 0:NQ], mv[:, :, 1], LN_EPS, None, ALU.add).then_inc(var_ready, 1)

            def norm_apply(src, dst, rstd_count, ready):
                dve.wait_ge(rstd_ready, rstd_count)
                for q in range(NQ):
                    ins = d.tensor_scalar(dst[:, q, :], src[:, q, :], meanvar[:, 2 * q:2 * q + 1], rstd[:, q:q + 1],
                                          ALU.subtract, ALU.mult)
                    if q < NQ - 1:
                        did(ins)
                ins.then_inc(ready, 1)

            dve.wait_ge(const_ready, 2)
            dve.wait_ge(x_loaded, 16)
            norm_stats(X)
            norm_apply(X, xn, 1, xn_ready)
            steps.restart()
            dve.wait_ge(loads["vecs"], 16)

            def vcol(name, h):
                return vec[:, 2 * VEC[name] + h:2 * VEC[name] + h + 1]

            def hidden(t, name, n, buf, ready, out):
                dve.wait_ge(ready, t.count(4, n + 1))
                free(d.scalar_tensor_tensor(out=buf[:, :], in0=buf[:, :], scalar=1.0, in1=ps(name + "g")[:, :],
                                            op0=ALU.add, op1=ALU.mult), name + "g")
                wait_freed(dve, t, name + "g")
                wait_filled(dve, t, name + "u")
                free(d.tensor_tensor(out[:, 2 * n:2 * n + 2, :].rearrange("p a b -> p (a b)"), buf[:, :],
                                     ps(name + "u")[:, :], ALU.mult), name + "u")

            def hidden_p(t, n):
                hidden(t, f"p{n}", n, th[n % 2], th_ready, hid)

            def hidden_n(t, n):
                hidden(t, f"n{n}", n, thB[n % 2], thB_ready, hidB)

            def mix_scaled(t, f):
                wait_filled(dve, t, "mix_" + f)
                for h in range(CH):
                    ins = d.scalar_tensor_tensor(out=mixed[f][:, h, :], in0=ps("mix_" + f)[:, h * T:(h + 1) * T],
                                                 scalar=vcol("maa_" + f, h), in1=dxT[:, h, :],
                                                 op0=ALU.add, op1=ALU.mult)
                    if h == 0:
                        did(ins)
                free(ins, "mix_" + f)

            def mix_add(t, f):
                wait_freed(dve, t, "mix_" + f)
                d.tensor_tensor(mixed[f][:, :, :], mixed[f][:, :, :], xnT[:, :, 1:T + 1],
                                ALU.add).then_inc(mix_ready, 1)

            def halves(t, s):
                return t.rearrange("p (b two s) -> p b two s", two=2, s=s)

            def level_args(n):
                s = LEVELS[n]
                c, f = halves(cum[:, 0:CH * T], s), halves(lev[n % 3][:, :], s)
                one_back = cum[:, s - 1:s - 1 + CH * T].rearrange("p (b w) -> p b w", w=2 * s)[:, :, 0:s]
                mid = c[:, :, 0, s - 1:s].to_broadcast([P, CH * T // (2 * s), s])
                did(d.tensor_tensor(f[:, :, 0, :], c[:, :, 0, :], mid, ALU.subtract))
                d.tensor_tensor(f[:, :, 1, :], mid, one_back, ALU.subtract).then_inc(arg_ready, 1)

            def level_scale(t, n):
                s = LEVELS[n]
                dve.wait_ge(fac_ready, t.count(7, n + 1))
                f, kk = halves(lev[n % 3][:, :], s), halves(flat(kT), s)
                did(d.tensor_tensor(f[:, :, 0, :], f[:, :, 0, :], kk[:, :, 0, :], ALU.mult))
                for par in range(2):
                    ins = d.tensor_tensor(paired(pair_q[n % 2], s, par), second_halves(lev[n % 3][:, :], s, par),
                                          second_halves(flat(rT), s, par), ALU.mult)
                    if par == 0:
                        did(ins)
                ins.then_inc(lev_ready, 1)

            def level_take(t, n):
                s = LEVELS[n]
                name, r = f"lev{s}", slice(0, key_rows(s))
                if s > 1:
                    wait_freed(dve, t, f"lev{LEVELS[n - 1]}")
                wait_filled(dve, t, name)
                dve.sem_inc(passed, 1)
                out = att[r, :].rearrange("p (b w) -> p b w", w=2 * s)[:, :, s:2 * s]
                free(d.copy_predicated(out, masks[r, n, :].rearrange("p (b s) -> p b s", s=s),
                                       ps(name)[r, :].rearrange("p (b s) -> p b s", s=s)), name)

            def sparsify(t, m):
                dve.wait_ge(abs_ready, t.count(4, 2 * m + 2))
                for i, first, count in ((0, 0, 3), (1, 3, 2), (2, 5, 1)):
                    did(d.tensor_tensor(beats[:, first:first + count, :],
                                        habs[:, i:i + 1, :].to_broadcast([P, count, T]),
                                        habs[:, i + 1:4, :], ALU.is_ge))
                after()
                B01, B02, B03, B12, B13, B23 = (beats[:, n, :] for n in range(6))
                W0, W1, W2, W3 = (wins[:, n, :] for n in range(4))
                did(d.tensor_tensor(W0, B01, B02, ALU.add))
                did(d.tensor_tensor(W1, B12, B13, ALU.add))
                did(d.tensor_tensor(W2, B23, B02, ALU.subtract))
                n3 = did(d.tensor_tensor(W3, B03, B13, ALU.add))
                after(n3 - 3)
                did(d.tensor_tensor(W0, W0, B03, ALU.add))
                after(n3 - 2)
                did(d.tensor_tensor(W1, W1, B01, ALU.subtract))
                after(n3 - 1)
                did(d.tensor_tensor(W2, W2, B12, ALU.subtract))
                after(n3)
                did(d.tensor_tensor(W3, W3, B23, ALU.add))
                for i, (w, least, op) in enumerate([(W0, 1.5, ALU.is_ge), (W1, 0.5, ALU.is_ge), (W2, -0.5, ALU.is_ge),
                                                    (W3, 1.5, ALU.is_le)]):
                    after(n3 + 1 + i)
                    ins = d.scalar_tensor_tensor(out=hid[:, 4 * m + i, :], in0=w, scalar=least,
                                                 in1=hid[:, 4 * m + i, :], op0=op, op1=ALU.mult)
                    if i < 3:
                        did(ins)
                ins.then_inc(sparse_ready, 1)

            def one(a, b):
                if a:
                    did(d.tensor_scalar(S[:, 0:1, :, :].rearrange("p z a b -> p (z a b)"),
                                        S[:, NQ:NQ + 1, :, :].rearrange("p z a b -> p (z a b)"),
                                        keep[:, bass.ds(a.at(), 1)], None, ALU.mult))
                    wait_freed(dve, a, "xT")
                    did(d.tensor_tensor(dxT[:, :, :], xnT[:, :, 0:T], xnT[:, :, 1:T + 1], ALU.subtract))
                    after()
                    for h in range(CH):
                        ins = d.scalar_tensor_tensor(out=xxxT[:, h, :], in0=dxT[:, h, :], scalar=vcol("maa_x", h),
                                                     in1=xnT[:, h, 1:T + 1], op0=ALU.mult, op1=ALU.add)
                        if h == 0:
                            did(ins)
                    ins.then_inc(xxx_ready, 1)
                    hidden_p(a, 0)
                    hidden_p(a, 1)
                    mix_scaled(a, "w")
                    mix_scaled(a, "k")
                    mix_add(a, "w")
                if b:
                    dve.wait_ge(soft_ready, b.count(1, 1))
                    free(d.scalar_tensor_tensor(out=sp[3][:, :], in0=ps("dt")[:, 0:NQ * SH], scalar=0.0, in1=sp[2][:, :],
                                                op0=ALU.max, op1=ALU.add), "dt")
                    wait_freed(dve, b, "dt")
                    d.tensor_tensor_scan(prefix[:, :], head_reset[:, :], sp[3][:, :], 0.0, ALU.mult,
                                         ALU.add).then_inc(prefix_ready, 1)
                if a:
                    mix_scaled(a, "r")
                    mix_add(a, "k")
                    mix_scaled(a, "v")
                    mix_add(a, "r")
                if b:
                    dve.wait_ge(prefix_ready, b.count(1, 1))
                    dve.wait_ge(cs_stored, b.count(16, 16))
                    wait_filled(dve, b, "csum")
                    free(d.scalar_tensor_tensor(out=cs_nat[:, :, :], in0=prefix[:, :].rearrange("p (q h) -> p q h", h=SH),
                                                scalar=-1.0,
                                                in1=ps("csum")[:, 0:NQ].unsqueeze(2).to_broadcast([P, NQ, SH]),
                                                op0=ALU.mult, op1=ALU.subtract), "csum")
                if a:
                    mix_add(a, "v")
                    wait_freed(dve, a, "w")
                    did(d.tensor_scalar(lev[2][:, :], lev[2][:, :], DECAY_CAP, None, ALU.min))
                    mix_scaled(a, "g")
                    after()
                    for h in range(CH):
                        ins = d.tensor_tensor_scan(cum[:, h * T:(h + 1) * T], chunk_reset[:, :],
                                                   lev[2][:, h * T:(h + 1) * T], 0.0, ALU.mult, ALU.add)
                        if h == 0:
                            did(ins)
                    ins.then_inc(cum_ready, 1)
                    mix_add(a, "g")
                    dve.wait_ge(cum_ready, a.count(1, 1))
                    dve.wait_ge(masks_ready, 1)
                    level_args(0)
                    level_args(1)
                    dve.wait_ge(x_loaded, a.count(16, 32))
                    norm_stats(X)
                    level_take(a, 6)
                    level_scale(a, 0)
                    level_args(2)
                    level_scale(a, 1)
                    norm_apply(X, xn, a.count(3, 2), xn_ready)
                    dve.wait_ge(g_tanh, a.count(1, 1))
                    free(d.scalar_tensor_tensor(out=flat(gT), in0=flat(gT), scalar=1.0, in1=ps("g")[:, :],
                                                op0=ALU.add, op1=ALU.mult), "g")
                if b:
                    for n in range(2):
                        dve.wait_ge(res_tanh, b.count(2, n + 1))
                        gv = gate[:, 2 * n:2 * n + 2, :].rearrange("p a b -> p (a b)")
                        free(d.scalar_tensor_tensor(out=gv, in0=gv, scalar=1.0, in1=ps(f"res{n}")[:, :],
                                                    op0=ALU.add, op1=ALU.mult), f"res{n}")
                if a:
                    level_take(a, 0)
                    level_args(3)
                    level_scale(a, 2)
                    level_take(a, 1)
                    level_args(4)
                    level_scale(a, 3)

                if b:
                    wait_filled(dve, b, "csT")
                    free(d.tensor_scalar(cs_col[:, :], ps("csT")[:, 0:NQ * SCH], -1.0, None, ALU.mult), "csT")
                    wait_freed(dve, b, "csT")
                    dve.wait_ge(cs_masked, b.count(1, 1))
                    d.tensor_tensor(to_end[:, :], cs_row[:, :, P - 1], cs_col[:, :], ALU.add).then_inc(end_arg, 1)
                    dve.wait_ge(to_end_ready, b.count(1, 1))
                    for s in range(NQ):
                        wait_filled(dve, b, f"bt{s}")
                        free(d.tensor_tensor(Brow[:, s, 0:SCH - 1, :],
                                             ps(f"bt{s}")[:, 0:(SCH - 1) * SD].rearrange("p (c d) -> p c d", d=SD),
                                             to_end[:, s * SCH:(s + 1) * SCH - 1].unsqueeze(2).to_broadcast(
                                                 [P, SCH - 1, SD]), ALU.mult), f"bt{s}")
                if a:
                    level_take(a, 2)
                    level_args(5)
                    level_scale(a, 4)
                    level_take(a, 3)
                    cq = cum[:, 0:CH * T].rearrange("p (a b) -> p a b", b=P)
                    d.tensor_tensor(flat(k0f).rearrange("p (a b) -> p a b", b=P), cq,
                                    cq[:, :, P - 1:P].to_broadcast([P, CH * NQ, P]),
                                    ALU.subtract).then_inc(arg_ready, 1)
                    level_scale(a, 5)
                    for h in range(CH):
                        ins = d.scalar_tensor_tensor(out=prodT[:, h, :], in0=kT[:, h, :], scalar=vcol("bonus", h),
                                                     in1=rT[:, h, :], op0=ALU.mult, op1=ALU.mult)
                        if h == 0:
                            did(ins)
                    ins.then_inc(prod_ready, 1)
                    level_take(a, 4)
                if b:
                    for n in range(4):
                        dve.wait_ge(L_exp, b.count(NQ, n // 2 + 1))
                        wait_filled(dve, b, f"sc{n}")
                        w = flat(cs_row)[:, n * 512:(n + 1) * 512]
                        free(d.tensor_tensor(w, w, ps(f"sc{n}")[:, :], ALU.mult), f"sc{n}")
                if a:
                    hidden_p(a, 2)
                    level_take(a, 5)
                    dve.wait_ge(fac_ready, a.count(7, 7))
                    wait_filled(dve, a, "lev1")
                    d.tensor_tensor(flat(kT), flat(kT), flat(k0f), ALU.mult).then_inc(prod_ready, 1)
                    dve.wait_ge(dec0_ready, a.count(1, 1))
                    rq = flat(rT).rearrange("p (a b) -> p a b", b=P)
                    d.tensor_tensor(rq, rq, dec[:, :, 0:P], ALU.mult).then_inc(prod_ready, 1)
                if b:
                    wait_filled(dve, b, "st")
                    dve.wait_ge(cs_half_exp, b.count(1, 1))
                    did(d.tensor_copy(S1[:, 1, :], ps("st")[:, 0:SD]))
                    for c in range(1, SCH - 1):
                        after()
                        ins = d.scalar_tensor_tensor(out=S1[:, c + 1, :], in0=S1[:, c, :], scalar=chunk_dec[:, c:c + 1],
                                                     in1=ps("st")[:, c * SD:(c + 1) * SD], op0=ALU.mult, op1=ALU.add)
                        if c < SCH - 2:
                            did(ins)
                    free(ins, "st")
                if a:
                    sparsify(a, 0)
                    hidden_p(a, 3)
                    d.tensor_scalar(xnT[:, :, 0:1], xnT[:, :, T:T + 1], keep[:, bass.ds(a.next().at(), 1)], None,
                                    ALU.mult).then_inc(carry_ready, 1)
                    wait_filled(dve, a, "kv")
                    kv = ps("kv")[:, :].rearrange("p (q h c) -> p q h c", q=NQ, h=CH)
                    for q in range(NQ):
                        if q:
                            after()
                        for h in range(CH):
                            for par in range(2):
                                r, cols = slice(64 * par, 64 * par + 64), slice(64 * par, 64 * par + 64)
                                ins = d.scalar_tensor_tensor(out=S[r, q + 1, h, cols], in0=S[r, q, h, cols],
                                                             scalar=dec[r, h * NQ + q, P:P + 1], in1=kv[r, q, h, cols],
                                                             op0=ALU.mult, op1=ALU.add)
                                if (q, h, par) != (NQ - 1, CH - 1, 1):
                                    did(ins)
                    free(ins, "kv")
                    sparsify(a, 1)
                    wait_filled(dve, a, "bonus")
                    free(d.tensor_copy(bonus[:, :], ps("bonus")[:, 0:NQ * HEADS]), "bonus")
                    wait_filled(dve, a, "y")
                    wait_freed(dve, a, "bonus")
                    for n in range(NQ * HEADS):
                        q, h = n // HEADS, n % HEADS
                        ins = d.scalar_tensor_tensor(out=y[:, q, h * HD:(h + 1) * HD], in0=v[:, q, h * HD:(h + 1) * HD],
                                                     scalar=bonus[:, n:n + 1],
                                                     in1=ps("y")[:, n * HD:(n + 1) * HD], op0=ALU.mult, op1=ALU.add)
                        if n < NQ * HEADS - 1:
                            did(ins)
                    free(ins, "y")
                    y3, yc3, ysq3 = (flat(t).rearrange("p (n d) -> p n d", d=HD) for t in (y, yc, ysq))
                    wait_freed(dve, a, "y")
                    did(d.tensor_reduce(gsum[:, :], y3, AX.X, ALU.add))
                    after()
                    did(d.tensor_scalar(gsum[:, :], gsum[:, :], 1.0 / HD, None, ALU.mult))
                    after()
                    d.tensor_tensor(yc3, y3, gsum[:, :].unsqueeze(2).to_broadcast([P, NQ * HEADS, HD]),
                                    ALU.subtract).then_inc(yc_ready, 1)
                if b:
                    for s in range(NQ):
                        wait_filled(dve, b, f"ys{s}")
                        gv = gate[:, :, s * P:(s + 1) * P]
                        free(d.tensor_tensor(gv, gv, ps(f"ys{s}")[:, :].rearrange("p (t m) -> p m t", m=SH // 2),
                                             ALU.mult), f"ys{s}")
                if a:
                    dve.wait_ge(ysq_ready, a.count(1, 1))
                    did(d.tensor_reduce(gsum[:, :], ysq3, AX.X, ALU.add))
                    after()
                    d.tensor_scalar(var_eps[:, :], gsum[:, :], 1.0 / HD, GN_EPS, ALU.mult, ALU.add).then_inc(var_ready, 1)
                if b:
                    hidden_n(b, 0)
                if a:
                    dve.wait_ge(rstd_ready, a.count(3, 3))
                    d.tensor_tensor(y3, yc3, rstd[:, :].unsqueeze(2).to_broadcast([P, NQ * HEADS, HD]),
                                    ALU.mult).then_inc(yn_ready, 1)
                    dve.wait_ge(thF_ready, a.count(1, 1))
                    free(d.scalar_tensor_tensor(out=thF[:, :], in0=thF[:, :], scalar=1.0, in1=ps("F0")[:, :],
                                                op0=ALU.add, op1=ALU.mult), "F0")
                    wait_freed(dve, a, "yT")
                    d.tensor_tensor(flat(ygT), flat(ynT), flat(gT), ALU.mult).then_inc(yg_ready, 1)
                if b:
                    hidden_n(b, 1)
                    hidden_n(b, 2)
                if a:
                    wait_filled(dve, a, "s0")
                    wait_freed(dve, a, "F0")
                    free(d.tensor_tensor(thF[:, :], thF[:, :], ps("s0")[:, :], ALU.mult), "s0")
                    wait_freed(dve, a, "s0")
                    dve.wait_ge(x1_loaded, a.count(16, 16))
                    d.scalar_tensor_tensor(out=flat(x1), in0=thF[:, :], scalar=0.125, in1=flat(x1),
                                           op0=ALU.mult, op1=ALU.add).then_inc(x1_ready, 1)
                    dve.wait_ge(x1_ready, a.count(1, 1))
                    norm_stats(x1)
                if b:
                    hidden_n(b, 3)
                    dve.wait_ge(thFB_ready, b.count(1, 1))
                    free(d.scalar_tensor_tensor(out=thFB[:, :], in0=thFB[:, :], scalar=1.0, in1=ps("F1")[:, :],
                                                op0=ALU.add, op1=ALU.mult), "F1")
                if a:
                    norm_apply(x1, xn1, a.count(3, 4), xn1_ready)
                if b:
                    wait_freed(dve, b, "F1")
                    wait_filled(dve, b, "s1")
                    free(d.tensor_tensor(thFB[:, :], thFB[:, :], ps("s1")[:, :], ALU.mult), "s1")
                    wait_freed(dve, b, "s1")
                    d.scalar_tensor_tensor(out=thFB[:, :], in0=thFB[:, :], scalar=0.125, in1=flat(x1_prev),
                                           op0=ALU.mult, op1=ALU.add).then_inc(out_ready, 1)
                steps.restart()

            rounds(dve, one)

        @block.tensor
        def _(pe):
            t_ = nc.tensor

            def open_bank(t, name):
                b = BANK[name]
                pe.wait_ge(freed[b], t.count(PER[b], NTH[name]))

            def close_bank(ins, name):
                ins.then_inc(filled[BANK[name]], 1)

            def project(t, name, parts, first_row=0):
                open_bank(t, name)
                for col, rows, ws, xs in parts:
                    for k, (w, x) in enumerate(zip(ws, xs)):
                        n = x.free_size()
                        ins = t_.matmul(ps(name)[first_row:first_row + rows, col:col + n], w, x, start=(k == 0),
                                        stop=(k == len(ws) - 1))
                close_bank(ins, name)

            def weights_first(t, name, w, k, cols, x, width=P):
                project(t, name, [(i * T, width, [w(h, c, width) for h in range(k)], [x(h) for h in range(k)])
                                  for i, c in enumerate(cols)])

            def packed(n, width):
                return lambda h, c, w: W[n][:, h * width + c:h * width + c + w]

            def halves_of(t):
                return lambda h: t[:, h, :]

            def ffn(t, name, gate_w, up_w, pair, x):
                for suffix, w in (("g", gate_w), ("u", up_w)):
                    weights_first(t, name + suffix, packed(w, HID), CH, [2 * pair * P, (2 * pair + 1) * P], x)

            def ffn_p(t, n):
                ffn(t, f"p{n}", "f_gate", "f_up", n, lambda h: xnT[:, h, 1:T + 1])

            def ffn_n(t, n):
                ffn(t, f"n{n}", "n_gate", "n_up", n, halves_of(xn1T))

            def ffn_down(t, name, w, units):
                project(t, name, [(q * C, P, [units[:, m, q * P:(q + 1) * P] for m in range(8)],
                                   [W[w][:, m * C:(m + 1) * C] for m in range(8)]) for q in range(NQ)])

            def transposes(t, name, src):
                open_bank(t, name)
                for h in range(CH):
                    for q in range(NQ):
                        ins = t_.transpose(ps(name)[:, h * T + q * P:h * T + (q + 1) * P],
                                           src[:, q, h * P:(h + 1) * P], ident[:, :])
                close_bank(ins, name)

            def mix(t, f):
                n = FEAT[f]
                if n < 4:
                    w, src = W["w_mix2a"][32 * n:32 * n + 32, :], aT[32 * n:32 * n + 32, :]
                else:
                    w, src = W["w_mix2b"], aT4
                project(t, "mix_" + f, [(h * T, P, [w[:, h * P:(h + 1) * P]], [src]) for h in range(CH)])

            def proj(t, f):
                i = "rkvgo".index(f)
                weights_first(t, f, lambda h, c, w: W["w_rkvgo"][:, i * 2 * C + h * C + c:i * 2 * C + h * C + c + w],
                              CH, [0, P], halves_of(mixed[f]))

            def level(t, s, keys_of, queries):
                name, rows = f"lev{s}", key_rows(s)
                open_bank(t, name)
                if rows < P:
                    pe.sem_inc(passed, 1)
                for g in range(CH * NQ):
                    ins = t_.matmul(ps(name)[0:rows, g * P:(g + 1) * P], keys_of[:, g * P:g * P + rows],
                                    queries[:, g * P:(g + 1) * P], start=True, stop=True)
                close_bank(ins, name)

            def scaled_level(t, n):
                pe.wait_ge(lev_ready, t.count(6, n + 1))
                level(t, LEVELS[n], lev[n % 3], pair_q[n % 2])

            def tokens_first(w, width, q, col):
                return (col, P, [xn1T[:, h, q * P:(q + 1) * P] for h in range(CH)],
                        [W[w][:, h * width:(h + 1) * width] for h in range(CH)])

            def ssd_proj(t, name, w, half):
                weights_first(t, name, packed(w, SH * SD), CH, [2 * half * P, (2 * half + 1) * P], halves_of(xn1T))

            Bf, Cf = (BC[:, n, :, :].rearrange("p t h -> p (t h)") for n in range(2))

            def ssd_scores(t, n):
                s = n // 2
                r = slice(64 * s, 64 * s + 64)
                open_bank(t, f"sc{n}")
                for i in range(4):
                    c = (n % 2) * 4 + i
                    ins = t_.matmul(ps(f"sc{n}")[:, i * P:(i + 1) * P], Bf[r, c * P:(c + 1) * P],
                                    Cf[r, c * P:(c + 1) * P], start=True, stop=True)
                close_bank(ins, f"sc{n}")

            def ssd_y(t, s):
                r = slice(64 * s, 64 * s + 64)
                open_bank(t, f"ys{s}")
                for c in range(SCH):
                    m = cs_row[:, s * SCH + c, :].rearrange("p (n e) -> p e n", e=2)
                    cd = cs_half[r, c * P:(c + 1) * P].rearrange("p (n e) -> p e n", e=2)
                    for par in range(2):
                        out = ps(f"ys{s}")[64 * par:64 * par + 64, c * 64:(c + 1) * 64]
                        ins = t_.matmul(out, Xrow[:, s, c, :], m[:, par, :], start=(c == 0), stop=(c == 0),
                                        skip_group_check=True)
                        if c:
                            ins = t_.matmul(out, S1[r, c, :], cd[:, par, :], start=False, stop=True,
                                            skip_group_check=True)
                close_bank(ins, f"ys{s}")

            def loaded(first, group, count):
                if first:
                    pe.wait_ge(loads[group], 16 * count)

            def one(a, b):
                first_a, first_b = not b, a and b and (a.reg is not None)
                if a:
                    wait_freed(pe, a, "xT")
                    loaded(first_a, "ffn0", 2)
                    ffn_p(a, 0)
                    pe.wait_ge(xxx_ready, a.count(1, 1))
                    loaded(first_a, "mix", 3)
                    w1 = packed("w_mix1", NMIX * DMIX)
                    project(a, "a", [(0, P, [w1(h, 0, P) for h in range(CH)], [xxxT[:, h, :] for h in range(CH)]),
                                     (T, DMIX, [w1(h, P, DMIX) for h in range(CH)], [xxxT[:, h, :] for h in range(CH)])])
                if b:
                    pe.wait_ge(xn1_ready, b.count(1, 1))
                    transposes(b, "xT1", xn1)
                if a:
                    ffn_p(a, 1)
                if b:
                    loaded(first_b, "ssd", 6)
                    wait_freed(pe, b, "xT1")
                    project(b, "dt", [tokens_first("w_dt", SH, q, q * SH) for q in range(NQ)])
                    project(b, "X0", [tokens_first("w_X", SH * SD, 0, 0)])
                if a:
                    pe.wait_ge(a_ready, a.count(1, 1))
                    mix(a, "w")
                    mix(a, "k")
                if b:
                    project(b, "X1", [tokens_first("w_X", SH * SD, 1, 0)])
                if a:
                    mix(a, "r")
                    loaded(first_a, "proj", 3)
                    pe.wait_ge(mix_ready, a.count(5, 1))
                    project(a, "dw", [(0, DDEC, [W["w_dec1"][:, h * DDEC:(h + 1) * DDEC] for h in range(CH)],
                                       [mixed["w"][:, h, :] for h in range(CH)])], first_row=DDEC)
                if b:
                    ssd_proj(b, "B0", "w_B", 0)
                if a:
                    mix(a, "v")
                    pe.wait_ge(mix_ready, a.count(5, 2))
                    proj(a, "k")
                if b:
                    ssd_proj(b, "B1", "w_B", 1)
                    pe.wait_ge(prefix_ready, b.count(1, 1))
                    project(b, "csum", [(0, P, [before[:, :]],
                                         [prefix[:, :].rearrange("p (q h) -> p q h", h=SH)[:, :, SH - 1]])])
                if a:
                    wait_freed(pe, a, "dw")
                    project(a, "w", [(h * T, P, [W["w_dec2"][:, h * P:(h + 1) * P]], [decT]) for h in range(CH)])
                    wait_freed(pe, a, "a")
                    mix(a, "g")
                    pe.wait_ge(mix_ready, a.count(5, 3))
                    proj(a, "r")
                if b:
                    ssd_proj(b, "C0", "w_C", 0)
                if a:
                    pe.wait_ge(mix_ready, a.count(5, 4))
                    project(a, "v", [(q * C, P, [mixed["v"][:, h, q * P:(q + 1) * P] for h in range(CH)],
                                      [W["w_rkvgo"][:, 4 * C + h * C:4 * C + (h + 1) * C] for h in range(CH)])
                                     for q in range(NQ)])
                    wait_freed(pe, a, "k")
                    wait_freed(pe, a, "r")
                    level(a, 1, flat(kT), pair_q[1])
                if b:
                    ssd_proj(b, "C1", "w_C", 1)
                if a:
                    pe.wait_ge(mix_ready, a.count(5, 5))
                    proj(a, "g")
                if b:
                    ssd_proj(b, "res0", "w_res", 0)
                    ssd_proj(b, "res1", "w_res", 1)
                if a:
                    scaled_level(a, 0)
                    scaled_level(a, 1)
                if b:
                    pe.wait_ge(cs_loaded, b.count(64, 80))
                    open_bank(b, "csT")
                    pe.sem_inc(passed, 1)
                    close_bank(t_.transpose(ps("csT")[:, 0:NQ * SCH], cs16[:, :], ident[0:NQ * SCH, 0:NQ * SCH]), "csT")
                    wait_freed(pe, b, "B1")
                    for s in range(NQ):
                        r = slice(64 * s, 64 * s + 64)
                        open_bank(b, f"bt{s}")
                        pe.sem_inc(passed, 1)
                        for c in range(SCH - 1):
                            ins = t_.transpose(ps(f"bt{s}")[:, c * SD:(c + 1) * SD], Bf[r, c * P:(c + 1) * P],
                                               ident[r, r])
                        close_bank(ins, f"bt{s}")
                    wait_freed(pe, b, "C1")
                    ssd_scores(b, 0)
                if a:
                    scaled_level(a, 2)
                    scaled_level(a, 3)
                if b:
                    for n in range(1, 4):
                        ssd_scores(b, n)
                if a:
                    scaled_level(a, 4)
                    ffn_p(a, 2)
                    scaled_level(a, 5)
                if b:
                    pe.wait_ge(X_rows, b.count(16, 32))
                    open_bank(b, "st")
                    for s in range(NQ):
                        wait_freed(pe, b, f"bt{s}")
                        for c in range(SCH - 1):
                            ins = t_.matmul(ps("st")[64 * s:64 * s + 64, c * SD:(c + 1) * SD], Brow[:, s, c, :],
                                            Xrow[:, s, c, :], start=True, stop=True)
                    close_bank(ins, "st")
                if a:
                    ffn_p(a, 3)
                    pe.wait_ge(prod_ready, a.count(3, 2))
                    open_bank(a, "k0T")
                    for q in range(NQ):
                        for h in range(CH):
                            ins = t_.transpose(ps("k0T")[:, q * C + h * P:q * C + (h + 1) * P],
                                               kT[:, h, q * P:(q + 1) * P], ident[:, :])
                    close_bank(ins, "k0T")
                if b:
                    pe.wait_ge(Cdec_ready, b.count(1, 1))
                    wait_freed(pe, b, "sc1")
                    wait_freed(pe, b, "st")
                    ssd_y(b, 0)
                if a:
                    wait_freed(pe, a, "k0T")
                    wait_freed(pe, a, "v")
                    project(a, "kv", [(q * C + h * P, P, [k0n[:, q, h * P:(h + 1) * P]], [v[:, q, h * P:(h + 1) * P]])
                                      for q in range(NQ) for h in range(CH)])
                if b:
                    wait_freed(pe, b, "sc3")
                    ssd_y(b, 1)
                    loaded(first_b, "ffn1", 3)
                    ffn_n(b, 0)
                if a:
                    pe.wait_ge(prod_ready, a.count(3, 1))
                    project(a, "bonus", [(q * HEADS, P, [prodT[:, h, q * P:(q + 1) * P] for h in range(CH)],
                                          [head_sel[:, h, :] for h in range(CH)]) for q in range(NQ)])
                    wait_freed(pe, a, "kv")
                    wait_freed(pe, a, "lev2")
                    pe.wait_ge(prod_ready, a.count(3, 3))
                    open_bank(a, "y")
                    for q in range(NQ):
                        for h in range(CH):
                            n = q * C + h * P
                            t_.matmul(ps("y")[:, n:n + P], rT[:, h, q * P:(q + 1) * P], S[:, q, h, :],
                                      start=(n == 0), stop=False, skip_group_check=True)
                        for hd in range(HEADS):
                            n, i = q * C + hd * HD, ((hd // 2) * NQ + q) * 2 + hd % 2
                            ins = t_.matmul(ps("y")[:, n:n + HD], att[:, i * P:(i + 1) * P],
                                            v[:, q, hd * HD:(hd + 1) * HD], start=False, stop=True,
                                            skip_group_check=True)
                    close_bank(ins, "y")
                    loaded(first_a, "down0", 1)
                    pe.wait_ge(sparse_ready, a.count(2, 2))
                    ffn_down(a, "F0", "f_down", hid)
                    pe.wait_ge(yn_ready, a.count(1, 1))
                    transposes(a, "yT", y)
                if b:
                    ffn_n(b, 1)
                if a:
                    pe.wait_ge(yg_ready, a.count(1, 1))
                    project(a, "s0", [(q * C, P, [ygT[:, h, q * P:(q + 1) * P] for h in range(CH)],
                                       [W["w_rkvgo"][:, 8 * C + h * C:8 * C + (h + 1) * C] for h in range(CH)])
                                      for q in range(NQ)])
                if b:
                    ffn_n(b, 2)
                    ffn_n(b, 3)
                if a:
                    pe.wait_ge(xn_ready, a.count(1, 2))
                    transposes(a.next(), "xT", xn)
                if b:
                    wait_freed(pe, b, "ys0")
                    wait_freed(pe, b, "ys1")
                    project(b, "s1", [(q * C, P, [gate[:, m, q * P:(q + 1) * P] for m in range(SH // 2)],
                                       [W["w_sout"][:, m * C:(m + 1) * C] for m in range(SH // 2)])
                                      for q in range(NQ)])
                    wait_freed(pe, b, "n3u")
                    ffn_down(b, "F1", "n_down", hidB)

            for f in freed:
                pe.sem_inc(f, 1)
            pe.wait_ge(const_ready, 2)
            pe.wait_ge(xn_ready, 1)
            transposes(Tile(None, 0), "xT", xn)
            rounds(pe, one)
    return nc


def _tiles(np, w):
    k, n = w.shape[0] // P, w.shape[1]
    return np.ascontiguousarray(w.reshape(k, P, n).transpose(1, 0, 2).reshape(P, k * n))


def _layout(np, v):
    pre = "L0_attn_"
    vecs = np.stack([v[pre + n].reshape(C) for n in
                     ("time_maa_x", "time_maa_w", "time_maa_k", "time_maa_v", "time_maa_r", "time_maa_g",
                      "time_decay", "time_faaaa", "ln_gamma", "ln_beta")])
    out = {"x": v[pre + "x"].reshape(TOKENS, C),
           "vecs": vecs.reshape(len(VEC), CH, P).transpose(2, 0, 1).reshape(P, len(VEC) * CH),
           "w_mix1": _tiles(np, v[pre + "time_maa_w1"]),
           "w_mix2a": v[pre + "time_maa_w2"][0:4].reshape(4 * DMIX, C),
           "w_mix2b": v[pre + "time_maa_w2"][4],
           "w_dec1": _tiles(np, v[pre + "time_decay_w1"]),
           "w_dec2": v[pre + "time_decay_w2"],
           "w_rkvgo": np.concatenate([_tiles(np, v[pre + "W_" + n].T) for n in "rkvgo"], axis=1)}

    def units(w):
        return w.reshape(C, 2, P, 4).transpose(0, 1, 3, 2).reshape(C, HID)

    out["f_gate"] = _tiles(np, units(v["L0_ffn_w_gate"]))
    out["f_up"] = _tiles(np, units(v["L0_ffn_w_up"]))
    out["f_down"] = v["L0_ffn_w_down"].reshape(2, P, 4, C).transpose(1, 0, 2, 3).reshape(P, 8 * C)
    inner = SH * SD
    w_in = v["L1_attn_w_in"]
    out["w_X"] = _tiles(np, w_in[0:inner].T)
    out["w_res"] = _tiles(np, w_in[inner:].T)
    par = v["L1_attn_w_param"].reshape(SH, 1 + 2 * SD, C)
    out["w_dt"] = _tiles(np, par[:, 0].T)
    out["w_B"] = _tiles(np, par[:, 1:1 + SD].reshape(inner, C).T)
    out["w_C"] = _tiles(np, par[:, 1 + SD:].reshape(inner, C).T)
    out["w_sout"] = _tiles(np, v["L1_attn_w_out"].T)
    out["n_gate"] = _tiles(np, v["L1_ffn_w_gate"].T)
    out["n_up"] = _tiles(np, v["L1_ffn_w_up"].T)
    out["n_down"] = _tiles(np, v["L1_ffn_w_down"].T)
    return {n: np.ascontiguousarray(a) for n, a in out.items()}


def kernel(**inputs):
    import numpy as np
    import concourse.bacc as bacc
    from concourse.bass_utils import run_bass_kernel_spmd

    arrays = _layout(np, {n: np.asarray(a) for n, a in inputs.items()})
    nc = bacc.Bacc("TRN2", target_bir_lowering=False, num_devices=1)
    aps = {n: nc.dram_tensor("in_" + n, a.shape, mybir.dt.from_np(a.dtype), kind="ExternalInput").ap()
           for n, a in arrays.items()}
    aps["out"] = nc.dram_tensor("out_tokens", (TOKENS, C), F32, kind="ExternalOutput").ap()
    aps["cs_dram"] = nc.dram_tensor("cs_dram", (T * SH,), F32).ap()
    aps["x_dram"] = nc.dram_tensor("x_dram", (T * SH * SD,), F32).ap()
    build_block(nc, aps)
    r = run_bass_kernel_spmd(nc, [{"in_" + n: a for n, a in arrays.items()}], core_ids=[0])
    return r.results[0]["out_tokens"].reshape(BATCH, TOKENS // BATCH, C)
```

```python
from contextlib import ExitStack

import concourse.bass as bass
from concourse import mybir

F32 = mybir.dt.float32
BF16 = mybir.dt.bfloat16
I8 = mybir.dt.int8
ALU = mybir.AluOpType
ACT = mybir.ActivationFunctionType
AX = mybir.AxisListType

P = 128
TOKENS, BATCH, C = 2048, 2, 256
T = 256
NT = TOKENS // T
NQ = T // P
CH = C // P
HEADS, HD = 4, 64
DMIX, NMIX, DDEC = 32, 5, 64
HID = 1024
SH, SD = 8, 64
SEQ_T = 128
SCH = SEQ_T * SH // P
CHT = P // SH
LN_EPS = 1e-5
GN_EPS = 1e-5 * 8.0 ** 2
DECAY_CAP = 110.0
NEG = -1.0e30
LEVELS = [64, 32, 16, 8, 4, 2, 1]

VEC = {n: i for i, n in enumerate(["maa_x", "maa_w", "maa_k", "maa_v", "maa_r", "maa_g", "decay", "bonus", "gamma", "beta"])}
FEAT = {"w": 0, "k": 1, "v": 2, "r": 3, "g": 4}

RING = 4
FILLS = [["xT", "p0g", "p0u", "a", "p1g", "p1u", "mix_w", "mix_k", "mix_r", "dw", "mix_v", "k", "w", "mix_g", "r",
          "v", "lev1", "g", "lev64", "lev32", "lev16", "lev8",
          "lev4", "p2g", "p2u", "lev2", "p3g", "p3u", "k0T", "kv", "bonus", "y", "F0", "yT",
          "s0"],
         ["xT1", "dt", "X0", "X1", "B0", "B1", "csum", "C0", "C1", "res0", "res1", "csT", "bt0", "bt1", "sc0",
          "sc1", "sc2", "sc3", "st", "ys0", "ys1", "n0g", "n0u", "n1g", "n1u", "n2g", "n2u", "n3g", "n3u", "s1",
          "F1"]]
BANK = {n: ring * RING + i % RING for ring in range(2) for i, n in enumerate(FILLS[ring])}
NTH = {n: i // RING + 1 for ring in range(2) for i, n in enumerate(FILLS[ring])}
BANKS = 2 * RING
PER = [sum(BANK[n] == b for n in FILLS[b // RING]) for b in range(BANKS)]


LAST_FILLS = ["xT1", "dt", "X0", "X1", "B0", "B1", "csum", "C0", "C1", "n0g", "n0u", "n1g", "n1u", "res0", "res1",
              "csT", "bt0", "bt1", "sc0", "sc1", "sc2", "sc3", "n2g", "n2u", "st", "n3g", "n3u", "ys0", "ys1", "F1",
              "s1"]
FILLED_BEFORE = [NT * PER[b] + (b == BANK["xT"]) if b < RING else (NT - 1) * PER[b] for b in range(BANKS)]


class Tile:

    def __init__(self, reg, off=0, last=False):
        self.reg, self.off, self.last = reg, off, last

    def count(self, per, n):
        return n + per * self.off if self.reg is None else self.reg * per + (n + per * self.off)

    def place(self, name):
        if self.last:
            i = LAST_FILLS.index(name)
            return i % BANKS, FILLED_BEFORE[i % BANKS] + i // BANKS + 1
        b = BANK[name]
        return b, self.count(PER[b], NTH[name])

    def at(self):
        return self.off if self.reg is None else self.reg + self.off

    def next(self):
        return Tile(self.reg, self.off + 1)


def build_block(nc, A):
    with ExitStack() as ctx:
        def sb(name, shape, dt=F32):
            return ctx.enter_context(nc.sbuf_tensor(name, shape, dt))

        def sem(name):
            return ctx.enter_context(nc.semaphore(name))

        W = {n: sb("sb_" + n, list(A[n].shape)) for n in A
             if n not in ("x", "out", "cs_dram", "x_dram", "w_mix2b", "w_dec2")}
        low = sb("sb_mix2b_dec2", [P, C])
        W["w_mix2b"], W["w_dec2"] = low[0:DMIX, :], low[DDEC:P, :]
        vec = W["vecs"]

        ident = sb("ident", [P, P])
        masks = sb("masks", [P, len(LEVELS), 512], I8)
        causal = sb("causal", [P, P])
        before = sb("before", [P, P])
        chunk_reset = sb("chunk_reset", [P, T])
        head_reset = sb("head_reset", [P, NQ * SH])
        head_u = sb("head_u", [P, CH, HEADS])
        keep = sb("keep", [P, NT + 1])
        half_neg = sb("half_neg", [P, 8])

        X = sb("X", [P, NQ, C])
        xn = sb("xn", [P, NQ, C])
        xnT = sb("xnT", [P, CH, T + 1])
        dxT = sb("dxT", [P, CH, T])
        mixed = {f: sb("mixed_" + f, [P, CH, T]) for f in "wkrvg"}
        aT = sb("aT", [P, T])
        aT4_decT = sb("aT4_decT", [P, T])
        aT4, decT = aT4_decT[0:DMIX, :], aT4_decT[DDEC:P, :]
        kT = sb("kT", [P, CH, T])
        rT = sb("rT", [P, CH, T])
        v = sb("v", [P, NQ, C])
        gT = sb("gT", [P, CH, T])
        cum = sb("cum", [P, CH * T + 64])
        dec = sb("dec", [P, CH * NQ, P + 1])
        lev = [sb(f"lev{i}_kr", [P, CH * T]) for i in range(3)]
        pair_q = [sb(f"pair_q{i}", [P, NQ * HEADS * 64]) for i in range(2)]
        att = sb("att", [P, NQ * HEADS * P])
        S = sb("S", [P, NQ + 1, CH, P])
        x1 = sb("x1", [P, NQ, C])
        x1_prev = sb("x1_prev", [P, NQ, C])
        stats = sb("stats", [P, NQ * 6])
        meanvar = sb("meanvar", [P, NQ * 2])
        var_eps = sb("var_eps", [P, NQ * HEADS])
        rstd = sb("rstd", [P, NQ * HEADS])
        gsum = sb("gsum", [P, NQ * HEADS])
        th = [sb(f"th{i}", [P, 512]) for i in range(2)]
        thF = sb("thF", [P, NQ * C])
        hid = sb("hid", [P, 8, T])
        habs = sb("habs", [P, 4, T])
        beats = sb("beats", [P, 6, T], BF16)
        wins = sb("wins", [P, 4, T], BF16)
        xxxT = k0f = k0n = ygT = mixed["w"]
        y, yc, ysq, ynT = mixed["k"], mixed["r"], mixed["v"], mixed["g"]
        prodT = dxT

        xn1T = sb("xn1T", [P, CH, T])
        BC = sb("BC", [P, 2, SEQ_T, SH])
        cs_row = sb("cs_row", [P, 2 * SCH, P])
        cs_half = sb("cs_half", [P, SEQ_T * SH])
        prefix = sb("prefix", [P, NQ * SH])
        cs_nat = sb("cs_nat", [P, NQ, SH])
        cs16 = sb("cs16", [NQ * SCH, P])
        cs_col = sb("cs_col", [P, NQ * SCH])
        to_end = sb("to_end", [P, NQ * SCH])
        chunk_dec = sb("chunk_dec", [P, SCH])
        sp = [sb(f"sp{i}", [P, NQ * SH]) for i in range(4)]
        S1 = sb("S1", [P, SCH, SD])
        gate = sb("gate", [P, SH // 2, T])
        thB = [sb(f"thB{i}", [P, 512]) for i in range(2)]
        thFB = sb("thFB", [P, NQ * C])
        hidB = sb("hidB", [P, 8, T])
        Xnat = gate[:, :, :].rearrange("p a b -> p (a b)").rearrange("p (q n) -> p q n", q=NQ)
        Brow, Xrow = (hidB[:, 4 * i:4 * i + 4, :].rearrange("p a b -> p (a b)").rearrange(
            "p (q c d) -> p q c d", q=NQ, c=SCH) for i in range(2))
        xn1 = habs[:, 0:2, :]

        bank = [ctx.enter_context(nc.psum_tensor(f"bank{b}", [P, 512], F32)) for b in range(BANKS)]

        def ps(t, name):
            return bank[t.place(name)[0]]

        filled = [sem(f"filled{b}") for b in range(BANKS)]
        freed = [sem(f"freed{b}") for b in range(BANKS)]
        loads = {g: sem("loads_" + g) for g in ("vecs", "ffn0", "mix", "proj", "down0", "ssd", "ffn1")}
        x_loaded = sem("x_loaded")
        const_ready = sem("const_ready")
        masks_ready = sem("masks_ready")
        pool_step = sem("pool_step")
        act_step = sem("act_step")
        dve_step = sem("dve_step")
        passed = sem("passed")
        carry_ready = sem("carry_ready")
        xn_ready = sem("xn_ready")
        xn1_ready = sem("xn1_ready")
        xxx_ready = sem("xxx_ready")
        a_ready = sem("a_ready")
        mix_ready = sem("mix_ready")
        cum_ready = sem("cum_ready")
        g_tanh = sem("g_tanh")
        arg_ready = sem("arg_ready")
        fac_ready = sem("fac_ready")
        dec0_ready = sem("dec0_ready")
        lev_ready = sem("lev_ready")
        k0_ready = sem("k0_ready")
        th_ready = sem("th_ready")
        thB_ready = sem("thB_ready")
        abs_ready = sem("abs_ready")
        beats_ready = sem("beats_ready")
        wins_ready = sem("wins_ready")
        sparse_ready = sem("sparse_ready")
        rk_ready = sem("rk_ready")
        q0_ready = sem("q0_ready")
        yc_ready = sem("yc_ready")
        ysq_ready = sem("ysq_ready")
        var_ready = sem("var_ready")
        rstd_ready = sem("rstd_ready")
        yn_ready = sem("yn_ready")
        yg_ready = sem("yg_ready")
        thF_ready = sem("thF_ready")
        thFB_ready = sem("thFB_ready")
        x1_loaded = sem("x1_loaded")
        x1_ready = sem("x1_ready")
        out_ready = sem("out_ready")
        out_stored = sem("out_stored")
        x1_saved = sem("x1_saved")
        soft_ready = sem("soft_ready")
        prefix_ready = sem("prefix_ready")
        cs_stored = sem("cs_stored")
        cs_loaded = sem("cs_loaded")
        X_stored = sem("X_stored")
        X_rows = sem("X_rows")
        res_tanh = sem("res_tanh")
        cs_half_exp = sem("cs_half_exp")
        end_arg = sem("end_arg")
        to_end_ready = sem("to_end_ready")
        cs_masked = sem("cs_masked")
        L_exp = sem("L_exp")
        Cdec_ready = sem("Cdec_ready")

        block = ctx.enter_context(nc.Block())

        class Steps:

            def __init__(self, eng, s):
                self.eng, self.s, self.n = eng, s, 0

            def did(self, ins):
                self.n += 1
                ins.then_inc(self.s, 1)
                return self.n

            def after(self, n=None):
                if self.n:
                    self.eng.wait_ge(self.s, self.n if n is None else n)

            def restart(self):
                self.after()
                self.eng.sem_clear(self.s)
                self.n = 0

        def wait_filled(eng, t, name):
            b, n = t.place(name)
            eng.wait_ge(filled[b], n)

        def wait_freed(eng, t, name):
            b, n = t.place(name)
            eng.wait_ge(freed[b], n + 1)

        def free(ins, t, name):
            ins.then_inc(freed[t.place(name)[0]], 1)

        def flat(t):
            return t[:, :, :].rearrange("p a b -> p (a b)")

        def second_halves(t, s, par):
            return t[64 * par:64 * par + 64, :].rearrange("p (g b two s) -> p g b two s", g=CH * NQ, two=2, s=s)[:, :, :, 1, :]

        def paired(t, s, par):
            return t[64 * par:64 * par + 64, :].rearrange("p (g e b s) -> p g e b s", g=CH * NQ, e=2, s=s)[:, :, par, :, :]

        def key_rows(s):
            return P - s if s >= 32 else P

        cs_dram, x_dram = A["cs_dram"], A["x_dram"]

        def sparse_count(ops, steps):
            B01, B02, B03, B12, B13, B23 = (beats[:, n, :] for n in range(6))
            W0, W1, W2, W3 = (wins[:, n, :] for n in range(4))
            steps.did(ops.tensor_tensor(W0, B01, B02, ALU.add))
            steps.did(ops.tensor_tensor(W1, B12, B13, ALU.add))
            steps.did(ops.tensor_tensor(W2, B23, B02, ALU.subtract))
            n3 = steps.did(ops.tensor_tensor(W3, B03, B13, ALU.add))
            steps.after(n3 - 3)
            steps.did(ops.tensor_tensor(W0, W0, B03, ALU.add))
            steps.after(n3 - 2)
            steps.did(ops.tensor_tensor(W1, W1, B01, ALU.subtract))
            steps.after(n3 - 1)
            steps.did(ops.tensor_tensor(W2, W2, B12, ALU.subtract))
            steps.after(n3)
            return ops.tensor_tensor(W3, W3, B23, ALU.add)

        def rounds(eng, one):
            one(Tile(None, 0), None)
            with eng.Fori(1, NT) as it:
                one(Tile(it), Tile(it, -1))
            one(None, Tile(None, NT - 1, last=True))

        @block.sync
        def _(sp_):
            def load(names, group):
                for n in names:
                    dst = W[n] if n in ("w_mix2b", "w_dec2") else W[n][:, :]
                    sp_.dma_start(dst, A[n]).then_inc(loads[group], 16)

            def tokens(name, first):
                return A[name][bass.ds(first, T), :].rearrange("(q p) c -> p q c", p=P)

            def wait(s, value):
                sp_.wait_ge(s, value)
                sp_.sem_inc(passed, 1)

            def one(a, b, last=False):
                if a:
                    wait(xn_ready, a.count(1, 1))
                    sp_.dma_start(X[:, :, :], tokens("x", a.at() * T if last else a.next().at() * T)).then_inc(x_loaded, 16)
                    wait(x1_saved, a.count(1, 1))
                    if b:
                        wait(xn1_ready, b.count(1, 1))
                    sp_.dma_start(x1[:, :, :], tokens("x", a.at() * T)).then_inc(x1_loaded, 16)
                if b:
                    wait_freed(sp_, b, "X1")
                    sp_.sem_inc(passed, 1)
                    wait(X_rows, b.count(16, 16))
                    sp_.dma_start(x_dram.rearrange("(q p n) -> p q n", q=NQ, p=P), Xnat).then_inc(X_stored, 16)
                    wait_freed(sp_, b, "csum")
                    sp_.sem_inc(passed, 1)
                    wait(cs_loaded, b.count(64, 16))
                    sp_.dma_start(cs_dram.rearrange("(q p h) -> p q h", q=NQ, p=P), cs_nat[:, :, :]).then_inc(cs_stored, 16)
                    wait(cs_stored, b.count(16, 32))
                    sp_.dma_start(cs16[:, :], cs_dram.rearrange("(c p) -> c p", p=P)).then_inc(cs_loaded, 16)
                    sp_.dma_start(flat(cs_row), cs_dram.partition_broadcast(P)).then_inc(cs_loaded, 16)
                    n = SEQ_T * SH
                    for q in range(NQ):
                        sp_.dma_start(cs_half[64 * q:64 * q + 64, :],
                                      cs_dram[q * n:(q + 1) * n].partition_broadcast(64)).then_inc(cs_loaded, 16)
                    wait(X_stored, b.count(16, 32))
                    sp_.dma_start(Xrow.rearrange("p q c d -> p (q c) d"),
                                  x_dram.rearrange("(c p d) -> p c d", p=P, d=SD)).then_inc(X_rows, 16)
                    wait(out_ready, b.count(1, 2))
                    sp_.dma_start(tokens("out", b.at() * T), thFB[:, :].rearrange("p (q c) -> p q c", q=NQ)).then_inc(
                        out_stored, 16)

            for s in (X_rows, X_stored, cs_stored, cs_loaded, out_stored):
                sp_.sem_inc(s, 16)
            for s in (x1_saved, out_ready):
                sp_.sem_inc(s, 1)
            sp_.dma_start(X[:, :, :], tokens("x", 0)).then_inc(x_loaded, 16)
            load(["vecs"], "vecs")
            load(["f_gate", "f_up"], "ffn0")
            load(["w_mix1", "w_mix2a", "w_mix2b"], "mix")
            load(["w_dec1", "w_dec2", "w_rkvgo"], "proj")
            load(["f_down"], "down0")
            load(["w_dt", "w_X", "w_B", "w_C", "w_res", "w_sout"], "ssd")
            load(["n_gate", "n_up", "n_down"], "ffn1")
            one(Tile(None, 0), None)
            with sp_.Fori(1, NT - 1) as it:
                one(Tile(it), Tile(it, -1))
            one(Tile(None, NT - 1), Tile(None, NT - 2), last=True)
            one(None, Tile(None, NT - 1, last=True))
            sp_.wait_ge(out_stored, 16 * (NT + 1))

        @block.gpsimd
        def _(pool):
            steps = Steps(pool, pool_step)

            def did(ins):
                steps.did(ins)
                steps.after()

            g = nc.gpsimd
            did(g.memset(ident[:, :], 0.0))
            did(g.affine_select(out=ident[:, :], in_=ident[:, :], compare_op=ALU.not_equal, fill=1.0, base=0,
                                pattern=[[-1, P]], channel_multiplier=1))
            did(g.memset(half_neg[:, :], -0.5))
            g.memset(rstd[:, :], 1.0).then_inc(const_ready, 1)

            def rsqrt(count, n):
                pool.wait_ge(var_ready, count)
                g.tensor_tensor(rstd[:, 0:n], var_eps[:, 0:n], half_neg[:, 0:n], ALU.pow).then_inc(rstd_ready, 1)

            pool.wait_ge(const_ready, 2)
            rsqrt(1, NQ)
            did(g.memset(causal[:, :], 0.0))
            did(g.affine_select(out=causal[:, :], in_=causal[:, :], compare_op=ALU.is_ge, fill=NEG, base=0,
                                pattern=[[1, P]], channel_multiplier=-1))
            did(g.memset(before[:, :], 1.0))
            bv = before[:, :].rearrange("p (b q) -> p b q", q=CHT)
            did(g.affine_select(out=bv, in_=bv, compare_op=ALU.is_ge, fill=0.0, base=0,
                                pattern=[[-CHT, P // CHT], [0, CHT]], channel_multiplier=1))
            did(g.affine_select(out=bv, in_=bv, compare_op=ALU.is_gt, fill=0.0, base=0,
                                pattern=[[CHT, P // CHT], [1, CHT]], channel_multiplier=-1))
            for n, s in enumerate(LEVELS):
                tmp = lev[n % 2][:, 0:64]
                tv = tmp.rearrange("p (b q) -> p b q", q=s)
                did(g.memset(tmp, 1.0))
                did(g.affine_select(out=tv, in_=tv, compare_op=ALU.is_ge, fill=0.0, base=0,
                                    pattern=[[-2 * s, 64 // s], [0, s]], channel_multiplier=1))
                did(g.affine_select(out=tv, in_=tv, compare_op=ALU.is_ge, fill=0.0, base=s - 1,
                                    pattern=[[2 * s, 64 // s], [0, s]], channel_multiplier=-1))
                did(g.tensor_copy(masks[:, n, :].rearrange("p (r x) -> p r x", x=64),
                                  tmp.unsqueeze(1).to_broadcast([P, NQ * HEADS, 64])))
            pool.sem_inc(masks_ready, 1)
            steps.restart()

            def one(a, b):
                if a:
                    pool.wait_ge(beats_ready, a.count(1, 1))
                    steps.did(sparse_count(g, steps))
                    steps.after()
                    pool.sem_inc(wins_ready, 1)
                    rsqrt(a.count(3, 2), NQ)
                if b:
                    pool.wait_ge(cs_loaded, b.count(64, 80))
                    g.tensor_tensor(cs_row[:, :, :], cs_row[:, :, :],
                                    causal[:, :].unsqueeze(1).to_broadcast([P, NQ * SCH, P]),
                                    ALU.add).then_inc(cs_masked, 1)
                if a:
                    wait_freed(pool, a, "mix_g")
                    wait_freed(pool, a, "r")
                    g.tensor_tensor(prodT[:, :, :], kT[:, :, :], rT[:, :, :], ALU.mult).then_inc(rk_ready, 1)
                if b:
                    pool.wait_ge(cs_half_exp, b.count(1, 1))
                    wait_freed(pool, b, "C1")
                    g.tensor_tensor(cs_half[:, :], cs_half[:, :], BC[:, 1, :, :].rearrange("p t h -> p (t h)"),
                                    ALU.mult).then_inc(Cdec_ready, 1)
                if a:
                    pool.wait_ge(lev_ready, a.count(6, 6))
                    pool.wait_ge(dec0_ready, a.count(1, 1))
                    rq = flat(rT).rearrange("p (a b) -> p a b", b=P)
                    g.tensor_tensor(rq, rq, dec[:, :, 0:P], ALU.mult).then_inc(q0_ready, 1)
                    rsqrt(a.count(3, 3), NQ * HEADS)
                    rsqrt(a.count(3, 4), NQ)
                steps.restart()

            rounds(pool, one)

        @block.scalar
        def _(act):
            steps = Steps(act, act_step)
            a_ = nc.scalar

            def ffn_tanh(t, name, buf, ready, made=None):
                wait_filled(act, t, name + "g")
                if made:
                    wait_freed(act, t, made + "u")
                a_.activation(buf[:, :], ps(t, name + "g")[:, :], ACT.Tanh, scale=0.5).then_inc(ready, 1)

            def ffn_abs(t, n):
                wait_freed(act, t, f"p{n}u")
                if n >= 2:
                    act.wait_ge(beats_ready, t.count(1, 1))
                i = 2 * (n % 2)
                a_.activation(habs[:, i:i + 2, :], hid[:, 2 * n:2 * n + 2, :], ACT.Abs).then_inc(abs_ready, 1)

            def copy(t, dst, name, parts):
                wait_filled(act, t, name)
                free(a_.activation(dst, ps(t, name)[:, :].rearrange("p (h t) -> p h t", h=parts), ACT.Identity), t, name)

            def level_exp(t, n):
                act.wait_ge(arg_ready, t.count(7, n + 1))
                a_.activation(lev[n % 3][:, :], lev[n % 3][:, :], ACT.Exp).then_inc(fac_ready, 1)

            def bc(t, name, which, pair):
                wait_filled(act, t, name)
                src = ps(t, name)[:, :].rearrange("p (m s t) -> p m s t", m=2, s=NQ)
                for par in range(2):
                    for s in range(NQ):
                        cols = BC[64 * s:64 * s + 64, which, :, :].rearrange("p t (m e) -> p e m t", e=2)
                        ins = a_.activation(cols[:, par, 2 * pair:2 * pair + 2, :],
                                            src[64 * par:64 * par + 64, :, s, :], ACT.Identity)
                free(ins, t, name)

            def x_copy(t, q):
                act.wait_ge(X_stored, t.count(16, 16))
                wait_filled(act, t, f"X{q}")
                free(a_.activation(Xnat[:, q, :], ps(t, f"X{q}")[:, :], ACT.Identity), t, f"X{q}")

            def xnT_copy(t):
                wait_filled(act, t, "xT")
                free(a_.activation(xnT[:, :, 1:T + 1], ps(t, "xT")[:, :].rearrange("p (h t) -> p h t", h=CH),
                                   ACT.Identity), t, "xT")

            def one(a, b):
                if a:
                    ffn_tanh(a, "p0", th[0], th_ready)
                    wait_filled(act, a, "a")
                    a_.activation(aT[:, :], ps(a, "a")[:, 0:T], ACT.Tanh).then_inc(a_ready, 1)
                    free(a_.activation(aT4, ps(a, "a")[0:DMIX, T:2 * T], ACT.Tanh), a, "a")
                if b:
                    copy(b, xn1T[:, :, :], "xT1", CH)
                    act.wait_ge(x1_ready, b.count(1, 1))
                    act.wait_ge(out_ready, b.count(1, 1))
                    a_.activation(flat(x1_prev), flat(x1), ACT.Identity).then_inc(x1_saved, 1)
                if a:
                    ffn_tanh(a, "p1", th[1], th_ready)
                    ffn_abs(a, 0)
                if b:
                    wait_filled(act, b, "dt")
                    steps.did(a_.activation(sp[0][:, :], ps(b, "dt")[:, 0:NQ * SH], ACT.Abs))
                    steps.after()
                    steps.did(a_.activation(sp[1][:, :], sp[0][:, :], ACT.Exp, scale=-1.0))
                    steps.after()
                    a_.activation(sp[2][:, :], sp[1][:, :], ACT.Ln, bias=1.0).then_inc(soft_ready, 1)
                    x_copy(b, 0)
                if a:
                    ffn_abs(a, 1)
                if b:
                    x_copy(b, 1)
                if a:
                    wait_filled(act, a, "dw")
                    free(a_.activation(decT, ps(a, "dw")[DDEC:P, 0:T], ACT.Tanh), a, "dw")
                if b:
                    bc(b, "B0", 0, 0)
                if a:
                    copy(a, kT[:, :, :], "k", CH)
                if b:
                    bc(b, "B1", 0, 1)
                if a:
                    wait_filled(act, a, "w")
                    for h in range(CH):
                        ins = a_.activation(lev[2][:, h * T:(h + 1) * T], ps(a, "w")[:, h * T:(h + 1) * T], ACT.Exp,
                                            bias=vec[:, 2 * VEC["decay"] + h:2 * VEC["decay"] + h + 1])
                    free(ins, a, "w")
                    wait_filled(act, a, "r")
                    a_.activation(flat(rT), ps(a, "r")[:, :], ACT.Identity)
                    for par in range(2):
                        ins = a_.activation(paired(pair_q[1], 1, par), second_halves(ps(a, "r")[:, :], 1, par), ACT.Identity)
                    free(ins, a, "r")
                if b:
                    bc(b, "C0", 1, 0)
                if a:
                    level_exp(a, 0)
                    level_exp(a, 1)
                    act.wait_ge(cum_ready, a.count(1, 1))
                    a_.activation(dec[:, :, 1:P + 1], cum[:, 0:CH * T].rearrange("p (a b) -> p a b", b=P), ACT.Exp,
                                  scale=-1.0).then_inc(dec0_ready, 1)
                    copy(a, v[:, :, :], "v", NQ)
                if b:
                    bc(b, "C1", 1, 1)
                if a:
                    level_exp(a, 2)
                    wait_filled(act, a, "g")
                    a_.activation(flat(gT), ps(a, "g")[:, :], ACT.Tanh, scale=0.5).then_inc(g_tanh, 1)
                if b and b.last:
                    ffn_tanh(b, "n0", thB[0], thB_ready)
                    ffn_tanh(b, "n1", thB[1], thB_ready)

                def res_tanhs(n):
                    wait_filled(act, b, f"res{n}")
                    a_.activation(gate[:, 2 * n:2 * n + 2, :].rearrange("p a b -> p (a b)"), ps(b, f"res{n}")[:, :],
                                  ACT.Tanh, scale=0.5).then_inc(res_tanh, 1)

                if b:
                    act.wait_ge(X_stored, b.count(16, 32))
                    res_tanhs(0)
                if a:
                    level_exp(a, 3)
                if b:
                    res_tanhs(1)
                if a:
                    level_exp(a, 4)
                if b:
                    act.wait_ge(cs_loaded, b.count(64, 80))
                    steps.did(a_.activation(chunk_dec[:, :], cs_half[:, :].rearrange("p (c w) -> p c w", w=P)[:, :, P - 1],
                                            ACT.Exp))
                    steps.after()
                    a_.activation(cs_half[:, :], cs_half[:, :], ACT.Exp).then_inc(cs_half_exp, 1)
                    act.wait_ge(end_arg, b.count(1, 1))
                    a_.activation(to_end[:, :], to_end[:, :], ACT.Exp).then_inc(to_end_ready, 1)

                def L_exps(s):
                    act.wait_ge(cs_masked, b.count(1, 1))
                    for n in range(s * SCH, (s + 1) * SCH):
                        ins = a_.activation(cs_row[:, n, :], cs_row[:, n, :], ACT.Exp, bias=cs_col[:, n:n + 1])
                    ins.then_inc(L_exp, 1)

                if b:
                    L_exps(0)
                if a:
                    level_exp(a, 5)
                if b:
                    L_exps(1)
                if a:
                    act.wait_ge(arg_ready, a.count(7, 7))
                    a_.activation(flat(k0f), flat(k0f), ACT.Exp).then_inc(fac_ready, 1)
                    ffn_tanh(a, "p2", th[0], th_ready, "p0")
                    ffn_tanh(a, "p3", th[1], th_ready, "p1")
                    copy(a, k0n[:, :, :], "k0T", NQ)
                    ffn_abs(a, 2)
                    ffn_abs(a, 3)
                if b and b.last:
                    ffn_tanh(b, "n2", thB[0], thB_ready, "n0")
                    ffn_tanh(b, "n3", thB[1], thB_ready, "n1")
                elif b:
                    ffn_tanh(b, "n0", thB[0], thB_ready)
                if a:
                    act.wait_ge(yc_ready, a.count(1, 1))
                    a_.activation(flat(ysq), flat(yc), ACT.Square).then_inc(ysq_ready, 1)
                    wait_filled(act, a, "F0")
                    a_.activation(thF[:, :], ps(a, "F0")[:, :], ACT.Tanh, scale=0.25).then_inc(thF_ready, 1)
                    wait_filled(act, a, "yT")
                    for h in range(CH):
                        g0, b0 = 2 * VEC["gamma"] + h, 2 * VEC["beta"] + h
                        ins = a_.activation(ynT[:, h, :], ps(a, "yT")[:, h * T:(h + 1) * T], ACT.Identity,
                                            scale=vec[:, g0:g0 + 1], bias=vec[:, b0:b0 + 1])
                    free(ins, a, "yT")
                if b and not b.last:
                    ffn_tanh(b, "n1", thB[1], thB_ready)
                    ffn_tanh(b, "n2", thB[0], thB_ready, "n0")
                    ffn_tanh(b, "n3", thB[1], thB_ready, "n1")
                if b:
                    act.wait_ge(out_stored, b.count(16, 16))
                    wait_filled(act, b, "F1")
                    a_.activation(thFB[:, :], ps(b, "F1")[:, :], ACT.Tanh, scale=0.25).then_inc(thFB_ready, 1)
                if a:
                    act.wait_ge(carry_ready, a.count(1, 1))
                    xnT_copy(a.next())
                steps.restart()

            act.wait_ge(loads["vecs"], 16)
            act.wait_ge(const_ready, 2)
            xnT_copy(Tile(None, 0))
            rounds(act, one)

        @block.vector
        def _(dve):
            steps = Steps(dve, dve_step)
            did, after = steps.did, steps.after
            d = nc.vector

            for t in (flat(xnT), att[:, :], pair_q[0][:, :], pair_q[1][:, :], S[:, :, :, :].rearrange("p a b c -> p (a b c)"), flat(head_u)):
                did(d.memset(t, 0.0))
            for t in (flat(dec), chunk_reset[:, :], head_reset[:, :], keep[:, :]):
                did(d.memset(t, 1.0))
            after()
            for t in (chunk_reset[:, :].rearrange("p (a b) -> p a b", b=P)[:, :, 0:1],
                      head_reset[:, :].rearrange("p (a b) -> p a b", b=SH)[:, :, 0:1],
                      keep[:, 0:NT].rearrange("p (a b) -> p a b", b=NT // BATCH)[:, :, 0:1]):
                did(d.memset(t, 0.0))
            after()
            dve.sem_inc(const_ready, 1)

            def norm_stats(src):
                for q in range(NQ):
                    did(d.bn_stats(stats[:, 6 * q:6 * q + 6], src[:, q, :]))
                after()
                for q in range(NQ):
                    did(d.bn_aggr(meanvar[:, 2 * q:2 * q + 2], stats[:, 6 * q:6 * q + 6]))
                after()
                mv = meanvar[:, :].rearrange("p (q two) -> p q two", two=2)
                d.tensor_scalar(var_eps[:, 0:NQ], mv[:, :, 1], LN_EPS, None, ALU.add).then_inc(var_ready, 1)

            def norm_apply(src, dst, rstd_count, ready):
                dve.wait_ge(rstd_ready, rstd_count)
                for q in range(NQ):
                    ins = d.tensor_scalar(dst[:, q, :], src[:, q, :], meanvar[:, 2 * q:2 * q + 1], rstd[:, q:q + 1],
                                          ALU.subtract, ALU.mult)
                    if q < NQ - 1:
                        did(ins)
                ins.then_inc(ready, 1)

            dve.wait_ge(const_ready, 2)
            dve.wait_ge(x_loaded, 16)
            norm_stats(X)
            norm_apply(X, xn, 1, xn_ready)
            dve.wait_ge(loads["vecs"], 16)
            for h in range(HEADS):
                r, n = slice(64 * (h % 2), 64 * (h % 2) + 64), 2 * VEC["bonus"] + h // 2
                did(d.tensor_copy(head_u[r, h // 2, h:h + 1], vec[r, n:n + 1]))
            steps.restart()

            def vcol(name, h):
                return vec[:, 2 * VEC[name] + h:2 * VEC[name] + h + 1]

            def hidden(t, name, n, buf, ready, out):
                dve.wait_ge(ready, t.count(4, n + 1))
                free(d.scalar_tensor_tensor(out=buf[:, :], in0=buf[:, :], scalar=1.0, in1=ps(t, name + "g")[:, :],
                                            op0=ALU.add, op1=ALU.mult), t, name + "g")
                wait_freed(dve, t, name + "g")
                wait_filled(dve, t, name + "u")
                free(d.tensor_tensor(out[:, 2 * n:2 * n + 2, :].rearrange("p a b -> p (a b)"), buf[:, :],
                                     ps(t, name + "u")[:, :], ALU.mult), t, name + "u")

            def hidden_p(t, n):
                hidden(t, f"p{n}", n, th[n % 2], th_ready, hid)

            def hidden_n(t, n):
                hidden(t, f"n{n}", n, thB[n % 2], thB_ready, hid if t.last else hidB)

            def mix_scaled(t, f):
                wait_filled(dve, t, "mix_" + f)
                for h in range(CH):
                    ins = d.scalar_tensor_tensor(out=mixed[f][:, h, :], in0=ps(t, "mix_" + f)[:, h * T:(h + 1) * T],
                                                 scalar=vcol("maa_" + f, h), in1=dxT[:, h, :],
                                                 op0=ALU.add, op1=ALU.mult)
                    if h == 0:
                        did(ins)
                free(ins, t, "mix_" + f)

            def mix_add(t, f):
                wait_freed(dve, t, "mix_" + f)
                d.tensor_tensor(mixed[f][:, :, :], mixed[f][:, :, :], xnT[:, :, 1:T + 1],
                                ALU.add).then_inc(mix_ready, 1)

            def halves(t, s):
                return t.rearrange("p (b two s) -> p b two s", two=2, s=s)

            def level_args(n):
                s = LEVELS[n]
                c, f = halves(cum[:, 0:CH * T], s), halves(lev[n % 3][:, :], s)
                one_back = cum[:, s - 1:s - 1 + CH * T].rearrange("p (b w) -> p b w", w=2 * s)[:, :, 0:s]
                mid = c[:, :, 0, s - 1:s].to_broadcast([P, CH * T // (2 * s), s])
                did(d.tensor_tensor(f[:, :, 0, :], c[:, :, 0, :], mid, ALU.subtract))
                d.tensor_tensor(f[:, :, 1, :], mid, one_back, ALU.subtract).then_inc(arg_ready, 1)

            def level_scale(t, n):
                s = LEVELS[n]
                dve.wait_ge(fac_ready, t.count(7, n + 1))
                f, kk = halves(lev[n % 3][:, :], s), halves(flat(kT), s)
                did(d.tensor_tensor(f[:, :, 0, :], f[:, :, 0, :], kk[:, :, 0, :], ALU.mult))
                for par in range(2):
                    ins = d.tensor_tensor(paired(pair_q[n % 2], s, par), second_halves(lev[n % 3][:, :], s, par),
                                          second_halves(flat(rT), s, par), ALU.mult)
                    if par == 0:
                        did(ins)
                ins.then_inc(lev_ready, 1)

            def level_take(t, n):
                s = LEVELS[n]
                name, r = f"lev{s}", slice(0, key_rows(s))
                if s > 1:
                    wait_freed(dve, t, f"lev{LEVELS[n - 1]}")
                wait_filled(dve, t, name)
                dve.sem_inc(passed, 1)
                out = att[r, :].rearrange("p (b w) -> p b w", w=2 * s)[:, :, s:2 * s]
                free(d.copy_predicated(out, masks[r, n, :].rearrange("p (b s) -> p b s", s=s),
                                       ps(t, name)[r, :].rearrange("p (b s) -> p b s", s=s)), t, name)

            def sparse_compare(t, m):
                dve.wait_ge(abs_ready, t.count(4, 2 * m + 2))
                for i, first, count in ((0, 0, 3), (1, 3, 2), (2, 5, 1)):
                    did(d.tensor_tensor(beats[:, first:first + count, :],
                                        habs[:, i:i + 1, :].to_broadcast([P, count, T]),
                                        habs[:, i + 1:4, :], ALU.is_ge))

            def sparse_select(m):
                for i, (least, op) in enumerate([(1.5, ALU.is_ge), (0.5, ALU.is_ge), (-0.5, ALU.is_ge),
                                                 (1.5, ALU.is_le)]):
                    ins = d.scalar_tensor_tensor(out=hid[:, 4 * m + i, :], in0=wins[:, i, :], scalar=least,
                                                 in1=hid[:, 4 * m + i, :], op0=op, op1=ALU.mult)
                    if i < 3:
                        did(ins)
                ins.then_inc(sparse_ready, 1)

            def one(a, b):
                if a:
                    wait_freed(dve, a, "xT")
                    did(d.tensor_tensor(dxT[:, :, :], xnT[:, :, 0:T], xnT[:, :, 1:T + 1], ALU.subtract))
                    after()
                    for h in range(CH):
                        ins = d.scalar_tensor_tensor(out=xxxT[:, h, :], in0=dxT[:, h, :], scalar=vcol("maa_x", h),
                                                     in1=xnT[:, h, 1:T + 1], op0=ALU.mult, op1=ALU.add)
                        if h == 0:
                            did(ins)
                    ins.then_inc(xxx_ready, 1)
                    did(d.tensor_scalar(S[:, 0:1, :, :].rearrange("p z a b -> p (z a b)"),
                                        S[:, NQ:NQ + 1, :, :].rearrange("p z a b -> p (z a b)"),
                                        keep[:, bass.ds(a.at(), 1)], None, ALU.mult))
                    hidden_p(a, 0)
                    hidden_p(a, 1)
                    mix_scaled(a, "w")
                    mix_scaled(a, "k")
                    mix_add(a, "w")
                if b:
                    dve.wait_ge(soft_ready, b.count(1, 1))
                    free(d.scalar_tensor_tensor(out=sp[3][:, :], in0=ps(b, "dt")[:, 0:NQ * SH], scalar=0.0, in1=sp[2][:, :],
                                                op0=ALU.max, op1=ALU.add), b, "dt")
                    wait_freed(dve, b, "dt")
                    d.tensor_tensor_scan(prefix[:, :], head_reset[:, :], sp[3][:, :], 0.0, ALU.mult,
                                         ALU.add).then_inc(prefix_ready, 1)
                if a:
                    mix_scaled(a, "r")
                    mix_add(a, "k")
                    mix_scaled(a, "v")
                    mix_add(a, "r")
                    sparse_compare(a, 0)
                    after()
                    dve.sem_inc(beats_ready, 1)
                if b:
                    dve.wait_ge(prefix_ready, b.count(1, 1))
                    dve.wait_ge(cs_stored, b.count(16, 16))
                    wait_filled(dve, b, "csum")
                    free(d.scalar_tensor_tensor(out=cs_nat[:, :, :], in0=prefix[:, :].rearrange("p (q h) -> p q h", h=SH),
                                                scalar=-1.0,
                                                in1=ps(b, "csum")[:, 0:NQ].unsqueeze(2).to_broadcast([P, NQ, SH]),
                                                op0=ALU.mult, op1=ALU.subtract), b, "csum")
                if a:
                    mix_add(a, "v")
                    wait_freed(dve, a, "w")
                    did(d.tensor_scalar(lev[2][:, :], lev[2][:, :], DECAY_CAP, None, ALU.min))
                    mix_scaled(a, "g")
                    after()
                    for h in range(CH):
                        ins = d.tensor_tensor_scan(cum[:, h * T:(h + 1) * T], chunk_reset[:, :],
                                                   lev[2][:, h * T:(h + 1) * T], 0.0, ALU.mult, ALU.add)
                        if h == 0:
                            did(ins)
                    ins.then_inc(cum_ready, 1)
                    mix_add(a, "g")
                    dve.wait_ge(cum_ready, a.count(1, 1))
                    dve.wait_ge(masks_ready, 1)
                    level_args(0)
                    level_args(1)
                    dve.wait_ge(x_loaded, a.count(16, 32))
                    norm_stats(X)
                    level_take(a, 6)
                    level_scale(a, 0)
                    level_args(2)
                    level_scale(a, 1)
                    norm_apply(X, xn, a.count(3, 2), xn_ready)
                    dve.wait_ge(g_tanh, a.count(1, 1))
                    free(d.scalar_tensor_tensor(out=flat(gT), in0=flat(gT), scalar=1.0, in1=ps(a, "g")[:, :],
                                                op0=ALU.add, op1=ALU.mult), a, "g")
                if b and b.last:
                    hidden_n(b, 0)
                    hidden_n(b, 1)

                def res_gate(n):
                    dve.wait_ge(res_tanh, b.count(2, n + 1))
                    gv = gate[:, 2 * n:2 * n + 2, :].rearrange("p a b -> p (a b)")
                    free(d.scalar_tensor_tensor(out=gv, in0=gv, scalar=1.0, in1=ps(b, f"res{n}")[:, :],
                                                op0=ALU.add, op1=ALU.mult), b, f"res{n}")

                if a:
                    level_take(a, 0)
                    level_args(3)
                    level_scale(a, 2)
                if b:
                    res_gate(0)
                if a:
                    level_take(a, 1)
                    level_args(4)
                    level_scale(a, 3)
                if b:
                    res_gate(1)
                    wait_filled(dve, b, "csT")
                    free(d.tensor_scalar(cs_col[:, :], ps(b, "csT")[:, 0:NQ * SCH], -1.0, None, ALU.mult), b, "csT")
                    wait_freed(dve, b, "csT")
                    dve.wait_ge(cs_masked, b.count(1, 1))
                    d.tensor_tensor(to_end[:, :], cs_row[:, :, P - 1], cs_col[:, :], ALU.add).then_inc(end_arg, 1)
                    dve.wait_ge(to_end_ready, b.count(1, 1))
                    for s in range(NQ):
                        wait_filled(dve, b, f"bt{s}")
                        free(d.tensor_tensor(Brow[:, s, 0:SCH - 1, :],
                                             ps(b, f"bt{s}")[:, 0:(SCH - 1) * SD].rearrange("p (c d) -> p c d", d=SD),
                                             to_end[:, s * SCH:(s + 1) * SCH - 1].unsqueeze(2).to_broadcast(
                                                 [P, SCH - 1, SD]), ALU.mult), b, f"bt{s}")
                if a:
                    level_take(a, 2)
                    level_args(5)
                    level_scale(a, 4)
                    level_take(a, 3)
                    cq = cum[:, 0:CH * T].rearrange("p (a b) -> p a b", b=P)
                    d.tensor_tensor(flat(k0f).rearrange("p (a b) -> p a b", b=P), cq,
                                    cq[:, :, P - 1:P].to_broadcast([P, CH * NQ, P]),
                                    ALU.subtract).then_inc(arg_ready, 1)
                    level_scale(a, 5)
                    level_take(a, 4)
                if b:
                    for n in range(4):
                        dve.wait_ge(L_exp, b.count(NQ, n // 2 + 1))
                        wait_filled(dve, b, f"sc{n}")
                        w = flat(cs_row)[:, n * 512:(n + 1) * 512]
                        free(d.tensor_tensor(w, w, ps(b, f"sc{n}")[:, :], ALU.mult), b, f"sc{n}")
                if a:
                    hidden_p(a, 2)
                    level_take(a, 5)
                    dve.wait_ge(fac_ready, a.count(7, 7))
                    wait_filled(dve, a, "lev1")
                    dve.wait_ge(rk_ready, a.count(1, 1))
                    d.tensor_tensor(flat(kT), flat(kT), flat(k0f), ALU.mult).then_inc(k0_ready, 1)
                if b and b.last:
                    hidden_n(b, 2)
                if b:
                    wait_filled(dve, b, "st")
                    dve.wait_ge(cs_half_exp, b.count(1, 1))
                    did(d.tensor_copy(S1[:, 1, :], ps(b, "st")[:, 0:SD]))
                    for c in range(1, SCH - 1):
                        after()
                        ins = d.scalar_tensor_tensor(out=S1[:, c + 1, :], in0=S1[:, c, :], scalar=chunk_dec[:, c:c + 1],
                                                     in1=ps(b, "st")[:, c * SD:(c + 1) * SD], op0=ALU.mult, op1=ALU.add)
                        if c < SCH - 2:
                            did(ins)
                    free(ins, b, "st")
                    if b.last:
                        hidden_n(b, 3)
                if a:
                    dve.wait_ge(wins_ready, a.count(1, 1))
                    sparse_select(0)
                    hidden_p(a, 3)
                    d.tensor_scalar(xnT[:, :, 0:1], xnT[:, :, T:T + 1], keep[:, bass.ds(a.next().at(), 1)], None,
                                    ALU.mult).then_inc(carry_ready, 1)
                    wait_filled(dve, a, "kv")
                    kv = ps(a, "kv")[:, :].rearrange("p (q h c) -> p q h c", q=NQ, h=CH)
                    for q in range(NQ):
                        if q:
                            after()
                        for h in range(CH):
                            for par in range(2):
                                r, cols = slice(64 * par, 64 * par + 64), slice(64 * par, 64 * par + 64)
                                ins = d.scalar_tensor_tensor(out=S[r, q + 1, h, cols], in0=S[r, q, h, cols],
                                                             scalar=dec[r, h * NQ + q, P:P + 1], in1=kv[r, q, h, cols],
                                                             op0=ALU.mult, op1=ALU.add)
                                if (q, h, par) != (NQ - 1, CH - 1, 1):
                                    did(ins)
                    free(ins, a, "kv")
                    sparse_compare(a, 1)
                    after()
                    did(sparse_count(d, steps))
                    after()
                    sparse_select(1)
                    wait_filled(dve, a, "bonus")
                    y3, v3 = (flat(t).rearrange("p (n d) -> p n d", d=HD) for t in (y, v))
                    free(d.tensor_tensor(y3, v3, ps(a, "bonus")[:, 0:NQ * HEADS].unsqueeze(2).to_broadcast(
                        [P, NQ * HEADS, HD]), ALU.mult), a, "bonus")
                    wait_freed(dve, a, "bonus")
                    wait_filled(dve, a, "y")
                    ins = d.tensor_tensor(flat(y), flat(y), ps(a, "y")[:, :], ALU.add)
                    free(ins, a, "y")
                    yc3, ysq3 = (flat(t).rearrange("p (n d) -> p n d", d=HD) for t in (yc, ysq))
                    wait_freed(dve, a, "y")
                    did(d.tensor_reduce(gsum[:, :], y3, AX.X, ALU.add))
                    after()
                    did(d.tensor_scalar(gsum[:, :], gsum[:, :], 1.0 / HD, None, ALU.mult))
                    after()
                    d.tensor_tensor(yc3, y3, gsum[:, :].unsqueeze(2).to_broadcast([P, NQ * HEADS, HD]),
                                    ALU.subtract).then_inc(yc_ready, 1)
                if b:
                    for s in range(NQ):
                        wait_filled(dve, b, f"ys{s}")
                        gv = gate[:, :, s * P:(s + 1) * P]
                        free(d.tensor_tensor(gv, gv, ps(b, f"ys{s}")[:, :].rearrange("p (t m) -> p m t", m=SH // 2),
                                             ALU.mult), b, f"ys{s}")
                if a:
                    dve.wait_ge(ysq_ready, a.count(1, 1))
                    did(d.tensor_reduce(gsum[:, :], ysq3, AX.X, ALU.add))
                    after()
                    d.tensor_scalar(var_eps[:, :], gsum[:, :], 1.0 / HD, GN_EPS, ALU.mult, ALU.add).then_inc(var_ready, 1)
                if b and not b.last:
                    hidden_n(b, 0)
                if a:
                    dve.wait_ge(rstd_ready, a.count(3, 3))
                    d.tensor_tensor(y3, yc3, rstd[:, :].unsqueeze(2).to_broadcast([P, NQ * HEADS, HD]),
                                    ALU.mult).then_inc(yn_ready, 1)
                    dve.wait_ge(thF_ready, a.count(1, 1))
                    free(d.scalar_tensor_tensor(out=thF[:, :], in0=thF[:, :], scalar=1.0, in1=ps(a, "F0")[:, :],
                                                op0=ALU.add, op1=ALU.mult), a, "F0")
                    wait_freed(dve, a, "yT")
                    d.tensor_tensor(flat(ygT), flat(ynT), flat(gT), ALU.mult).then_inc(yg_ready, 1)
                if b and not b.last:
                    hidden_n(b, 1)
                    hidden_n(b, 2)
                if a:
                    wait_filled(dve, a, "s0")
                    wait_freed(dve, a, "F0")
                    free(d.tensor_tensor(thF[:, :], thF[:, :], ps(a, "s0")[:, :], ALU.mult), a, "s0")
                    wait_freed(dve, a, "s0")
                    dve.wait_ge(x1_loaded, a.count(16, 16))
                    d.scalar_tensor_tensor(out=flat(x1), in0=thF[:, :], scalar=0.125, in1=flat(x1),
                                           op0=ALU.mult, op1=ALU.add).then_inc(x1_ready, 1)
                    dve.wait_ge(x1_ready, a.count(1, 1))
                    norm_stats(x1)
                if b:
                    if not b.last:
                        hidden_n(b, 3)
                    dve.wait_ge(thFB_ready, b.count(1, 1))
                    free(d.scalar_tensor_tensor(out=thFB[:, :], in0=thFB[:, :], scalar=1.0, in1=ps(b, "F1")[:, :],
                                                op0=ALU.add, op1=ALU.mult), b, "F1")
                if a:
                    norm_apply(x1, xn1, a.count(3, 4), xn1_ready)
                if b:
                    wait_freed(dve, b, "F1")
                    wait_filled(dve, b, "s1")
                    free(d.tensor_tensor(thFB[:, :], thFB[:, :], ps(b, "s1")[:, :], ALU.mult), b, "s1")
                    wait_freed(dve, b, "s1")
                    d.scalar_tensor_tensor(out=thFB[:, :], in0=thFB[:, :], scalar=0.125, in1=flat(x1_prev),
                                           op0=ALU.mult, op1=ALU.add).then_inc(out_ready, 1)
                steps.restart()

            rounds(dve, one)

        @block.tensor
        def _(pe):
            t_ = nc.tensor

            def open_bank(t, name):
                b, n = t.place(name)
                pe.wait_ge(freed[b], n)

            def close_bank(ins, t, name):
                ins.then_inc(filled[t.place(name)[0]], 1)

            def project(t, name, parts, first_row=0):
                open_bank(t, name)
                for col, rows, ws, xs in parts:
                    for k, (w, x) in enumerate(zip(ws, xs)):
                        n = x.free_size()
                        ins = t_.matmul(ps(t, name)[first_row:first_row + rows, col:col + n], w, x, start=(k == 0),
                                        stop=(k == len(ws) - 1))
                close_bank(ins, t, name)

            def weights_first(t, name, w, k, cols, x, width=P):
                project(t, name, [(i * T, width, [w(h, c, width) for h in range(k)], [x(h) for h in range(k)])
                                  for i, c in enumerate(cols)])

            def packed(n, width):
                return lambda h, c, w: W[n][:, h * width + c:h * width + c + w]

            def halves_of(t):
                return lambda h: t[:, h, :]

            def ffn(t, name, gate_w, up_w, pair, x):
                for suffix, w in (("g", gate_w), ("u", up_w)):
                    weights_first(t, name + suffix, packed(w, HID), CH, [2 * pair * P, (2 * pair + 1) * P], x)

            def ffn_p(t, n):
                ffn(t, f"p{n}", "f_gate", "f_up", n, lambda h: xnT[:, h, 1:T + 1])

            def ffn_n(t, n):
                ffn(t, f"n{n}", "n_gate", "n_up", n, halves_of(xn1T))

            def ffn_down(t, name, w, units):
                project(t, name, [(q * C, P, [units[:, m, q * P:(q + 1) * P] for m in range(8)],
                                   [W[w][:, m * C:(m + 1) * C] for m in range(8)]) for q in range(NQ)])

            def ffn_1(t, units):
                wait_freed(pe, t, "n3u")
                ffn_down(t, "F1", "n_down", units)

            def transposes(t, name, src):
                open_bank(t, name)
                for h in range(CH):
                    for q in range(NQ):
                        ins = t_.transpose(ps(t, name)[:, h * T + q * P:h * T + (q + 1) * P],
                                           src[:, q, h * P:(h + 1) * P], ident[:, :])
                close_bank(ins, t, name)

            def mix(t, f):
                n = FEAT[f]
                if n < 4:
                    w, src = W["w_mix2a"][32 * n:32 * n + 32, :], aT[32 * n:32 * n + 32, :]
                else:
                    w, src = W["w_mix2b"], aT4
                project(t, "mix_" + f, [(h * T, P, [w[:, h * P:(h + 1) * P]], [src]) for h in range(CH)])

            def proj(t, f):
                i = "rkvgo".index(f)
                weights_first(t, f, lambda h, c, w: W["w_rkvgo"][:, i * 2 * C + h * C + c:i * 2 * C + h * C + c + w],
                              CH, [0, P], halves_of(mixed[f]))

            def level(t, s, keys_of, queries):
                name, rows = f"lev{s}", key_rows(s)
                open_bank(t, name)
                if rows < P:
                    pe.sem_inc(passed, 1)
                for g in range(CH * NQ):
                    ins = t_.matmul(ps(t, name)[0:rows, g * P:(g + 1) * P], keys_of[:, g * P:g * P + rows],
                                    queries[:, g * P:(g + 1) * P], start=True, stop=True)
                close_bank(ins, t, name)

            def scaled_level(t, n):
                pe.wait_ge(lev_ready, t.count(6, n + 1))
                level(t, LEVELS[n], lev[n % 3], pair_q[n % 2])

            def tokens_first(w, width, q, col):
                return (col, P, [xn1T[:, h, q * P:(q + 1) * P] for h in range(CH)],
                        [W[w][:, h * width:(h + 1) * width] for h in range(CH)])

            def ssd_proj(t, name, w, half):
                weights_first(t, name, packed(w, SH * SD), CH, [2 * half * P, (2 * half + 1) * P], halves_of(xn1T))

            Bf, Cf = (BC[:, n, :, :].rearrange("p t h -> p (t h)") for n in range(2))

            def ssd_scores(t, n):
                s = n // 2
                r = slice(64 * s, 64 * s + 64)
                open_bank(t, f"sc{n}")
                for i in range(4):
                    c = (n % 2) * 4 + i
                    ins = t_.matmul(ps(t, f"sc{n}")[:, i * P:(i + 1) * P], Bf[r, c * P:(c + 1) * P],
                                    Cf[r, c * P:(c + 1) * P], start=True, stop=True)
                close_bank(ins, t, f"sc{n}")

            def ssd_y(t, s):
                r = slice(64 * s, 64 * s + 64)
                open_bank(t, f"ys{s}")
                for c in range(SCH):
                    m = cs_row[:, s * SCH + c, :].rearrange("p (n e) -> p e n", e=2)
                    cd = cs_half[r, c * P:(c + 1) * P].rearrange("p (n e) -> p e n", e=2)
                    for par in range(2):
                        out = ps(t, f"ys{s}")[64 * par:64 * par + 64, c * 64:(c + 1) * 64]
                        ins = t_.matmul(out, Xrow[:, s, c, :], m[:, par, :], start=(c == 0), stop=(c == 0),
                                        skip_group_check=True)
                        if c:
                            ins = t_.matmul(out, S1[r, c, :], cd[:, par, :], start=False, stop=True,
                                            skip_group_check=True)
                close_bank(ins, t, f"ys{s}")

            def loaded(first, group, count):
                if first:
                    pe.wait_ge(loads[group], 16 * count)

            def one(a, b):
                first_a, first_b = not b, a and b and (a.reg is not None)
                if a:
                    wait_freed(pe, a, "xT")
                    loaded(first_a, "ffn0", 2)
                    ffn_p(a, 0)
                    pe.wait_ge(xxx_ready, a.count(1, 1))
                    loaded(first_a, "mix", 3)
                    w1 = packed("w_mix1", NMIX * DMIX)
                    project(a, "a", [(0, P, [w1(h, 0, P) for h in range(CH)], [xxxT[:, h, :] for h in range(CH)]),
                                     (T, DMIX, [w1(h, P, DMIX) for h in range(CH)], [xxxT[:, h, :] for h in range(CH)])])
                if b:
                    pe.wait_ge(xn1_ready, b.count(1, 1))
                    transposes(b, "xT1", xn1)
                if a:
                    ffn_p(a, 1)
                if b:
                    loaded(first_b, "ssd", 6)
                    wait_freed(pe, b, "xT1")
                    project(b, "dt", [tokens_first("w_dt", SH, q, q * SH) for q in range(NQ)])
                    project(b, "X0", [tokens_first("w_X", SH * SD, 0, 0)])
                if a:
                    pe.wait_ge(a_ready, a.count(1, 1))
                    mix(a, "w")
                    mix(a, "k")
                if b:
                    project(b, "X1", [tokens_first("w_X", SH * SD, 1, 0)])
                if a:
                    mix(a, "r")
                    loaded(first_a, "proj", 3)
                    pe.wait_ge(mix_ready, a.count(5, 1))
                    project(a, "dw", [(0, DDEC, [W["w_dec1"][:, h * DDEC:(h + 1) * DDEC] for h in range(CH)],
                                       [mixed["w"][:, h, :] for h in range(CH)])], first_row=DDEC)
                if b:
                    ssd_proj(b, "B0", "w_B", 0)
                if a:
                    mix(a, "v")
                    pe.wait_ge(mix_ready, a.count(5, 2))
                    proj(a, "k")
                if b:
                    ssd_proj(b, "B1", "w_B", 1)
                    pe.wait_ge(prefix_ready, b.count(1, 1))
                    project(b, "csum", [(0, P, [before[:, :]],
                                         [prefix[:, :].rearrange("p (q h) -> p q h", h=SH)[:, :, SH - 1]])])
                if a:
                    wait_freed(pe, a, "dw")
                    project(a, "w", [(h * T, P, [W["w_dec2"][:, h * P:(h + 1) * P]], [decT]) for h in range(CH)])
                    wait_freed(pe, a, "a")
                    mix(a, "g")
                    pe.wait_ge(mix_ready, a.count(5, 3))
                    proj(a, "r")
                if b:
                    ssd_proj(b, "C0", "w_C", 0)
                if a:
                    pe.wait_ge(mix_ready, a.count(5, 4))
                    project(a, "v", [(q * C, P, [mixed["v"][:, h, q * P:(q + 1) * P] for h in range(CH)],
                                      [W["w_rkvgo"][:, 4 * C + h * C:4 * C + (h + 1) * C] for h in range(CH)])
                                     for q in range(NQ)])
                    wait_freed(pe, a, "k")
                    wait_freed(pe, a, "r")
                    level(a, 1, flat(kT), pair_q[1])
                if b:
                    ssd_proj(b, "C1", "w_C", 1)
                if b and b.last:
                    ffn_n(b, 0)
                    ffn_n(b, 1)
                if a:
                    pe.wait_ge(mix_ready, a.count(5, 5))
                    proj(a, "g")
                    scaled_level(a, 0)
                    scaled_level(a, 1)
                if b:
                    ssd_proj(b, "res0", "w_res", 0)
                    ssd_proj(b, "res1", "w_res", 1)
                    pe.wait_ge(cs_loaded, b.count(64, 80))
                    open_bank(b, "csT")
                    pe.sem_inc(passed, 1)
                    close_bank(t_.transpose(ps(b, "csT")[:, 0:NQ * SCH], cs16[:, :], ident[0:NQ * SCH, 0:NQ * SCH]), b, "csT")
                    wait_freed(pe, b, "B1")
                    for s in range(NQ):
                        r = slice(64 * s, 64 * s + 64)
                        open_bank(b, f"bt{s}")
                        pe.sem_inc(passed, 1)
                        for c in range(SCH - 1):
                            ins = t_.transpose(ps(b, f"bt{s}")[:, c * SD:(c + 1) * SD], Bf[r, c * P:(c + 1) * P],
                                               ident[r, r])
                        close_bank(ins, b, f"bt{s}")
                    wait_freed(pe, b, "C1")
                if a:
                    scaled_level(a, 2)
                    scaled_level(a, 3)
                if b:
                    for n in range(4):
                        ssd_scores(b, n)
                if a:
                    scaled_level(a, 4)
                    ffn_p(a, 2)
                    scaled_level(a, 5)
                if b and b.last:
                    ffn_n(b, 2)
                if b:
                    pe.wait_ge(X_rows, b.count(16, 32))
                    open_bank(b, "st")
                    for s in range(NQ):
                        wait_freed(pe, b, f"bt{s}")
                        for c in range(SCH - 1):
                            ins = t_.matmul(ps(b, "st")[64 * s:64 * s + 64, c * SD:(c + 1) * SD], Brow[:, s, c, :],
                                            Xrow[:, s, c, :], start=True, stop=True)
                    close_bank(ins, b, "st")
                if b and b.last:
                    ffn_n(b, 3)
                if a:
                    ffn_p(a, 3)
                    pe.wait_ge(k0_ready, a.count(1, 1))
                    open_bank(a, "k0T")
                    for q in range(NQ):
                        for h in range(CH):
                            ins = t_.transpose(ps(a, "k0T")[:, q * C + h * P:q * C + (h + 1) * P],
                                               kT[:, h, q * P:(q + 1) * P], ident[:, :])
                    close_bank(ins, a, "k0T")
                if b:
                    pe.wait_ge(Cdec_ready, b.count(1, 1))
                    wait_freed(pe, b, "sc1")
                    wait_freed(pe, b, "st")
                    ssd_y(b, 0)
                if a:
                    wait_freed(pe, a, "k0T")
                    wait_freed(pe, a, "v")
                    project(a, "kv", [(q * C + h * P, P, [k0n[:, q, h * P:(h + 1) * P]], [v[:, q, h * P:(h + 1) * P]])
                                      for q in range(NQ) for h in range(CH)])
                if b:
                    wait_freed(pe, b, "sc3")
                    ssd_y(b, 1)
                    loaded(first_b, "ffn1", 3)
                    if not b.last:
                        ffn_n(b, 0)
                if a:
                    pe.wait_ge(rk_ready, a.count(1, 1))
                    project(a, "bonus", [(q * HEADS, P, [prodT[:, h, q * P:(q + 1) * P] for h in range(CH)],
                                          [head_u[:, h, :] for h in range(CH)]) for q in range(NQ)])
                    wait_freed(pe, a, "kv")
                    wait_freed(pe, a, "lev2")
                    pe.wait_ge(q0_ready, a.count(1, 1))
                    open_bank(a, "y")
                    for q in range(NQ):
                        for h in range(CH):
                            n = q * C + h * P
                            t_.matmul(ps(a, "y")[:, n:n + P], rT[:, h, q * P:(q + 1) * P], S[:, q, h, :],
                                      start=(n == 0), stop=False, skip_group_check=True)
                        for hd in range(HEADS):
                            n, i = q * C + hd * HD, ((hd // 2) * NQ + q) * 2 + hd % 2
                            ins = t_.matmul(ps(a, "y")[:, n:n + HD], att[:, i * P:(i + 1) * P],
                                            v[:, q, hd * HD:(hd + 1) * HD], start=False, stop=True,
                                            skip_group_check=True)
                    close_bank(ins, a, "y")
                    loaded(first_a, "down0", 1)
                    pe.wait_ge(sparse_ready, a.count(2, 2))
                    ffn_down(a, "F0", "f_down", hid)
                    pe.wait_ge(yn_ready, a.count(1, 1))
                    transposes(a, "yT", y)
                if b and not b.last:
                    ffn_n(b, 1)
                if a:
                    pe.wait_ge(yg_ready, a.count(1, 1))
                    project(a, "s0", [(q * C, P, [ygT[:, h, q * P:(q + 1) * P] for h in range(CH)],
                                       [W["w_rkvgo"][:, 8 * C + h * C:8 * C + (h + 1) * C] for h in range(CH)])
                                      for q in range(NQ)])
                if b and not b.last:
                    ffn_n(b, 2)
                    ffn_n(b, 3)
                if a:
                    pe.wait_ge(xn_ready, a.count(1, 2))
                    transposes(a.next(), "xT", xn)
                if b:
                    if b.last:
                        ffn_1(b, hid)
                    wait_freed(pe, b, "ys0")
                    wait_freed(pe, b, "ys1")
                    project(b, "s1", [(q * C, P, [gate[:, m, q * P:(q + 1) * P] for m in range(SH // 2)],
                                       [W["w_sout"][:, m * C:(m + 1) * C] for m in range(SH // 2)])
                                      for q in range(NQ)])
                    if not b.last:
                        ffn_1(b, hidB)

            for f in freed:
                pe.sem_inc(f, 1)
            pe.wait_ge(const_ready, 2)
            pe.wait_ge(xn_ready, 1)
            transposes(Tile(None, 0), "xT", xn)
            rounds(pe, one)
    return nc


def _tiles(np, w):
    k, n = w.shape[0] // P, w.shape[1]
    return np.ascontiguousarray(w.reshape(k, P, n).transpose(1, 0, 2).reshape(P, k * n))


def _layout(np, v):
    pre = "L0_attn_"
    vecs = np.stack([v[pre + n].reshape(C) for n in
                     ("time_maa_x", "time_maa_w", "time_maa_k", "time_maa_v", "time_maa_r", "time_maa_g",
                      "time_decay", "time_faaaa", "ln_gamma", "ln_beta")])
    out = {"x": v[pre + "x"].reshape(TOKENS, C),
           "vecs": vecs.reshape(len(VEC), CH, P).transpose(2, 0, 1).reshape(P, len(VEC) * CH),
           "w_mix1": _tiles(np, v[pre + "time_maa_w1"]),
           "w_mix2a": v[pre + "time_maa_w2"][0:4].reshape(4 * DMIX, C),
           "w_mix2b": v[pre + "time_maa_w2"][4],
           "w_dec1": _tiles(np, v[pre + "time_decay_w1"]),
           "w_dec2": v[pre + "time_decay_w2"],
           "w_rkvgo": np.concatenate([_tiles(np, v[pre + "W_" + n].T) for n in "rkvgo"], axis=1)}

    def units(w):
        return w.reshape(C, 2, P, 4).transpose(0, 1, 3, 2).reshape(C, HID)

    out["f_gate"] = _tiles(np, units(v["L0_ffn_w_gate"]))
    out["f_up"] = _tiles(np, units(v["L0_ffn_w_up"]))
    out["f_down"] = v["L0_ffn_w_down"].reshape(2, P, 4, C).transpose(1, 0, 2, 3).reshape(P, 8 * C)
    inner = SH * SD
    w_in = v["L1_attn_w_in"]
    out["w_X"] = _tiles(np, w_in[0:inner].T)
    out["w_res"] = _tiles(np, w_in[inner:].T)
    par = v["L1_attn_w_param"].reshape(SH, 1 + 2 * SD, C)
    out["w_dt"] = _tiles(np, par[:, 0].T)
    out["w_B"] = _tiles(np, par[:, 1:1 + SD].reshape(inner, C).T)
    out["w_C"] = _tiles(np, par[:, 1 + SD:].reshape(inner, C).T)
    out["w_sout"] = _tiles(np, v["L1_attn_w_out"].T)
    out["n_gate"] = _tiles(np, v["L1_ffn_w_gate"].T)
    out["n_up"] = _tiles(np, v["L1_ffn_w_up"].T)
    out["n_down"] = _tiles(np, v["L1_ffn_w_down"].T)
    return {n: np.ascontiguousarray(a) for n, a in out.items()}


def kernel(**inputs):
    import numpy as np
    import concourse.bacc as bacc
    from concourse.bass_utils import run_bass_kernel_spmd

    arrays = _layout(np, {n: np.asarray(a) for n, a in inputs.items()})
    nc = bacc.Bacc("TRN2", target_bir_lowering=False, num_devices=1)
    aps = {n: nc.dram_tensor("in_" + n, a.shape, mybir.dt.from_np(a.dtype), kind="ExternalInput").ap()
           for n, a in arrays.items()}
    aps["out"] = nc.dram_tensor("out_tokens", (TOKENS, C), F32, kind="ExternalOutput").ap()
    aps["cs_dram"] = nc.dram_tensor("cs_dram", (T * SH,), F32).ap()
    aps["x_dram"] = nc.dram_tensor("x_dram", (T * SH * SD,), F32).ap()
    build_block(nc, aps)
    r = run_bass_kernel_spmd(nc, [{"in_" + n: a for n, a in arrays.items()}], core_ids=[0])
    return r.results[0]["out_tokens"].reshape(BATCH, TOKENS // BATCH, C)
```
